# Optimizing a Trainium2 kernel written in Bass

```python
import numpy as np
import jax
import jax.numpy as jnp

def _softmax(x, axis=-1):
    return jax.nn.softmax(x, axis=axis)

def _gelu(x):
    return jax.nn.gelu(x, approximate=True)

def _silu(x):
    return jax.nn.silu(x)

def _sigmoid(x):
    return jax.nn.sigmoid(x)

def _layernorm(x, axis=-1, eps=1e-05):
    m = jnp.mean(x, axis=axis, keepdims=True)
    v = jnp.var(x, axis=axis, keepdims=True)
    return (x - m) / jnp.sqrt(v + eps)

def _scatter_add(tgt, idx, src, axis=0):
    return tgt.at[idx].add(src)

def _segment_sum(src, seg, n):
    return jax.ops.segment_sum(src, seg, n)
kernel_name = 'mk_adj_resnorm_d2_adj_r2_7542be'

def setup_inputs(seed: int=0):
    np.random.seed(seed)
    _w = jnp.asarray

    def _rec_inputs():
        import jax
        import jax.numpy as jnp
        _gk = jax.random.key(seed)
        x = -0.000929 + 1 * jax.random.normal(jax.random.fold_in(_gk, 1), (3327, 128), jnp.float32)
        _a = jax.random.bernoulli(jax.random.fold_in(_gk, 2), 0.00240457, (3327, 3327))
        _a = jnp.logical_or(_a, jnp.eye(3327, dtype=bool))
        _af = _a.astype(jnp.float32)
        _af = _af * jax.random.uniform(jax.random.fold_in(_gk, 3), (3327, 3327), jnp.float32, 0.05, 1)
        adj = _af
        return (x, adj)
    x, adj = _rec_inputs()

    def _L0_gnn_setup():
        import jax, jax.numpy as jnp
        import numpy as np
        N, H, HEADS = (2048, 128, 3)
        ALPHA = 0.2
        NEG_INF = -9000000000000000.0

        def _sign_adj(key, n, density):
            k1, k2 = jax.random.split(key)
            mask = jax.random.uniform(k1, (n, n)) < density
            sign = jnp.where(jax.random.uniform(k2, (n, n)) < 0.5, -1.0, 1.0)
            adj = jnp.where(mask, sign, 0.0).astype(jnp.float32)
            idx = jnp.arange(n)
            return adj.at[idx, idx].set(1.0)

        def _gru_cell(x, hstate, Wih, Whh, bih, bhh):
            gi = x @ Wih.T + bih
            gh = hstate @ Whh.T + bhh
            ir, iz, inn = jnp.split(gi, 3, axis=1)
            hr, hz, hn = jnp.split(gh, 3, axis=1)
            r = jax.nn.sigmoid(ir + hr)
            z = jax.nn.sigmoid(iz + hz)
            n = jnp.tanh(inn + r * hn)
            return (1.0 - z) * n + z * hstate

        def _gat_head(h, node_adj, edge_adj, W, a):
            hW = h @ W
            hp = (node_adj > 0).astype(hW.dtype) @ hW
            hm = (node_adj < 0).astype(hW.dtype) @ hW
            e_plus = jax.nn.leaky_relu(jnp.concatenate([hp, hm], axis=1) @ a, ALPHA)[:, 0]
            e_minus = jax.nn.leaky_relu(jnp.concatenate([hm, hp], axis=1) @ a, ALPHA)[:, 0]
            att = jnp.where(edge_adj > 0, e_plus[None, :], NEG_INF)
            att = jnp.where(edge_adj < 0, e_minus[None, :], att)
            att = jax.nn.softmax(att, axis=1)
            return att * edge_adj @ hW
        key = jax.random.key(seed)
        ks = jax.random.split(key, 16)
        std = 0.01
        gain = 1.414
        return {'h': jax.random.normal(ks[0], (N, H), jnp.float32), 'node_adj': _sign_adj(ks[1], N, 0.005), 'edge_adj': _sign_adj(ks[2], N, 0.005), 'gat_W': jax.random.normal(ks[3], (HEADS, H, H), jnp.float32) * (gain / np.sqrt(H, dtype=np.float32)), 'gat_a': jax.random.normal(ks[4], (HEADS, 2 * H, 1), jnp.float32) * 0.1, 'edge_Wih': jax.random.normal(ks[5], (3 * H, H), jnp.float32) * std, 'edge_Whh': jax.random.normal(ks[6], (3 * H, H), jnp.float32) * std, 'edge_bih': jnp.zeros((3 * H,), jnp.float32), 'edge_bhh': jnp.zeros((3 * H,), jnp.float32), 'node_Wih': jax.random.normal(ks[7], (3 * H, H), jnp.float32) * std, 'node_Whh': jax.random.normal(ks[8], (3 * H, H), jnp.float32) * std, 'node_bih': jnp.zeros((3 * H,), jnp.float32), 'node_bhh': jnp.zeros((3 * H,), jnp.float32)}
    _L0_gnn_all = _L0_gnn_setup()
    _L0_gnn_in = {k: v for k, v in _L0_gnn_all.items() if k in ('gat_W', 'gat_a', 'edge_Wih', 'edge_Whh', 'edge_bih', 'edge_bhh', 'node_Wih', 'node_Whh', 'node_bih', 'node_bhh')}
    del _L0_gnn_all

    def _L1_gnn_setup():
        import jax, jax.numpy as jnp
        import numpy as np
        key = jax.random.key(seed)
        k1, k2, k3, k4 = jax.random.split(key, 4)
        N, F_in, F_out = (4096, 128, 128)
        x = jax.random.normal(k1, (N, F_in), dtype=jnp.float32)
        adj = jax.random.uniform(k2, (N, N), dtype=jnp.float32)
        lim = 1.0 / np.sqrt(F_in)
        W = jax.random.uniform(k3, (F_out, F_in), dtype=jnp.float32, minval=-lim, maxval=lim)
        b = jax.random.uniform(k4, (F_out,), dtype=jnp.float32, minval=-lim, maxval=lim)
        return {'x': x, 'adj': adj, 'W': W, 'b': b}
    _L1_gnn_all = _L1_gnn_setup()
    _L1_gnn_in = {k: v for k, v in _L1_gnn_all.items() if k in ('W', 'b')}
    del _L1_gnn_all
    return {'x': x, 'adj': adj, 'L0_gnn_gat_W': _L0_gnn_in['gat_W'], 'L0_gnn_gat_a': _L0_gnn_in['gat_a'], 'L0_gnn_edge_Wih': _L0_gnn_in['edge_Wih'], 'L0_gnn_edge_Whh': _L0_gnn_in['edge_Whh'], 'L0_gnn_edge_bih': _L0_gnn_in['edge_bih'], 'L0_gnn_edge_bhh': _L0_gnn_in['edge_bhh'], 'L0_gnn_node_Wih': _L0_gnn_in['node_Wih'], 'L0_gnn_node_Whh': _L0_gnn_in['node_Whh'], 'L0_gnn_node_bih': _L0_gnn_in['node_bih'], 'L0_gnn_node_bhh': _L0_gnn_in['node_bhh'], 'L1_gnn_W': _L1_gnn_in['W'], 'L1_gnn_b': _L1_gnn_in['b']}

def reference(x, adj, L0_gnn_gat_W, L0_gnn_gat_a, L0_gnn_edge_Wih, L0_gnn_edge_Whh, L0_gnn_edge_bih, L0_gnn_edge_bhh, L0_gnn_node_Wih, L0_gnn_node_Whh, L0_gnn_node_bih, L0_gnn_node_bhh, L1_gnn_W, L1_gnn_b):
    import jax
    import jax.numpy as jnp

    def _L0_gnn_ref(h, node_adj, edge_adj, gat_W, gat_a, edge_Wih, edge_Whh, edge_bih, edge_bhh, node_Wih, node_Whh, node_bih, node_bhh):
        import jax, jax.numpy as jnp
        import numpy as np
        N, H, HEADS = (2048, 128, 3)
        ALPHA = 0.2
        NEG_INF = -9000000000000000.0

        def _sign_adj(key, n, density):
            k1, k2 = jax.random.split(key)
            mask = jax.random.uniform(k1, (n, n)) < density
            sign = jnp.where(jax.random.uniform(k2, (n, n)) < 0.5, -1.0, 1.0)
            adj = jnp.where(mask, sign, 0.0).astype(jnp.float32)
            idx = jnp.arange(n)
            return adj.at[idx, idx].set(1.0)

        def _gru_cell(x, hstate, Wih, Whh, bih, bhh):
            gi = x @ Wih.T + bih
            gh = hstate @ Whh.T + bhh
            ir, iz, inn = jnp.split(gi, 3, axis=1)
            hr, hz, hn = jnp.split(gh, 3, axis=1)
            r = jax.nn.sigmoid(ir + hr)
            z = jax.nn.sigmoid(iz + hz)
            n = jnp.tanh(inn + r * hn)
            return (1.0 - z) * n + z * hstate

        def _gat_head(h, node_adj, edge_adj, W, a):
            hW = h @ W
            hp = (node_adj > 0).astype(hW.dtype) @ hW
            hm = (node_adj < 0).astype(hW.dtype) @ hW
            e_plus = jax.nn.leaky_relu(jnp.concatenate([hp, hm], axis=1) @ a, ALPHA)[:, 0]
            e_minus = jax.nn.leaky_relu(jnp.concatenate([hm, hp], axis=1) @ a, ALPHA)[:, 0]
            att = jnp.where(edge_adj > 0, e_plus[None, :], NEG_INF)
            att = jnp.where(edge_adj < 0, e_minus[None, :], att)
            att = jax.nn.softmax(att, axis=1)
            return att * edge_adj @ hW
        dn = jnp.diag(node_adj)
        de = jnp.diag(edge_adj)
        idx = jnp.arange(node_adj.shape[0])
        node_adj_norm = node_adj.at[idx, idx].add(-dn)
        edge_adj_norm = edge_adj.at[idx, idx].add(-de)
        node_support = node_adj_norm @ h
        edge_output = _gru_cell(node_support, h, edge_Wih, edge_Whh, edge_bih, edge_bhh)
        edge_support = _gat_head(h, node_adj_norm, edge_adj_norm, gat_W[0], gat_a[0])
        for i in range(1, HEADS):
            edge_support = edge_support + _gat_head(h, node_adj_norm, edge_adj_norm, gat_W[i], gat_a[i])
        edge_support = edge_support / HEADS
        node_output = _gru_cell(edge_support, h, node_Wih, node_Whh, node_bih, node_bhh)
        return de[:, None] * edge_output + dn[:, None] * node_output

    def _L1_gnn_ref(x, adj, W, b):
        import jax, jax.numpy as jnp
        import numpy as np
        N = adj.shape[0]
        adj = adj + jnp.eye(N, dtype=adj.dtype)
        deg = adj.sum(axis=1)
        deg_inv_sqrt = deg ** (-0.5)
        deg_inv_sqrt = jnp.where(jnp.isinf(deg_inv_sqrt), 0.0, deg_inv_sqrt)
        adj_normalized = deg_inv_sqrt[:, None] * adj * deg_inv_sqrt[None, :]
        support = x @ W.T + b
        return adj_normalized @ support
    x = _layernorm(x + _L0_gnn_ref(x, adj, adj, L0_gnn_gat_W, L0_gnn_gat_a, L0_gnn_edge_Wih, L0_gnn_edge_Whh, L0_gnn_edge_bih, L0_gnn_edge_bhh, L0_gnn_node_Wih, L0_gnn_node_Whh, L0_gnn_node_bih, L0_gnn_node_bhh), axis=-1)
    x = _layernorm(x + _L1_gnn_ref(x, adj, L1_gnn_W, L1_gnn_b), axis=-1)
    return x

_drawn_inputs = setup_inputs


def setup_inputs(seed=0):
    import zlib

    import numpy as np

    out = dict(_drawn_inputs(seed))
    spreads = {'L0_gnn_edge_bih': (0.0, 0.38),
     'L0_gnn_edge_bhh': (0.0, 0.668),
     'L0_gnn_node_bih': (0.0, 0.413),
     'L0_gnn_node_bhh': (0.0, 0.644)}
    factors = {'L0_gnn_gat_W': 6.661,
     'L0_gnn_gat_a': 7.883,
     'L0_gnn_edge_Whh': 4.21,
     'L0_gnn_node_Wih': 6.642,
     'L0_gnn_node_Whh': 4.162}
    for name, (base, spread) in spreads.items():
        noise = np.random.default_rng([zlib.crc32(name.encode()), seed]).standard_normal(out[name].shape)
        drawn = base * np.exp(spread * noise) if base else spread * noise
        out[name] = jnp.asarray(drawn.astype(out[name].dtype))
    for name, factor in factors.items():
        out[name] = (out[name] * factor).astype(out[name].dtype)
    return out
```

```python
import concourse.bass as bass
from concourse import mybir
from concourse.alu_op_type import AluOpType as ALU
from contextlib import ExitStack


N = 3327
P = 128
T = (N + P - 1) // P
NP = T * P
H = 128
HEADS = 3
E2 = 2 * HEADS
EW = 32
COUNT = 3 * E2
ALPHA = 0.2
EPS = 1e-5
FLOOR = 104.0

F32 = mybir.dt.float32
F32R = mybir.dt.float32r
BF16 = mybir.dt.bfloat16
U8 = mybir.dt.uint8
I32 = mybir.dt.int32
ACT = mybir.ActivationFunctionType
AX = mybir.AxisListType.X

HALF = NP // 2
BANK = HALF // 4
CT = 6
CW = CT * P
CHUNKS = T // CT
RT = T - CHUNKS * CT


def slot_before(j, ring, steps):
    if j >= ring:
        return j - ring
    return max(k for k in range(steps) if k % ring == j % ring) - steps


def loads_before(j, ring):
    return j // ring


def loads_per_round(j, ring, steps):
    return len(range(j % ring, steps, ring))


class Tools:

    def __init__(self, nc, ctx):
        self.nc, self.ctx, self.n = nc, ctx, 0

    def sb(self, name, shape, dt=F32):
        return self.ctx.enter_context(self.nc.sbuf_tensor(name, shape, dt))

    def ps(self, name, shape, dt=F32):
        return self.ctx.enter_context(self.nc.psum_tensor(name, shape, dt))

    def sem(self, name):
        return self.ctx.enter_context(self.nc.semaphore(name))


def project(nc, keep, d):
    hw, upm, umm, x_hi, x_lo, ident, not_i = (keep[k] for k in ("hw", "up", "um", "x_hi", "x_lo", "ident", "not_i"))
    with ExitStack() as ctx:
        t = Tools(nc, ctx)
        xT = t.sb("a_xT", [P, NP])
        x_sb = t.sb("a_x", [P, T, H])
        wext = t.sb("a_wext", [P, HEADS * H + E2])
        a_row = t.sb("a_arow", [P, E2, H])
        junk = t.sb("a_junk", [P, H])
        u = t.sb("a_u", [P, T, E2])
        part = t.sb("a_part", [P, T, E2], BF16)
        rest = t.sb("a_rest", [P, T, E2])
        pp = [t.ps(f"a_pp{i}", [P, 512]) for i in range(4)]
        x_in, xT_in, w_in, a_in = t.sem("x_in"), t.sem("xT_in"), t.sem("w_in"), t.sem("a_in")
        zeroed, folded, mm, hw_out, u_out, link, made = (
            t.sem(s) for s in ("zeroed", "folded", "mm", "hw_out", "u_out", "link", "made"))
        block = ctx.enter_context(nc.Block())

        @block.sync
        def _(sp):
            sp.dma_start(wext[:, 0:HEADS * H], d["gat_w"]).then_inc(w_in, 16)
            sp.dma_start(xT[:, :], d["xT"]).then_inc(xT_in, 16)
            sp.dma_start(a_row[:, :, :].rearrange("p c f -> p (c f)"), d["gat_a"].partition_broadcast(P)).then_inc(a_in, 16)
            sp.dma_start(x_sb[:, :, :], d["x"]).then_inc(x_in, 16)

        @block.gpsimd
        def _(pool):
            pool.memset(ident[:, :], 0.0).then_inc(made, 1)
            pool.memset(not_i[:, :], 1.0).then_inc(made, 1)
            pool.wait_ge(made, 2)
            pool.affine_select(out=ident[:, :], in_=ident[:, :], compare_op=ALU.not_equal, fill=1.0,
                               base=0, pattern=[[-1, P]], channel_multiplier=1)
            pool.affine_select(out=not_i[:, :], in_=not_i[:, :], compare_op=ALU.not_equal, fill=0.0,
                               base=0, pattern=[[-1, P]], channel_multiplier=1)

        @block.tensor
        def _(pe):
            pe.wait_ge(w_in, 16)
            pe.wait_ge(folded, E2)
            pe.wait_ge(xT_in, 16)
            for k in range(T):
                if k >= 4:
                    pe.wait_ge(hw_out, k - 3)
                    pe.wait_ge(u_out, k - 3)
                nc.tensor.matmul(pp[k % 4][:, 0:HEADS * H + E2], xT[:, k * P:(k + 1) * P], wext[:, :],
                                 start=True, stop=True).then_inc(mm, 1)

        @block.scalar
        def _(act):
            for k in range(T):
                act.wait_ge(mm, k + 1)
                if k >= 1:
                    act.wait_ge(u_out, k + 1)
                else:
                    act.wait_ge(u_out, 1)
                nc.scalar.activation(hw[:, k, :], pp[k % 4][:, 0:HEADS * H], ACT.Copy).then_inc(hw_out, 1)

        @block.vector
        def _(dve):
            dve.memset(upm[:, :, :], 0.0).then_inc(zeroed, 1)
            dve.memset(umm[:, :, :], 0.0).then_inc(zeroed, 1)
            dve.wait_ge(w_in, 16)
            dve.wait_ge(a_in, 16)
            for c in range(E2):
                h, side = c % HEADS, c // HEADS
                if c:
                    dve.wait_ge(folded, c)
                dve.tensor_tensor_reduce(out=junk[:, :], in0=wext[:, h * H:(h + 1) * H], in1=a_row[:, 2 * h + side, :],
                                         scale=1.0, scalar=0.0, op0=ALU.mult, op1=ALU.add,
                                         accum_out=wext[:, HEADS * H + c:HEADS * H + c + 1]).then_inc(folded, 1)
            dve.wait_ge(x_in, 16)
            dve.tensor_copy(x_hi[:, :, :], x_sb[:, :, :]).then_inc(link, 1)
            dve.wait_ge(link, 1)
            dve.tensor_tensor(x_lo[:, :, :], x_sb[:, :, :], x_hi[:, :, :].bitcast(F32), ALU.subtract)
            for k in range(T):
                dve.wait_ge(mm, k + 1)
                dve.tensor_copy(u[:, k, :], pp[k % 4][:, HEADS * H:HEADS * H + E2]).then_inc(u_out, 1)
            dve.wait_ge(u_out, T)
            dve.wait_ge(zeroed, 2)
            n = 1

            def then(ins):
                nonlocal n
                n += 1
                ins.then_inc(link, 1)
                dve.wait_ge(link, n)

            def split(dst):
                then(dve.tensor_copy(part[:, :, :], u[:, :, :]))
                then(dve.tensor_copy(dst[:, :, 0:E2], part[:, :, :]))
                then(dve.tensor_tensor(rest[:, :, :], u[:, :, :], part[:, :, :], ALU.subtract))
                then(dve.tensor_copy(part[:, :, :], rest[:, :, :]))
                then(dve.tensor_copy(dst[:, :, E2:2 * E2], part[:, :, :]))
                then(dve.tensor_tensor(rest[:, :, :], rest[:, :, :], part[:, :, :], ALU.subtract))
                then(dve.tensor_copy(dst[:, :, 2 * E2:3 * E2], rest[:, :, :]))

            split(upm)
            then(dve.tensor_tensor(u[:, :, 0:HEADS], u[:, :, 0:HEADS], u[:, :, HEADS:E2], ALU.add))
            then(dve.tensor_copy(u[:, :, HEADS:E2], u[:, :, 0:HEADS]))
            split(umm)
            then(dve.memset(umm[:, :, COUNT:COUNT + 1], 1.0))


def aggregate(nc, keep, d):
    upm, umm, x_hi, x_lo, not_i, csum, ns, elog = (
        keep[k] for k in ("up", "um", "x_hi", "x_lo", "not_i", "csum", "ns", "elog"))
    RA, RB = 4, 2
    with ExitStack() as ctx:
        t = Tools(nc, ctx)
        at = [t.sb(f"b_at{i}", [P, HALF]) for i in range(RA)]
        hi = [t.sb(f"b_hi{i}", [P, HALF], F32R) for i in range(RB)]
        lo = [t.sb(f"b_lo{i}", [P, HALF], F32R) for i in range(RB)]
        sg = [t.sb(f"b_sg{i}", [P, HALF], BF16) for i in range(RB)]
        mi = [t.sb(f"b_mi{i}", [P, HALF], BF16) for i in range(RB)]
        acc_ns = [t.ps(f"b_ns{i}", [P, 512]) for i in range(4)]
        acc_e = [t.ps(f"b_e{i}", [P, 512]) for i in range(4)]
        at_in = [t.sem(f"at_in{i}") for i in range(RA)]
        diag_zero, act_done, lo_done, mask_done, sum_done, pe_done, acc_ready, ns_out, e_out, saved = (
            t.sem(s) for s in ("diag_zero", "act_done", "lo_done", "mask_done", "sum_done", "pe_done",
                               "acc_ready", "ns_out", "e_out", "saved"))
        hi_done = t.sem("hi_done")
        block = ctx.enter_context(nc.Block())

        @block.sync
        def _(sp):
            for half in range(2):
                for j in range(T):
                    before = T * half + slot_before(j, RA, T) + 1 + RA
                    sp.wait_ge(act_done, before)
                    sp.wait_ge(lo_done, before)
                    sp.wait_ge(sum_done, before)
                    sp.dma_start(at[j % RA][:, :], d["adjT"][j * P:(j + 1) * P, half * HALF:(half + 1) * HALF])\
                      .then_inc(at_in[j % RA], 16)

        @block.gpsimd
        def _(pool):
            pool.sem_inc(sum_done, RA)
            for half in range(2):
                for j in range(T):
                    pool.wait_ge(diag_zero, T * half + j + 1)
                    cs = csum[:, half * HALF:(half + 1) * HALF]
                    if j == 0:
                        pool.tensor_copy(cs, at[0][:, :]).then_inc(sum_done, 1)
                    else:
                        pool.wait_ge(sum_done, T * half + j + RA)
                        pool.tensor_tensor(cs, cs, at[j % RA][:, :], ALU.add).then_inc(sum_done, 1)

        @block.scalar
        def _(act):
            act.sem_inc(act_done, RA)
            act.sem_inc(ns_out, 1)
            with act.Fori(0, 2) as half:
                for j in range(T):
                    act.wait_ge(diag_zero, T * half + j + 1)
                    act.wait_ge(pe_done, T * half + slot_before(j, RB, T) + 1 + RB)
                    act.wait_ge(lo_done, T * half + slot_before(j, RB, T) + 1 + RA)
                    nc.scalar.activation(hi[j % RB][:, :], at[j % RA][:, :], ACT.Copy).then_inc(hi_done, 1)
                    nc.scalar.activation(sg[j % RB][:, :], at[j % RA][:, :], ACT.Sign).then_inc(act_done, 1)
                act.wait_ge(acc_ready, half + 1)
                for q in range(4):
                    nc.scalar.activation(ns[:, bass.ds(half * HALF + q * BANK, BANK)], acc_ns[q][:, 0:BANK],
                                         ACT.Copy).then_inc(ns_out, 1)

        @block.vector
        def _(dve):
            dve.sem_inc(lo_done, RA)
            dve.sem_inc(e_out, 1)
            for half in range(2):
                for j in range(T):
                    k = T * half + j
                    dve.wait_ge(at_in[j % RA], 16 * (half * loads_per_round(j, RA, T) + loads_before(j, RA) + 1))
                    c = j * P - half * HALF
                    if 0 <= c < HALF:
                        dve.tensor_tensor(at[j % RA][:, c:c + P], at[j % RA][:, c:c + P], not_i[:, :], ALU.mult)\
                           .then_inc(diag_zero, 1)
                        dve.wait_ge(diag_zero, k + 1)
                    else:
                        dve.sem_inc(diag_zero, 1)
                    dve.wait_ge(pe_done, k + 1)
                    dve.tensor_scalar(mi[j % RB][:, :], at[j % RA][:, :], 0.0, None, ALU.is_lt).then_inc(mask_done, 1)
                    dve.wait_ge(hi_done, k + 1)
                    dve.tensor_tensor(lo[j % RB][:, :], at[j % RA][:, :], hi[j % RB][:, :].bitcast(F32), ALU.subtract)\
                       .then_inc(lo_done, 1)
                dve.wait_ge(acc_ready, half + 1)
                for q in range(4):
                    at0 = half * HALF + q * BANK
                    dve.tensor_copy(elog[:, at0:at0 + BANK], acc_e[q][0:EW, 0:BANK]).then_inc(e_out, 1)

        @block.tensor
        def _(pe):
            pe.sem_inc(pe_done, RB)
            with pe.Fori(0, 2) as half:
                for j in range(T):
                    k = T * half + j
                    first, last = j == 0, j == T - 1
                    if first:
                        pe.wait_ge(ns_out, 4 * half + 1)
                        pe.wait_ge(e_out, 4 * half + 1)
                    pe.wait_ge(act_done, k + 1 + RA)
                    for w, m in ((x_hi, hi), (x_lo, hi)):
                        for q in range(4):
                            nc.tensor.matmul(acc_ns[q][:, 0:BANK], w[:, j, :], m[j % RB][:, q * BANK:(q + 1) * BANK],
                                             start=first and w is x_hi, stop=False)
                    for q in range(4):
                        nc.tensor.matmul(acc_e[q][0:EW, 0:BANK], upm[:, j, :], sg[j % RB][:, q * BANK:(q + 1) * BANK],
                                         start=first, stop=False)
                    pe.wait_ge(lo_done, k + 1 + RA)
                    pe.wait_ge(mask_done, k + 1)
                    for q in range(4):
                        nc.tensor.matmul(acc_ns[q][:, 0:BANK], x_hi[:, j, :], lo[j % RB][:, q * BANK:(q + 1) * BANK],
                                         start=False, stop=last)
                    for q in range(4):
                        mm = nc.tensor.matmul(acc_e[q][0:EW, 0:BANK], umm[:, j, :], mi[j % RB][:, q * BANK:(q + 1) * BANK],
                                              start=False, stop=last)
                    mm.then_inc(pe_done, 1)
                pe.wait_ge(pe_done, T * half + T + RB)
                pe.sem_inc(acc_ready, 1)


def logits(nc, keep, d):
    csum, elog, ecol, flag, dinv, diag, diag1, ident = (
        keep[k] for k in ("csum", "elog", "ecol", "flag", "dinv", "diag", "diag1", "ident"))
    CW7 = E2 + 1
    with ExitStack() as ctx:
        t = Tools(nc, ctx)
        sel = t.sb("c_sel", [EW, CW7])
        ones = t.sb("c_ones", [P, 1])
        raw = t.sb("c_raw", [P, T, CW7])
        e = t.sb("c_e", [P, T, E2])
        red = t.sb("c_red", [P, CW7])
        redg = t.sb("c_redg", [P, CW7])
        shift = t.sb("c_shift", [P, E2])
        erow = t.sb("c_erow", [HEADS * T, 2, P])
        deg = t.sb("c_deg", [P, T])
        root = t.sb("c_root", [P, T])
        safe = t.sb("c_safe", [P, T])
        quot = t.sb("c_quot", [P, T])
        some = t.sb("c_some", [P, T])
        p_e = t.ps("c_pe", [P, T, CW7])
        p_d = t.ps("c_pd", [P, T])
        p_t = t.ps("c_pt", [HEADS * T, 2, P])
        mm, made, link, reduced, everywhere, shifted, turned, copied, saved, deg_made, rooted, diag_in = (
            t.sem(s) for s in ("mm", "made", "link", "reduced", "everywhere", "shifted", "turned", "copied",
                               "e_saved", "deg_made", "rooted", "diag_in"))
        block = ctx.enter_context(nc.Block())

        @block.sync
        def _(sp):
            sp.dma_start(diag[:, :], d["diag"]).then_inc(diag_in, 16)
            sp.wait_ge(copied, 1)
            sp.dma_start(d["e_rows"].rearrange("s (c p) -> c s p", p=P), erow[:, :, :]).then_inc(saved, 16)
            sp.dma_start(d["ns"], keep["ns"][:, :]).then_inc(saved, 16)
            sp.wait_ge(saved, 32)

        @block.tensor
        def _(pe):
            pe.wait_ge(made, 2)
            for k in range(T):
                nc.tensor.matmul(p_e[:, k, :], elog[0:EW, k * P:(k + 1) * P], sel[:, :], start=True, stop=True)
            for k in range(T):
                m = nc.tensor.matmul(p_d[:, k:k + 1], csum[:, k * P:(k + 1) * P], ones[:, :], start=True, stop=True)
            m.then_inc(mm, 1)
            pe.wait_ge(shifted, 1)
            for s in range(2):
                m = nc.tensor.transpose(p_t[:, s, :], ecol[:, s * HEADS * T:(s + 1) * HEADS * T], ident[:, :])
            m.then_inc(turned, 1)

        @block.scalar
        def _(act):
            act.wait_ge(deg_made, 1)
            nc.scalar.activation(root[:, :], deg[:, :], ACT.Sqrt).then_inc(rooted, 1)

        @block.gpsimd
        def _(pool):
            pool.wait_ge(reduced, 1)
            pool.partition_all_reduce(redg[:, :], red[:, :], P, bass.bass_isa.ReduceOp.max).then_inc(everywhere, 1)

        @block.vector
        def _(dve):
            n = 0

            def then(ins):
                nonlocal n
                n += 1
                ins.then_inc(link, 1)
                dve.wait_ge(link, n)

            dve.memset(ones[:, :], 1.0).then_inc(made, 1)
            then(dve.tensor_tensor(sel[:, 0:E2], ident[0:EW, 0:E2], ident[0:EW, E2:2 * E2], ALU.add))
            then(dve.tensor_tensor(sel[:, 0:E2], sel[:, 0:E2], ident[0:EW, 2 * E2:3 * E2], ALU.add))
            dve.tensor_copy(sel[:, E2:CW7], ident[0:EW, COUNT:COUNT + 1]).then_inc(made, 1)
            dve.wait_ge(mm, 1)
            then(dve.tensor_copy(raw[:, :, :], p_e[:, :, :]))
            dve.wait_ge(diag_in, 16)
            then(dve.tensor_scalar(diag1[:, :], diag[:, :], 1.0, None, ALU.add))
            then(dve.tensor_tensor(deg[:, :], p_d[:, :], diag1[:, :], ALU.add))
            dve.sem_inc(deg_made, 1)
            then(dve.scalar_tensor_tensor(e[:, :, :], raw[:, :, 0:E2], ALPHA, raw[:, :, 0:E2], ALU.mult, ALU.max))
            then(dve.tensor_reduce(red[:, 0:E2], e[:, :, :].rearrange("p t c -> p c t"), AX, ALU.min))
            then(dve.tensor_scalar(red[:, 0:E2], red[:, 0:E2], -1.0, None, ALU.mult))
            dve.tensor_reduce(red[:, E2:CW7], raw[:, :, E2:CW7].rearrange("p t c -> p c t"), AX, ALU.add)\
               .then_inc(reduced, 1)
            dve.wait_ge(rooted, 1)
            then(dve.tensor_scalar(safe[:, :], root[:, :], 1e-30, None, ALU.max))
            then(dve.reciprocal(quot[:, :], safe[:, :]))
            then(dve.tensor_tensor(quot[:, :], quot[:, :], deg[:, :], ALU.mult))
            then(dve.tensor_tensor(safe[:, :], safe[:, :], quot[:, :], ALU.add))
            then(dve.tensor_scalar(safe[:, :], safe[:, :], 0.5, None, ALU.mult))
            then(dve.reciprocal(quot[:, :], safe[:, :]))
            then(dve.tensor_scalar(some[:, :], deg[:, :], 0.0, None, ALU.not_equal))
            then(dve.tensor_tensor(quot[:, :], quot[:, :], some[:, :], ALU.mult))
            then(dve.tensor_scalar(root[:, :], root[:, :], 0.0, None, ALU.mult))
            then(dve.tensor_tensor(dinv[:, :], quot[:, :], root[:, :], ALU.add))
            dve.wait_ge(everywhere, 1)
            then(dve.tensor_tensor(shift[:, 0:HEADS], redg[:, 0:HEADS], redg[:, HEADS:E2], ALU.max))
            then(dve.tensor_scalar(shift[:, 0:HEADS], shift[:, 0:HEADS], FLOOR, None, ALU.add))
            then(dve.tensor_copy(shift[:, HEADS:E2], shift[:, 0:HEADS]))
            dve.tensor_tensor(ecol[:, :].rearrange("p (c t) -> p c t", t=T), e[:, :, :].rearrange("p t c -> p c t"),
                              shift[:, :].unsqueeze(2).broadcast_to([P, E2, T]), ALU.add).then_inc(shifted, 1)
            then(dve.tensor_copy(flag[:, :], redg[:, E2:CW7]))
            dve.wait_ge(turned, 1)
            dve.tensor_copy(erow[:, :, :], p_t[:, :, :]).then_inc(copied, 1)


def attend(nc, keep, d):
    hw, ecol, ident, not_i = (keep[k] for k in ("hw", "ecol", "ident", "not_i"))
    RA, RE, RW = 4, 6, 6
    CREDIT = 16
    HW = CW // 2
    UNITS = [(j, h) for j in range(T) for h in range(HEADS)]
    ON_DVE = [(j, h) for j, h in UNITS if h == 2 and j % 3 == 1]
    ON_POOL = [u for u in UNITS if u not in ON_DVE]
    ND, NPL, NU = len(ON_DVE), len(ON_POOL), len(UNITS)
    with ExitStack() as ctx:
        t = Tools(nc, ctx)
        erow = t.sb("d_erow", [P, HEADS, NP])
        arow = [t.sb(f"d_arow{i}", [P, HALF]) for i in range(2)]
        ones_not_i = t.sb("d_ones_not_i", [P, 2 * CHUNKS - 1, P], BF16)
        mask = t.sb("d_mask", [P, NP], U8)
        L = [t.sb(f"d_l{i}", [P, NP]) for i in range(2)]
        mx = t.sb("d_mx", [P, HEADS * CT])
        scratch = t.sb("d_scratch", [P, 1])
        nm = t.sb("d_nm", [P, HEADS * CT])
        den = t.sb("d_den", [P, HEADS * CT])
        rden = t.sb("d_rden", [P, HEADS * CT])
        nmb = t.sb("d_nmb", [P, 2, HEADS, CW])
        invb = t.sb("d_invb", [P, HEADS, CW])
        at = [t.sb(f"d_at{i}", [P, CW]) for i in range(RA)]
        ex = [t.sb(f"d_ex{i}", [P, CW]) for i in range(RE)]
        W = [t.sb(f"d_w{i}", [P, CW]) for i in range(RW)]
        es = t.sb("d_es", [P, CW])
        es2 = t.sb("d_es2", [P, CW])
        acc = [t.ps(f"d_acc{h}", [P, 2, 512]) for h in range(HEADS)]
        aux = [t.ps(f"d_aux{i}", [P, 512]) for i in range(2)]
        at_in = [t.sem(f"at_in{i}") for i in range(RA)]
        arow_in = [t.sem(f"arow_in{i}") for i in range(2)]
        (erow_in, arow_read, arg_made, logit_made, nm_made, row_exp, exp_made, w_dve, w_pool, unit_done,
         spread, spread_out, rden_made, acc_free, es_made, es_saved, link) = (
            t.sem(s) for s in ("erow_in", "arow_read", "arg_made", "logit_made", "nm_made", "row_exp", "exp_made",
                               "w_dve", "w_pool", "unit_done", "spread", "spread_out", "rden_made", "acc_free",
                               "es_made", "es_saved", "d_link"))
        es_added, cleared, mask_whole = t.sem("es_added"), t.sem("cleared"), t.sem("mask_whole")
        first_seen = t.sem("first_seen")
        diag_zero, table_made = t.sem("diag_zero"), t.sem("table_made")
        block = ctx.enter_context(nc.Block())

        def tiles(q):
            return RT if isinstance(q, int) and q == 0 else CT

        def first_tile(q):
            return T - RT if isinstance(q, int) and q == 0 else (q - 1) * CT

        def tiles_before(q):
            return 0 if isinstance(q, int) and q == 0 else (q - 1) * CT + RT

        def width(q):
            return tiles(q) * P

        def weights_of(eng, q, j, h):
            back, j = (1, j + T) if j < 0 else (0, j)
            on, counter, per = (ON_POOL, w_pool, NPL) if (j, h) in ON_POOL else (ON_DVE, w_dve, ND)
            eng.wait_ge(counter, per * q + on.index((j, h)) + 1 - per * back + CREDIT)

        def row_step(r):
            return 3 + r * 20 // (HEADS * CT)

        def load_step(k, half):
            return 10 * k // 3 + 5 + half

        def spreads(k):
            return [(h, a, min(CT // 2, k - a)) for h in range(HEADS) for a in range(0, k, CT // 2)]

        def bank(q, i, inverse):
            return (i + (len(spreads(tiles(q))) if inverse else 0)) % 2

        def spreads_before(q):
            if isinstance(q, int) and q == 0:
                return 0
            return len(spreads(RT)) + (q - 1) * len(spreads(CT))

        def each_chunk(eng, step):
            step(0, True)
            with eng.Fori(1, CHUNKS) as q:
                step(q, True)
            step(CHUNKS, False)

        @block.sync
        def _(sp):
            def row_half(q, k, half):
                n = tiles_before(q) + k
                r0 = (first_tile(q) + k) * P
                if not isinstance(r0, int):
                    r0 = sp.snap(r0)
                sp.wait_ge(arow_read, 2 * n + half - 1 + CREDIT)
                sp.dma_start(arow[half][:, :], d["adj"][bass.ds(r0, P), half * HALF:(half + 1) * HALF])\
                  .then_inc(arow_in[half], 16)

            def chunk(q, more):
                w = width(q)
                col0 = first_tile(q) * P
                if not isinstance(q, int):
                    col0 = sp.snap(col0)
                for j in range(T):
                    before = slot_before(j, RA, T)
                    sp.wait_ge(unit_done, NU * q + HEADS * before + HEADS + CREDIT)
                    sp.dma_start(at[j % RA][:, 0:w], d["adjT"][j * P:(j + 1) * P, bass.ds(col0, w)])\
                      .then_inc(at_in[j % RA], 16)
                    if more:
                        for k in range(CT):
                            for half in range(2):
                                if load_step(k, half) == j:
                                    row_half(q + 1, k, half)
                sp.wait_ge(es_made, q + 1)
                sp.dma_start(d["es"][:, bass.ds(col0, w)], es[:, 0:w]).then_inc(es_saved, 16)

            for k in range(2):
                for half in range(2):
                    row_half(0, k, half)
                if k == 0:
                    for h in range(HEADS):
                        sp.dma_start(erow[:, h, :], d["e_rows"][0, h * NP:(h + 1) * NP].partition_broadcast(P))\
                          .then_inc(erow_in, 16)
            each_chunk(sp, chunk)
            sp.wait_ge(es_saved, 16 * (CHUNKS + 1))

        @block.gpsimd
        def _(pool):
            pool.sem_inc(w_pool, CREDIT)
            pool.memset(ones_not_i[:, :, :], 1.0).then_inc(table_made, 1)
            pool.wait_ge(table_made, 1)
            pool.tensor_copy(ones_not_i[:, CHUNKS - 1, :], not_i[:, :]).then_inc(table_made, 1)
            pool.wait_ge(table_made, 2)

            def arrived(q, j):
                pool.wait_ge(at_in[j % RA], 16 * (q * loads_per_round(j, RA, T) + loads_before(j, RA) + 1))

            def zero_diagonal(q, j):
                c = slice(j % CT * P, (j % CT + 1) * P)
                a = at[j % RA]
                small = j // CT == CHUNKS
                if isinstance(q, int):
                    if (q == 0) == small and (small or q == j // CT + 1):
                        pool.tensor_tensor(a[:, c], a[:, c], not_i[:, :], ALU.mult).then_inc(diag_zero, 1)
                        return
                elif not small:
                    which = ones_not_i[:, bass.ds(q - (j // CT + 1) + CHUNKS - 1, 1), :]
                    pool.tensor_tensor(a[:, c], a[:, c], which.rearrange("p a n -> p (a n)"), ALU.mult).then_inc(diag_zero, 1)
                    return
                pool.sem_inc(diag_zero, 1)

            def chunk(q, more):
                w = width(q)
                for j, h in ON_POOL:
                    u = 3 * j + h
                    last = (j, h + 1) not in ON_POOL
                    if last and j + 1 < T:
                        arrived(q, j + 1)
                    pool.wait_ge(diag_zero, T * q + j + 1)
                    pool.wait_ge(exp_made, NU * q + u + 1)
                    pool.wait_ge(unit_done, NU * q + u - RW + 1 + CREDIT)
                    pool.tensor_tensor(W[u % RW][:, 0:w], ex[u % RE][:, 0:w], at[j % RA][:, 0:w], ALU.mult)\
                        .then_inc(w_pool, 1)
                    if last and j + 1 < T:
                        zero_diagonal(q, j + 1)
                    elif last and more:
                        arrived(q + 1, 0)
                        pool.sem_inc(first_seen, 1)
                        zero_diagonal(q + 1, 0)

            arrived(0, 0)
            zero_diagonal(0, 0)
            each_chunk(pool, chunk)

        @block.scalar
        def _(act):
            act.sem_inc(row_exp, CREDIT)

            def row_unit(q, r):
                u = HEADS * tiles_before(q) + r
                k, h = divmod(r, HEADS)
                s = h * CT + k
                act.wait_ge(nm_made, u + 1)
                nc.scalar.activation(L[r % 2][:, :], L[r % 2][:, :], ACT.Exp, bias=nm[:, s:s + 1],
                                     accum_out=den[:, s:s + 1]).then_inc(row_exp, 1)

            def chunk(q, more):
                w = width(q)
                for j in range(T):
                    for h in range(HEADS):
                        u = 3 * j + h
                        act.wait_ge(arg_made, NU * q + u + 1)
                        nc.scalar.activation(ex[u % RE][:, 0:w], ex[u % RE][:, 0:w], ACT.Exp).then_inc(exp_made, 1)
                    if more:
                        for r in range(HEADS * CT):
                            if row_step(r) + 1 == j:
                                row_unit(q + 1, r)

            for r in range(HEADS * RT):
                row_unit(0, r)
            each_chunk(act, chunk)

        @block.vector
        def _(dve):
            dve.sem_inc(logit_made, CREDIT)
            dve.sem_inc(arow_read, CREDIT)
            dve.sem_inc(w_dve, CREDIT)
            dve.sem_inc(acc_free, HEADS)

            def mask_tile(q, k):
                n = tiles_before(q) + k
                for half in range(2):
                    dve.wait_ge(arow_in[half], 16 * n + 16)
                    dve.tensor_scalar(mask[:, half * HALF:(half + 1) * HALF], arow[half][:, :], 0.0, None, ALU.is_gt)\
                       .then_inc(arow_read, 1)
                dve.wait_ge(arow_read, 2 * n + 2 + CREDIT)
                c = bass.ds((first_tile(q) + k) * P, P)
                dve.tensor_tensor(mask[:, c], mask[:, c], not_i[:, :], ALU.mult).then_inc(mask_whole, 1)
                dve.wait_ge(mask_whole, n + 1)

            def args(q, j):
                if j == 0:
                    dve.wait_ge(spread_out, 2 * spreads_before(q) + len(spreads(tiles(q))))
                for h in range(HEADS):
                    u = 3 * j + h
                    weights_of(dve, q, j - 2, h)
                    dve.tensor_scalar(ex[u % RE][:, 0:width(q)],
                                      nmb[:, bass.ds(q & 1, 1), h, 0:width(q)].rearrange("p a n -> p (a n)"),
                                      ecol[:, h * T + j:h * T + j + 1], 0.0, ALU.add, ALU.min).then_inc(arg_made, 1)

            def row_unit(q, r):
                u = HEADS * tiles_before(q) + r
                k, h = divmod(r, HEADS)
                s = h * CT + k
                if h == 0:
                    mask_tile(q, k)
                dve.wait_ge(row_exp, u - 1 + CREDIT)
                dve.memset(scratch[:, :], 0.0)
                dve.wait_ge(erow_in, 16 * HEADS)
                dve.tensor_tensor_reduce(out=L[r % 2][:, :], in0=mask[:, :], in1=erow[:, h, :], scale=1.0,
                                         scalar=0.0, op0=ALU.mult, op1=ALU.max,
                                         accum_out=mx[:, s:s + 1]).then_inc(logit_made, 1)
                dve.wait_ge(logit_made, u + 1 + CREDIT)
                dve.tensor_scalar(nm[:, s:s + 1], mx[:, s:s + 1], -1.0, None, ALU.mult).then_inc(nm_made, 1)

            def invert(q):
                dve.wait_ge(row_exp, HEADS * (tiles_before(q) + tiles(q)) + CREDIT)
                dve.reciprocal(rden[:, :], den[:, :]).then_inc(link, 1)
                dve.wait_ge(link, 2 * q + 1)
                dve.tensor_scalar(rden[:, :], rden[:, :], 1.0 / HEADS, None, ALU.mult).then_inc(link, 1)
                dve.wait_ge(link, 2 * q + 2)

            def take(q, i, into):
                h, a, n = spreads(tiles(q))[i]
                done = 2 * spreads_before(q) + i + (0 if into is nmb else len(spreads(tiles(q))))
                dve.wait_ge(spread, done + 1)
                c = slice(a * P, (a + n) * P)
                out = nmb[:, bass.ds(q & 1, 1), h, c].rearrange("p a n -> p (a n)") if into is nmb else invb[:, h, c]
                dve.tensor_copy(out, aux[bank(q, i, into is invb)][:, 0:n * P]).then_inc(spread_out, 1)

            def chunk(q, more):
                w = width(q)
                for j in range(T):
                    if j + 1 < T:
                        args(q, j + 1)
                    for h in range(HEADS):
                        if (j, h) not in ON_DVE:
                            continue
                        u = 3 * j + h
                        dve.wait_ge(diag_zero, T * q + j + 1)
                        dve.wait_ge(exp_made, NU * q + u + 1)
                        dve.wait_ge(unit_done, NU * q + u - RW + 1 + CREDIT)
                        dve.tensor_tensor(W[u % RW][:, 0:w], ex[u % RE][:, 0:w], at[j % RA][:, 0:w], ALU.mult)\
                           .then_inc(w_dve, 1)
                    if 1 <= j and j - 1 < len(spreads(tiles(q))):
                        take(q, j - 1, invb)
                    if more:
                        for r in range(HEADS * CT):
                            if row_step(r) == j:
                                row_unit(q + 1, r)
                        if j == T - 2:
                            invert(q + 1)
                            for i in range(len(spreads(CT))):
                                take(q + 1, i, nmb)
                        if j == T - 1:
                            args(q + 1, 0)
                if not isinstance(q, int) or q > 0:
                    dve.wait_ge(es_saved, 16 * q)
                dve.wait_ge(spread_out, 2 * spreads_before(q) + 2 * len(spreads(tiles(q))))
                wb = min(w, HW)
                for h in range(HEADS):
                    dve.wait_ge(unit_done, NU * q + NU - HEADS + h + 1 + CREDIT)
                    a = acc[h][:, 0:w // wb, 0:wb]
                    i = invb[:, h, 0:w].rearrange("p (b n) -> p b n", n=wb)
                    o = (es if h == 0 else es2)[:, 0:w].rearrange("p (b n) -> p b n", n=wb)
                    dve.tensor_tensor(o, a, i, ALU.mult).then_inc(acc_free, 1)
                    dve.wait_ge(acc_free, HEADS * q + h + 1 + HEADS)
                    if h:
                        last = dve.tensor_tensor(es[:, 0:w], es[:, 0:w], es2[:, 0:w], ALU.add)
                        last.then_inc(es_added if h < HEADS - 1 else es_made, 1)
                        if h < HEADS - 1:
                            dve.wait_ge(es_added, q + 1)

            dve.memset(den[:, :], 1.0).then_inc(cleared, 1)
            dve.wait_ge(cleared, 1)
            for r in range(HEADS * RT):
                row_unit(0, r)
            invert(0)
            for i in range(len(spreads(RT))):
                take(0, i, nmb)
            args(0, 0)
            each_chunk(dve, chunk)

        @block.tensor
        def _(pe):
            pe.sem_inc(unit_done, CREDIT)

            def send(q, i, src):
                h, a, n = spreads(tiles(q))[i]
                done = 2 * spreads_before(q) + i + (0 if src is nm else len(spreads(tiles(q))))
                if not isinstance(done, int) or done > 1:
                    pe.wait_ge(spread_out, done - 1)
                for k in range(a, a + n):
                    s = h * CT + k
                    m = nc.tensor.matmul(aux[bank(q, i, src is rden)][:, (k - a) * P:(k - a + 1) * P],
                                         src[:, s:s + 1].to_broadcast([P, P]), ident[:, :], start=True, stop=True)
                m.then_inc(spread, 1)

            def chunk(q, more):
                w = width(q)
                for j in range(T):
                    for h in range(HEADS):
                        if j == 0:
                            pe.wait_ge(acc_free, HEADS * q + h + 1)
                        weights_of(pe, q, j, h)
                        for b in range(0, w, HW):
                            n = min(HW, w - b)
                            m = nc.tensor.matmul(acc[h][:, b // HW, 0:n], hw[:, j, h * H:(h + 1) * H],
                                                 W[(3 * j + h) % RW][:, b:b + n], start=(j == 0), stop=(j == T - 1))
                        m.then_inc(unit_done, 1)
                    if j < len(spreads(tiles(q))):
                        send(q, j, rden)
                    if more and j == T - 2:
                        pe.wait_ge(link, 2 * (q + 1) + 2)
                        for i in range(len(spreads(CT))):
                            send(q + 1, i, nm)

            pe.wait_ge(link, 2)
            for i in range(len(spreads(RT))):
                send(0, i, nm)
            each_chunk(pe, chunk)


def attend_signed(nc, keep, d):
    hw, ident, not_i, flag = (keep[k] for k in ("hw", "ident", "not_i", "flag"))
    GROUPS = [list(range(g, min(g + 4, T))) for g in range(0, T, 4)]
    NG = len(GROUPS)
    with ExitStack() as ctx:
        t = Tools(nc, ctx)
        arow = t.sb("g_arow", [P, NP])
        plus = t.sb("g_plus", [P, NP])
        minus = t.sb("g_minus", [P, NP])
        L = t.sb("g_l", [P, NP])
        W = t.sb("g_w", [P, NP])
        wt = t.sb("g_wt", [P, 512])
        mx, nm, den, rden = (t.sb(f"g_{s}", [P, 1]) for s in ("mx", "nm", "den", "rden"))
        est = t.sb("g_est", [P, P])
        turn = t.ps("g_turn", [P, 512])
        acc = t.ps("g_acc", [P, P])
        (a_in, e_in, diag_zero, logit, prob, weight, turned, copied, multiplied, est_made, est_saved, est_seen, link) = (
            t.sem(s) for s in ("g_a_in", "g_e_in", "g_diag", "g_logit", "g_prob", "g_weight", "g_turned", "g_copied",
                               "g_multiplied", "g_est_made", "g_est_saved", "g_est_seen", "g_link"))
        block = ctx.enter_context(nc.Block())

        def when_signed(eng, program, credits=(), end=lambda: None):
            negative = eng.value_load(flag[0:1, 0:1], min_val=0, max_val=1 << 24)
            with eng.If(negative > 0):
                for counter, n in credits:
                    eng.sem_inc(counter, n)
                with eng.Fori(0, T) as i:
                    program(i)
                end()

        @block.sync
        def _(sp):
            def tile(i):
                at_tile = sp.snap(i * P)
                sp.wait_ge(weight, HEADS * i + 1)
                sp.dma_start(arow[:, :], d["adj"][bass.ds(at_tile, P), :]).then_inc(a_in, 16)
                for h in range(HEADS):
                    sp.wait_ge(weight, HEADS * i + h + 1)
                    sp.dma_start(plus[:, :], d["e_rows"][0, h * NP:(h + 1) * NP].partition_broadcast(P)).then_inc(e_in, 16)
                    sp.dma_start(minus[:, :], d["e_rows"][1, h * NP:(h + 1) * NP].partition_broadcast(P)).then_inc(e_in, 16)
                sp.wait_ge(est_made, i + 2)
                sp.sem_inc(est_seen, 1)
                sp.dma_start(d["es"][:, bass.ds(at_tile, P)], est[:, :]).then_inc(est_saved, 16)
            when_signed(sp, tile, [(est_saved, 16)], lambda: sp.wait_ge(est_saved, 16 * T + 16))

        @block.scalar
        def _(act):
            def tile(i):
                for h in range(HEADS):
                    act.wait_ge(logit, HEADS * i + h + 1)
                    nc.scalar.activation(L[:, :], L[:, :], ACT.Exp, bias=nm[:, :], accum_out=den[:, :]).then_inc(prob, 1)
                    for g, group in enumerate(GROUPS):
                        n = NG * (HEADS * i + h) + g
                        act.wait_ge(turned, n + 1)
                        act.wait_ge(multiplied, n + 1)
                        nc.scalar.activation(wt[:, 0:len(group) * P], turn[:, 0:len(group) * P], ACT.Copy).then_inc(copied, 1)
            when_signed(act, tile, [(copied, 1)])

        @block.vector
        def _(dve):
            def tile(i):
                dve.wait_ge(a_in, 16 * i + 16)
                c = bass.ds(i * P, P)
                dve.tensor_tensor(arow[:, c], arow[:, c], not_i[:, :], ALU.mult).then_inc(diag_zero, 1)
                dve.wait_ge(diag_zero, i + 1)
                for h in range(HEADS):
                    u = HEADS * i + h
                    n = 0

                    def then(ins):
                        nonlocal n
                        n += 1
                        ins.then_inc(link, 1)
                        dve.wait_ge(link, 6 * u + n)

                    dve.wait_ge(e_in, 32 * u + 32)
                    then(dve.scalar_tensor_tensor(plus[:, :], arow[:, :], 0.0, plus[:, :], ALU.is_gt, ALU.mult))
                    then(dve.scalar_tensor_tensor(minus[:, :], arow[:, :], 0.0, minus[:, :], ALU.is_lt, ALU.mult))
                    then(dve.tensor_tensor(L[:, :], plus[:, :], minus[:, :], ALU.add))
                    then(dve.tensor_reduce(mx[:, :], L[:, :], AX, ALU.max))
                    dve.tensor_scalar(nm[:, :], mx[:, :], -1.0, None, ALU.mult).then_inc(logit, 1)
                    dve.wait_ge(prob, u + 1)
                    then(dve.reciprocal(rden[:, :], den[:, :]))
                    then(dve.tensor_scalar(rden[:, :], rden[:, :], 1.0 / HEADS, None, ALU.mult))
                    dve.wait_ge(multiplied, NG * u + 1)
                    dve.scalar_tensor_tensor(W[:, :], L[:, :], rden[:, :], arow[:, :], ALU.mult, ALU.mult)\
                       .then_inc(weight, 1)
                dve.wait_ge(multiplied, NG * HEADS * i + NG * HEADS + 1)
                dve.wait_ge(est_saved, 16 * i + 16)
                dve.tensor_copy(est[:, :], acc[:, :]).then_inc(est_made, 1)
            when_signed(dve, tile, [(weight, 1), (est_made, 1)])

        @block.tensor
        def _(pe):
            def tile(i):
                pe.wait_ge(est_made, i + 1)
                for h in range(HEADS):
                    pe.wait_ge(weight, HEADS * i + h + 2)
                    for g, group in enumerate(GROUPS):
                        n = NG * (HEADS * i + h) + g
                        pe.wait_ge(copied, n + 1)
                        for s, j in enumerate(group):
                            m = nc.tensor.transpose(turn[:, s * P:(s + 1) * P], W[:, j * P:(j + 1) * P], ident[:, :])
                        m.then_inc(turned, 1)
                        pe.wait_ge(copied, n + 2)
                        for s, j in enumerate(group):
                            m = nc.tensor.matmul(acc[:, :], hw[:, j, h * H:(h + 1) * H], wt[:, s * P:(s + 1) * P],
                                                 start=(h == 0 and j == 0), stop=(h == HEADS - 1 and j == T - 1))
                        m.then_inc(multiplied, 1)
            when_signed(pe, tile, [(multiplied, 1)])


def gru(nc, keep, d):
    go = keep["go"]
    CHUNK = BANK
    NC = NP // CHUNK
    with ExitStack() as ctx:
        t = Tools(nc, ctx)
        xT, ns, es = (t.sb(f"e_{s}", [P, NP]) for s in ("xT", "ns", "es"))
        w = t.sb("e_w", [P, 4, 3 * H])
        b = t.sb("e_b", [P, 4, 3])
        brz = t.sb("e_brz", [P, 2, 2])
        r, z, pre, cand, diff = ([t.sb(f"e_{s}{g}", [P, CHUNK]) for g in range(2)] for s in ("r", "z", "pre", "cand", "diff"))
        ps = [[t.ps(f"e_p{g}{i}", [P, 512]) for i in range(4)] for g in range(2)]
        x_in, ns_in, es_in, w_in = (t.sem(s) for s in ("x_in", "ns_in", "es_in", "w_in"))
        gates, sig, pre_made, cand_made, cell_done, link, bias_made = (
            t.sem(s) for s in ("gates", "sig", "pre_made", "cand_made", "cell_done", "link", "bias_made"))
        block = ctx.enter_context(nc.Block())
        R, Z, NI, NH = range(4)

        @block.sync
        def _(sp):
            sp.dma_start(w[:, :, :], d["gru_w"]).then_inc(w_in, 16)
            sp.dma_start(b[:, :, :], d["gru_b"]).then_inc(w_in, 16)
            sp.dma_start(xT[:, :], d["xT"]).then_inc(x_in, 16)
            sp.dma_start(ns[:, :], d["ns"]).then_inc(ns_in, 16)
            sp.dma_start(es[:, :], d["es"]).then_inc(es_in, 16)

        @block.tensor
        def _(pe):
            pe.wait_ge(w_in, 32)
            pe.wait_ge(x_in, 16)
            pe.wait_ge(ns_in, 16)
            pe.wait_ge(es_in, 16)
            with pe.Fori(0, NC) as c:
                cols = bass.ds(c * CHUNK, CHUNK)
                for g, src in enumerate((ns, es)):
                    pe.wait_ge(pre_made, 2 * c + g - 1 + 2)
                    pe.wait_ge(sig, 2 * c + g - 1 + 2)
                    for gate in (R, Z):
                        nc.tensor.matmul(ps[g][gate][:, 0:CHUNK], w[:, 2 * g, gate * H:(gate + 1) * H], src[:, cols], start=True, stop=False)
                        nc.tensor.matmul(ps[g][gate][:, 0:CHUNK], w[:, 2 * g + 1, gate * H:(gate + 1) * H], xT[:, cols], start=False, stop=True)
                    nc.tensor.matmul(ps[g][NI][:, 0:CHUNK], w[:, 2 * g, 2 * H:3 * H], src[:, cols], start=True, stop=True)
                    nc.tensor.matmul(ps[g][NH][:, 0:CHUNK], w[:, 2 * g + 1, 2 * H:3 * H], xT[:, cols], start=True, stop=True).then_inc(gates, 1)

        @block.scalar
        def _(act):
            act.sem_inc(sig, 2)
            act.wait_ge(bias_made, 1)
            with act.Fori(0, NC) as c:
                for g in range(2):
                    u = 2 * c + g
                    act.wait_ge(gates, u + 1)
                    act.wait_ge(cell_done, u - 1 + 2)
                    nc.scalar.activation(r[g][:, :], ps[g][R][:, 0:CHUNK], ACT.Sigmoid, bias=brz[:, g, R:R + 1])
                    nc.scalar.activation(z[g][:, :], ps[g][Z][:, 0:CHUNK], ACT.Sigmoid, bias=brz[:, g, Z:Z + 1]).then_inc(sig, 1)
                    act.wait_ge(pre_made, u + 1 + 2)
                    nc.scalar.activation(cand[g][:, :], pre[g][:, :], ACT.Tanh, bias=b[:, 2 * g, 2:3]).then_inc(cand_made, 1)

        @block.vector
        def _(dve):
            dve.sem_inc(pre_made, 2)
            dve.sem_inc(cell_done, 2)
            dve.wait_ge(w_in, 32)
            for g in range(2):
                m = dve.tensor_tensor(brz[:, g, :], b[:, 2 * g, 0:2], b[:, 2 * g + 1, 0:2], ALU.add)
            m.then_inc(bias_made, 1)
            dve.wait_ge(x_in, 16)
            with dve.Fori(0, NC) as c:
                cols = bass.ds(c * CHUNK, CHUNK)
                for g in range(2):
                    u = 2 * c + g
                    steps = 3 + g
                    base = 7 * c + 3 * g
                    dve.wait_ge(sig, u + 1 + 2)
                    dve.scalar_tensor_tensor(pre[g][:, :], ps[g][NH][:, 0:CHUNK], b[:, 2 * g + 1, 2:3], r[g][:, :], ALU.add, ALU.mult).then_inc(link, 1)
                    dve.wait_ge(link, base + 1)
                    dve.tensor_tensor(pre[g][:, :], ps[g][NI][:, 0:CHUNK], pre[g][:, :], ALU.add).then_inc(pre_made, 1)
                    dve.wait_ge(cand_made, u + 1)
                    dve.tensor_tensor(diff[g][:, :], xT[:, cols], cand[g][:, :], ALU.subtract).then_inc(link, 1)
                    dve.wait_ge(link, base + 2)
                    dve.tensor_tensor(diff[g][:, :], diff[g][:, :], z[g][:, :], ALU.mult).then_inc(link, 1)
                    dve.wait_ge(link, base + 3)
                    if g == 0:
                        dve.tensor_tensor(go[:, cols], diff[g][:, :], cand[g][:, :], ALU.add).then_inc(cell_done, 1)
                    else:
                        dve.tensor_tensor(diff[g][:, :], diff[g][:, :], cand[g][:, :], ALU.add).then_inc(link, 1)
                        dve.wait_ge(link, base + 4)
                        dve.wait_ge(cell_done, u + 2)
                        dve.tensor_tensor(go[:, cols], go[:, cols], diff[g][:, :], ALU.add).then_inc(cell_done, 1)


def wide(col):
    return col.unsqueeze(2).broadcast_to([P, T, H])


class Chain:

    def __init__(self, eng, sem):
        self.eng, self.sem, self.n = eng, sem, 0

    def __call__(self, ins):
        self.n += 1
        ins.then_inc(self.sem, 1)
        self.eng.wait_ge(self.sem, self.n)


def norm_dve(dve, then, t, v, out, sq, stat, var_made, root_made, times):
    mean, var, root, tmp = stat
    then(dve.tensor_reduce(mean[:, :], v[:, :, :], AX, ALU.add))
    then(dve.tensor_scalar(mean[:, :], mean[:, :], 1.0 / H, None, ALU.mult))
    then(dve.tensor_tensor(v[:, :, :], v[:, :, :], wide(mean[:, :]), ALU.subtract))
    then(dve.tensor_tensor(sq[:, :, :], v[:, :, :], v[:, :, :], ALU.mult))
    then(dve.tensor_reduce(var[:, :], sq[:, :, :], AX, ALU.add))
    dve.tensor_scalar(var[:, :], var[:, :], 1.0 / H, EPS, ALU.mult, ALU.add).then_inc(var_made, 1)
    dve.wait_ge(root_made, times)
    then(dve.reciprocal(tmp[:, :], root[:, :]))
    then(dve.tensor_tensor(tmp[:, :], tmp[:, :], var[:, :], ALU.mult))
    then(dve.tensor_tensor(tmp[:, :], tmp[:, :], root[:, :], ALU.add))
    then(dve.tensor_scalar(tmp[:, :], tmp[:, :], 0.5, None, ALU.mult))
    then(dve.reciprocal(root[:, :], tmp[:, :]))
    return dve.tensor_tensor(out[:, :, :], v[:, :, :], wide(root[:, :]), ALU.mult)


def first_norm(nc, keep, d):
    go, ident, diag, diag1, dinv, s_hi, s_lo, q = (
        keep[k] for k in ("go", "ident", "diag", "diag1", "dinv", "s_hi", "s_lo", "q"))
    with ExitStack() as ctx:
        t = Tools(nc, ctx)
        x = t.sb("h_x", [P, T, H])
        v = t.sb("h_v", [P, T, H])
        x1 = t.sb("h_x1", [P, T, H])
        x1T = t.sb("h_x1T", [P, T, P])
        w1 = t.sb("h_w1", [P, H])
        b1 = t.sb("h_b1", [P, H])
        own = t.sb("h_own", [P, T])
        stat = [t.sb(f"h_st{i}", [P, T]) for i in range(4)]
        ps = t.ps("h_ps", [P, T, P])
        x_in, w_in, link, turned, var_made, root_made, x1_made, x1_turned, x1T_made, proj, ps_free = (
            t.sem(s) for s in ("x_in", "w_in", "link", "turned", "var_made", "root_made", "x1_made", "x1_turned",
                               "x1T_made", "proj", "ps_free"))
        block = ctx.enter_context(nc.Block())

        @block.sync
        def _(sp):
            sp.dma_start(x[:, :, :], d["x"]).then_inc(x_in, 16)
            sp.dma_start(w1[:, :], d["w1"]).then_inc(w_in, 16)
            sp.dma_start(b1[:, :], d["b1"].partition_broadcast(P)).then_inc(w_in, 16)

        @block.tensor
        def _(pe):
            for k in range(T):
                m = nc.tensor.transpose(ps[:, k, :], go[:, k * P:(k + 1) * P], ident[:, :])
            m.then_inc(turned, 1)
            pe.wait_ge(x1_made, 1)
            for k in range(T):
                m = nc.tensor.transpose(ps[:, k, :], x1[:, k, :], ident[:, :])
            m.then_inc(x1_turned, 1)
            pe.wait_ge(x1T_made, 1)
            pe.wait_ge(w_in, 32)
            for k in range(T):
                m = nc.tensor.matmul(ps[:, k, :], x1T[:, k, :], w1[:, :], start=True, stop=True)
            m.then_inc(proj, 1)

        @block.scalar
        def _(act):
            act.wait_ge(var_made, 1)
            nc.scalar.activation(stat[2][:, :], stat[1][:, :], ACT.Sqrt).then_inc(root_made, 1)
            act.wait_ge(x1_turned, 1)
            nc.scalar.activation(x1T[:, :, :], ps[:, :, :], ACT.Copy).then_inc(x1T_made, 1)

        @block.vector
        def _(dve):
            then = Chain(dve, link)
            dve.wait_ge(turned, 1)
            then(dve.tensor_tensor(v[:, :, :], ps[:, :, :], wide(diag[:, :]), ALU.mult))
            dve.wait_ge(x_in, 16)
            then(dve.tensor_tensor(v[:, :, :], v[:, :, :], x[:, :, :], ALU.add))
            norm_dve(dve, then, t, v, x1, x, stat, var_made, root_made, 1).then_inc(x1_made, 1)
            then(dve.tensor_tensor(own[:, :], dinv[:, :], diag1[:, :], ALU.mult))
            dve.wait_ge(proj, 1)
            then(dve.tensor_tensor(v[:, :, :], ps[:, :, :], b1[:, :].unsqueeze(1).broadcast_to([P, T, H]), ALU.add))
            then(dve.tensor_tensor(v[:, :, :], v[:, :, :], wide(dinv[:, :]), ALU.mult))
            then(dve.tensor_copy(s_hi[:, :, :], v[:, :, :]))
            dve.tensor_tensor(s_lo[:, :, :], v[:, :, :], s_hi[:, :, :].bitcast(F32), ALU.subtract)
            then(dve.tensor_tensor(x[:, :, :], v[:, :, :], wide(own[:, :]), ALU.mult))
            dve.tensor_tensor(q[:, :, :], x[:, :, :], x1[:, :, :], ALU.add)


def spread_layer(nc, keep, d):
    ident, not_i, dinv, s_hi, s_lo, q = (keep[k] for k in ("ident", "not_i", "dinv", "s_hi", "s_lo", "q"))
    RA, RB = 4, 2
    BANKS = [(b, min(512, NP - b)) for b in range(0, NP, 512)]
    with ExitStack() as ctx:
        t = Tools(nc, ctx)
        at = [t.sb(f"f_at{i}", [P, NP]) for i in range(RA)]
        hi = [t.sb(f"f_hi{i}", [P, NP], F32R) for i in range(RB)]
        lo = [t.sb(f"f_lo{i}", [P, NP], F32R) for i in range(RB)]
        stat = [t.sb(f"f_st{i}", [P, T]) for i in range(4)]
        acc = t.ps("f_acc", [P, T, P])
        sums = acc[:, :, :].rearrange("p t f -> p (t f)")
        at_in = [t.sem(f"at_in{i}") for i in range(RA)]
        diag_zero, hi_done, lo_done, pe_done, sums_out, turned, link, var_made, root_made, y_made, y_saved = (
            t.sem(s) for s in ("diag_zero", "hi_done", "lo_done", "pe_done", "sums_out", "turned", "link",
                               "var_made", "root_made", "y_made", "y_saved"))
        block = ctx.enter_context(nc.Block())
        v = at[0][:, :].rearrange("p (t f) -> p t f", f=H)
        sq = at[1][:, :].rearrange("p (t f) -> p t f", f=H)
        y = at[2][:, :].rearrange("p (t f) -> p t f", f=H)
        accT = at[3]

        @block.sync
        def _(sp):
            for j in range(T):
                if j >= RA:
                    sp.wait_ge(hi_done, j - RA + 1)
                    sp.wait_ge(lo_done, j - RA + 1)
                sp.dma_start(at[j % RA][:, :], d["adjT"][j * P:(j + 1) * P, :]).then_inc(at_in[j % RA], 16)
            sp.wait_ge(y_made, 1)
            sp.dma_start(d["out"], y).then_inc(y_saved, 16)
            sp.wait_ge(y_saved, 16)

        @block.scalar
        def _(act):
            for j in range(T):
                act.wait_ge(diag_zero, j + 1)
                if j >= RB:
                    act.wait_ge(pe_done, j - RB + 1)
                    act.wait_ge(lo_done, j - RB + 1)
                nc.scalar.activation(hi[j % RB][:, :], at[j % RA][:, :], ACT.Copy).then_inc(hi_done, 1)
            act.wait_ge(pe_done, T)
            act.wait_ge(lo_done, T)
            nc.scalar.activation(accT[:, :], sums[:, :], ACT.Copy).then_inc(sums_out, 1)
            act.wait_ge(var_made, 1)
            nc.scalar.activation(stat[2][:, :], stat[1][:, :], ACT.Sqrt).then_inc(root_made, 1)

        @block.vector
        def _(dve):
            for j in range(T):
                dve.wait_ge(at_in[j % RA], 16 * (j // RA + 1))
                c = slice(j * P, (j + 1) * P)
                dve.tensor_tensor(at[j % RA][:, c], at[j % RA][:, c], not_i[:, :], ALU.mult).then_inc(diag_zero, 1)
                dve.wait_ge(hi_done, j + 1)
                if j >= RB:
                    dve.wait_ge(pe_done, j - RB + 1)
                dve.tensor_tensor(lo[j % RB][:, :], at[j % RA][:, :], hi[j % RB][:, :].bitcast(F32), ALU.subtract)\
                   .then_inc(lo_done, 1)
            then = Chain(dve, link)
            dve.wait_ge(turned, 1)
            then(dve.tensor_tensor(v, acc[:, :, :], wide(dinv[:, :]), ALU.mult))
            then(dve.tensor_tensor(v, v, q[:, :, :], ALU.add))
            norm_dve(dve, then, t, v, y, sq, stat, var_made, root_made, 1).then_inc(y_made, 1)

        @block.tensor
        def _(pe):
            for j in range(T):
                for w, m, ready in ((s_hi, hi, hi_done), (s_lo, hi, None), (s_hi, lo, lo_done)):
                    if ready is not None:
                        pe.wait_ge(ready, j + 1)
                    for b, n in BANKS:
                        mm = nc.tensor.matmul(sums[:, b:b + n], w[:, j, :], m[j % RB][:, b:b + n],
                                              start=(j == 0 and w is s_hi and m is hi), stop=(j == T - 1 and m is lo))
                mm.then_inc(pe_done, 1)
            pe.wait_ge(sums_out, 1)
            for k in range(T):
                m = nc.tensor.transpose(acc[:, k, :], accT[:, k * P:(k + 1) * P], ident[:, :])
            m.then_inc(turned, 1)


def build(nc, adj, adjT, x, xT, diag, gat_w, gat_a, gru_w, gru_b, w1, b1, out):
    scratch = {k: nc.dram_tensor(k, s, F32).ap() for k, s in (("e_rows", (2, HEADS * NP)), ("ns_d", (P, NP)), ("es_d", (P, NP)))}
    d = {"adj": adj, "adjT": adjT, "x": x, "xT": xT, "diag": diag, "gat_w": gat_w, "gat_a": gat_a,
         "gru_w": gru_w, "gru_b": gru_b, "w1": w1, "b1": b1,
         "e_rows": scratch["e_rows"], "ns": scratch["ns_d"], "es": scratch["es_d"],
         "out": out.rearrange("(t p) f -> p t f", p=P)}
    with ExitStack() as ctx:
        t = Tools(nc, ctx)
        keep = {"ident": t.sb("ident", [P, P]), "not_i": t.sb("not_i", [P, P]),
                "ecol": t.sb("ecol", [P, E2 * T]), "flag": t.sb("flag", [P, 1], I32),
                "dinv": t.sb("dinv", [P, T]), "diag": t.sb("diag", [P, T]), "diag1": t.sb("diag1", [P, T])}
        with ExitStack() as ctx1:
            t1 = Tools(nc, ctx1)
            keep["hw"] = t1.sb("hw", [P, T, HEADS * H])
            with ExitStack() as ctx2:
                t2 = Tools(nc, ctx2)
                keep |= {"x_hi": t2.sb("x_hi", [P, T, H], F32R), "x_lo": t2.sb("x_lo", [P, T, H], F32R),
                         "up": t2.sb("up", [P, T, EW], BF16), "um": t2.sb("um", [P, T, EW], BF16),
                         "ns": t2.sb("ns", [P, NP]), "csum": t2.sb("csum", [P, NP]), "elog": t2.sb("elog", [EW, NP])}
                project(nc, keep, d)
                aggregate(nc, keep, d)
                logits(nc, keep, d)
            attend(nc, keep, d)
            attend_signed(nc, keep, d)
        keep |= {"go": t.sb("go", [P, NP])}
        gru(nc, keep, d)
        keep |= {"s_hi": t.sb("s_hi", [P, T, H], F32R), "s_lo": t.sb("s_lo", [P, T, H], F32R), "q": t.sb("q", [P, T, H])}
        first_norm(nc, keep, d)
        spread_layer(nc, keep, d)


def kernel(x, adj, L0_gnn_gat_W, L0_gnn_gat_a, L0_gnn_edge_Wih, L0_gnn_edge_Whh, L0_gnn_edge_bih, L0_gnn_edge_bhh,
           L0_gnn_node_Wih, L0_gnn_node_Whh, L0_gnn_node_bih, L0_gnn_node_bhh, L1_gnn_W, L1_gnn_b):
    import numpy as np
    import concourse.bacc as bacc
    from concourse.bass_utils import run_bass_kernel_spmd

    def f(a):
        return np.ascontiguousarray(a)

    adj = np.asarray(adj)
    padded = np.zeros((NP, NP), adj.dtype)
    padded[:N, :N] = adj
    padded_t = np.zeros((NP, NP), adj.dtype)
    padded_t[:N, :N] = adj.T
    diag = np.zeros((NP,), adj.dtype)
    diag[:N] = np.diagonal(adj)
    xp = np.zeros((NP, H), np.asarray(x).dtype)
    xp[:N] = np.asarray(x)
    weights = (L0_gnn_edge_Wih, L0_gnn_edge_Whh, L0_gnn_node_Wih, L0_gnn_node_Whh)
    biases = (L0_gnn_edge_bih, L0_gnn_edge_bhh, L0_gnn_node_bih, L0_gnn_node_bhh)
    arrays = {
        "adj": padded, "adjT": padded_t,
        "x": f(xp.reshape(T, P, H).transpose(1, 0, 2)), "xT": f(xp.T), "diag": f(diag.reshape(T, P).T),
        "gat_w": f(np.asarray(L0_gnn_gat_W).transpose(1, 0, 2).reshape(H, HEADS * H)),
        "gat_a": f(np.asarray(L0_gnn_gat_a).reshape(HEADS * 2 * H)),
        "gru_w": f(np.stack([np.asarray(w).T for w in weights], axis=1)),
        "gru_b": f(np.stack([np.asarray(b).reshape(3, H).T for b in biases], axis=1)),
        "w1": f(np.asarray(L1_gnn_W).T), "b1": f(np.asarray(L1_gnn_b)),
    }
    nc = bacc.Bacc("TRN2", target_bir_lowering=False, num_devices=1)
    args = [nc.dram_tensor(f"in_{k}", a.shape, mybir.dt.from_np(a.dtype), kind="ExternalInput").ap()
            for k, a in arrays.items()]
    out = nc.dram_tensor("y", (NP, H), F32, kind="ExternalOutput").ap()
    build(nc, *args, out)
    r = run_bass_kernel_spmd(nc, [{f"in_{k}": a for k, a in arrays.items()}], core_ids=[0])
    return r.results[0]["y"][:N]
```

```python
import concourse.bass as bass
from concourse import mybir
from concourse.alu_op_type import AluOpType as ALU
from contextlib import ExitStack


N = 3327
P = 128
T = (N + P - 1) // P
NP = T * P
H = 128
HEADS = 3
E2 = 2 * HEADS
EW = 32
COUNT = 3 * E2
ALPHA = 0.2
EPS = 1e-5
FLOOR = 104.0

F32 = mybir.dt.float32
F32R = mybir.dt.float32r
BF16 = mybir.dt.bfloat16
U8 = mybir.dt.uint8
I32 = mybir.dt.int32
ACT = mybir.ActivationFunctionType
AX = mybir.AxisListType.X

HALF = NP // 2
BANK = HALF // 4
CT = 6
CW = CT * P
CHUNKS = T // CT
RT = T - CHUNKS * CT


def slot_before(j, ring, steps):
    if j >= ring:
        return j - ring
    return max(k for k in range(steps) if k % ring == j % ring) - steps


def loads_before(j, ring):
    return j // ring


def loads_per_round(j, ring, steps):
    return len(range(j % ring, steps, ring))


class Tools:

    def __init__(self, nc, ctx):
        self.nc, self.ctx, self.n = nc, ctx, 0

    def sb(self, name, shape, dt=F32):
        return self.ctx.enter_context(self.nc.sbuf_tensor(name, shape, dt))

    def ps(self, name, shape, dt=F32):
        return self.ctx.enter_context(self.nc.psum_tensor(name, shape, dt))

    def sem(self, name):
        return self.ctx.enter_context(self.nc.semaphore(name))


def project(nc, keep, d):
    hw, upm, umm, x_hi, x_lo, ident, not_i = (keep[k] for k in ("hw", "up", "um", "x_hi", "x_lo", "ident", "not_i"))
    with ExitStack() as ctx:
        t = Tools(nc, ctx)
        xT = t.sb("a_xT", [P, NP])
        x_sb = t.sb("a_x", [P, T, H])
        wext = t.sb("a_wext", [P, HEADS * H + E2])
        a_row = t.sb("a_arow", [P, E2, H])
        junk = t.sb("a_junk", [P, H])
        u = t.sb("a_u", [P, T, E2])
        part = t.sb("a_part", [P, T, E2], BF16)
        rest = t.sb("a_rest", [P, T, E2])
        pp = [t.ps(f"a_pp{i}", [P, 512]) for i in range(4)]
        x_in, xT_in, w_in, a_in = t.sem("x_in"), t.sem("xT_in"), t.sem("w_in"), t.sem("a_in")
        zeroed, folded, mm, hw_out, u_out, link, made = (
            t.sem(s) for s in ("zeroed", "folded", "mm", "hw_out", "u_out", "link", "made"))
        block = ctx.enter_context(nc.Block())

        @block.sync
        def _(sp):
            sp.dma_start(wext[:, 0:HEADS * H], d["gat_w"]).then_inc(w_in, 16)
            sp.dma_start(xT[:, :], d["xT"]).then_inc(xT_in, 16)
            sp.dma_start(a_row[:, :, :].rearrange("p c f -> p (c f)"), d["gat_a"].partition_broadcast(P)).then_inc(a_in, 16)
            sp.dma_start(x_sb[:, :, :], d["x"]).then_inc(x_in, 16)

        @block.gpsimd
        def _(pool):
            pool.memset(ident[:, :], 0.0).then_inc(made, 1)
            pool.memset(not_i[:, :], 1.0).then_inc(made, 1)
            pool.wait_ge(made, 2)
            pool.affine_select(out=ident[:, :], in_=ident[:, :], compare_op=ALU.not_equal, fill=1.0,
                               base=0, pattern=[[-1, P]], channel_multiplier=1)
            pool.affine_select(out=not_i[:, :], in_=not_i[:, :], compare_op=ALU.not_equal, fill=0.0,
                               base=0, pattern=[[-1, P]], channel_multiplier=1)

        @block.tensor
        def _(pe):
            pe.wait_ge(w_in, 16)
            pe.wait_ge(folded, E2)
            pe.wait_ge(xT_in, 16)
            for k in range(T):
                if k >= 4:
                    pe.wait_ge(hw_out, k - 3)
                    pe.wait_ge(u_out, k - 3)
                nc.tensor.matmul(pp[k % 4][:, 0:HEADS * H + E2], xT[:, k * P:(k + 1) * P], wext[:, :],
                                 start=True, stop=True).then_inc(mm, 1)

        @block.scalar
        def _(act):
            for k in range(T):
                act.wait_ge(mm, k + 1)
                if k >= 1:
                    act.wait_ge(u_out, k + 1)
                else:
                    act.wait_ge(u_out, 1)
                nc.scalar.activation(hw[:, k, :], pp[k % 4][:, 0:HEADS * H], ACT.Copy).then_inc(hw_out, 1)

        @block.vector
        def _(dve):
            dve.memset(upm[:, :, :], 0.0).then_inc(zeroed, 1)
            dve.memset(umm[:, :, :], 0.0).then_inc(zeroed, 1)
            dve.wait_ge(w_in, 16)
            dve.wait_ge(a_in, 16)
            for c in range(E2):
                h, side = c % HEADS, c // HEADS
                if c:
                    dve.wait_ge(folded, c)
                dve.tensor_tensor_reduce(out=junk[:, :], in0=wext[:, h * H:(h + 1) * H], in1=a_row[:, 2 * h + side, :],
                                         scale=1.0, scalar=0.0, op0=ALU.mult, op1=ALU.add,
                                         accum_out=wext[:, HEADS * H + c:HEADS * H + c + 1]).then_inc(folded, 1)
            dve.wait_ge(x_in, 16)
            dve.tensor_copy(x_hi[:, :, :], x_sb[:, :, :]).then_inc(link, 1)
            dve.wait_ge(link, 1)
            dve.tensor_tensor(x_lo[:, :, :], x_sb[:, :, :], x_hi[:, :, :].bitcast(F32), ALU.subtract)
            for k in range(T):
                dve.wait_ge(mm, k + 1)
                dve.tensor_copy(u[:, k, :], pp[k % 4][:, HEADS * H:HEADS * H + E2]).then_inc(u_out, 1)
            dve.wait_ge(u_out, T)
            dve.wait_ge(zeroed, 2)
            n = 1

            def then(ins):
                nonlocal n
                n += 1
                ins.then_inc(link, 1)
                dve.wait_ge(link, n)

            def split(dst):
                then(dve.tensor_copy(part[:, :, :], u[:, :, :]))
                then(dve.tensor_copy(dst[:, :, 0:E2], part[:, :, :]))
                then(dve.tensor_tensor(rest[:, :, :], u[:, :, :], part[:, :, :], ALU.subtract))
                then(dve.tensor_copy(part[:, :, :], rest[:, :, :]))
                then(dve.tensor_copy(dst[:, :, E2:2 * E2], part[:, :, :]))
                then(dve.tensor_tensor(rest[:, :, :], rest[:, :, :], part[:, :, :], ALU.subtract))
                then(dve.tensor_copy(dst[:, :, 2 * E2:3 * E2], rest[:, :, :]))

            split(upm)
            then(dve.tensor_tensor(u[:, :, 0:HEADS], u[:, :, 0:HEADS], u[:, :, HEADS:E2], ALU.add))
            then(dve.tensor_copy(u[:, :, HEADS:E2], u[:, :, 0:HEADS]))
            split(umm)
            then(dve.memset(umm[:, :, COUNT:COUNT + 1], 1.0))


def aggregate(nc, keep, d):
    upm, umm, x_hi, x_lo, not_i, csum, ns, elog = (
        keep[k] for k in ("up", "um", "x_hi", "x_lo", "not_i", "csum", "ns", "elog"))
    RA, RB = 4, 2
    with ExitStack() as ctx:
        t = Tools(nc, ctx)
        at = [t.sb(f"b_at{i}", [P, HALF]) for i in range(RA)]
        hi = [t.sb(f"b_hi{i}", [P, HALF], F32R) for i in range(RB)]
        lo = [t.sb(f"b_lo{i}", [P, HALF], F32R) for i in range(RB)]
        sg = [t.sb(f"b_sg{i}", [P, HALF], BF16) for i in range(RB)]
        mi = [t.sb(f"b_mi{i}", [P, HALF], BF16) for i in range(RB)]
        acc_ns = [t.ps(f"b_ns{i}", [P, 512]) for i in range(4)]
        acc_e = [t.ps(f"b_e{i}", [P, 512]) for i in range(4)]
        at_in = [t.sem(f"at_in{i}") for i in range(RA)]
        diag_zero, act_done, lo_done, mask_done, sum_done, pe_done, acc_ready, ns_out, e_out, saved = (
            t.sem(s) for s in ("diag_zero", "act_done", "lo_done", "mask_done", "sum_done", "pe_done",
                               "acc_ready", "ns_out", "e_out", "saved"))
        hi_done = t.sem("hi_done")
        block = ctx.enter_context(nc.Block())

        @block.sync
        def _(sp):
            for half in range(2):
                for j in range(T):
                    before = T * half + slot_before(j, RA, T) + 1 + RA
                    sp.wait_ge(act_done, before)
                    sp.wait_ge(lo_done, before)
                    sp.wait_ge(sum_done, before)
                    sp.dma_start(at[j % RA][:, :], d["adjT"][j * P:(j + 1) * P, half * HALF:(half + 1) * HALF])\
                      .then_inc(at_in[j % RA], 16)

        @block.gpsimd
        def _(pool):
            pool.sem_inc(sum_done, RA)
            for half in range(2):
                for j in range(T):
                    pool.wait_ge(diag_zero, T * half + j + 1)
                    cs = csum[:, half * HALF:(half + 1) * HALF]
                    if j == 0:
                        pool.tensor_copy(cs, at[0][:, :]).then_inc(sum_done, 1)
                    else:
                        pool.wait_ge(sum_done, T * half + j + RA)
                        pool.tensor_tensor(cs, cs, at[j % RA][:, :], ALU.add).then_inc(sum_done, 1)

        @block.scalar
        def _(act):
            act.sem_inc(act_done, RA)
            act.sem_inc(ns_out, 1)
            with act.Fori(0, 2) as half:
                for j in range(T):
                    act.wait_ge(diag_zero, T * half + j + 1)
                    act.wait_ge(pe_done, T * half + slot_before(j, RB, T) + 1 + RB)
                    act.wait_ge(lo_done, T * half + slot_before(j, RB, T) + 1 + RA)
                    nc.scalar.activation(hi[j % RB][:, :], at[j % RA][:, :], ACT.Copy).then_inc(hi_done, 1)
                    nc.scalar.activation(sg[j % RB][:, :], at[j % RA][:, :], ACT.Sign).then_inc(act_done, 1)
                act.wait_ge(acc_ready, half + 1)
                for q in range(4):
                    nc.scalar.activation(ns[:, bass.ds(half * HALF + q * BANK, BANK)], acc_ns[q][:, 0:BANK],
                                         ACT.Copy).then_inc(ns_out, 1)

        @block.vector
        def _(dve):
            dve.sem_inc(lo_done, RA)
            dve.sem_inc(e_out, 1)
            for half in range(2):
                for j in range(T):
                    k = T * half + j
                    dve.wait_ge(at_in[j % RA], 16 * (half * loads_per_round(j, RA, T) + loads_before(j, RA) + 1))
                    c = j * P - half * HALF
                    if 0 <= c < HALF:
                        dve.tensor_tensor(at[j % RA][:, c:c + P], at[j % RA][:, c:c + P], not_i[:, :], ALU.mult)\
                           .then_inc(diag_zero, 1)
                        dve.wait_ge(diag_zero, k + 1)
                    else:
                        dve.sem_inc(diag_zero, 1)
                    dve.wait_ge(pe_done, k + 1)
                    dve.tensor_scalar(mi[j % RB][:, :], at[j % RA][:, :], 0.0, None, ALU.is_lt).then_inc(mask_done, 1)
                    dve.wait_ge(hi_done, k + 1)
                    dve.tensor_tensor(lo[j % RB][:, :], at[j % RA][:, :], hi[j % RB][:, :].bitcast(F32), ALU.subtract)\
                       .then_inc(lo_done, 1)
                dve.wait_ge(acc_ready, half + 1)
                for q in range(4):
                    at0 = half * HALF + q * BANK
                    dve.tensor_copy(elog[:, at0:at0 + BANK], acc_e[q][0:EW, 0:BANK]).then_inc(e_out, 1)

        @block.tensor
        def _(pe):
            pe.sem_inc(pe_done, RB)
            with pe.Fori(0, 2) as half:
                for j in range(T):
                    k = T * half + j
                    first, last = j == 0, j == T - 1
                    if first:
                        pe.wait_ge(ns_out, 4 * half + 1)
                        pe.wait_ge(e_out, 4 * half + 1)
                    pe.wait_ge(act_done, k + 1 + RA)
                    for w, m in ((x_hi, hi), (x_lo, hi)):
                        for q in range(4):
                            nc.tensor.matmul(acc_ns[q][:, 0:BANK], w[:, j, :], m[j % RB][:, q * BANK:(q + 1) * BANK],
                                             start=first and w is x_hi, stop=False)
                    for q in range(4):
                        nc.tensor.matmul(acc_e[q][0:EW, 0:BANK], upm[:, j, :], sg[j % RB][:, q * BANK:(q + 1) * BANK],
                                         start=first, stop=False)
                    pe.wait_ge(lo_done, k + 1 + RA)
                    pe.wait_ge(mask_done, k + 1)
                    for q in range(4):
                        nc.tensor.matmul(acc_ns[q][:, 0:BANK], x_hi[:, j, :], lo[j % RB][:, q * BANK:(q + 1) * BANK],
                                         start=False, stop=last)
                    for q in range(4):
                        mm = nc.tensor.matmul(acc_e[q][0:EW, 0:BANK], umm[:, j, :], mi[j % RB][:, q * BANK:(q + 1) * BANK],
                                              start=False, stop=last)
                    mm.then_inc(pe_done, 1)
                pe.wait_ge(pe_done, T * half + T + RB)
                pe.sem_inc(acc_ready, 1)


def logits(nc, keep, d):
    csum, elog, ecol, flag, dinv, diag, diag1, ident = (
        keep[k] for k in ("csum", "elog", "ecol", "flag", "dinv", "diag", "diag1", "ident"))
    CW7 = E2 + 1
    with ExitStack() as ctx:
        t = Tools(nc, ctx)
        sel = t.sb("c_sel", [EW, CW7])
        ones = t.sb("c_ones", [P, 1])
        raw = t.sb("c_raw", [P, T, CW7])
        e = t.sb("c_e", [P, T, E2])
        red = t.sb("c_red", [P, CW7])
        redg = t.sb("c_redg", [P, CW7])
        shift = t.sb("c_shift", [P, E2])
        erow = t.sb("c_erow", [HEADS * T, 2, P])
        deg = t.sb("c_deg", [P, T])
        root = t.sb("c_root", [P, T])
        safe = t.sb("c_safe", [P, T])
        quot = t.sb("c_quot", [P, T])
        some = t.sb("c_some", [P, T])
        p_e = t.ps("c_pe", [P, T, CW7])
        p_d = t.ps("c_pd", [P, T])
        p_t = t.ps("c_pt", [HEADS * T, 2, P])
        mm, made, link, reduced, everywhere, shifted, turned, copied, saved, deg_made, rooted, diag_in = (
            t.sem(s) for s in ("mm", "made", "link", "reduced", "everywhere", "shifted", "turned", "copied",
                               "e_saved", "deg_made", "rooted", "diag_in"))
        block = ctx.enter_context(nc.Block())

        @block.sync
        def _(sp):
            sp.dma_start(diag[:, :], d["diag"]).then_inc(diag_in, 16)
            sp.wait_ge(copied, 1)
            sp.dma_start(d["e_rows"].rearrange("s (c p) -> c s p", p=P), erow[:, :, :]).then_inc(saved, 16)
            sp.dma_start(d["ns"], keep["ns"][:, :]).then_inc(saved, 16)
            sp.wait_ge(saved, 32)

        @block.tensor
        def _(pe):
            pe.wait_ge(made, 2)
            for k in range(T):
                nc.tensor.matmul(p_e[:, k, :], elog[0:EW, k * P:(k + 1) * P], sel[:, :], start=True, stop=True)
            for k in range(T):
                m = nc.tensor.matmul(p_d[:, k:k + 1], csum[:, k * P:(k + 1) * P], ones[:, :], start=True, stop=True)
            m.then_inc(mm, 1)
            pe.wait_ge(shifted, 1)
            for s in range(2):
                m = nc.tensor.transpose(p_t[:, s, :], ecol[:, s * HEADS * T:(s + 1) * HEADS * T], ident[:, :])
            m.then_inc(turned, 1)

        @block.scalar
        def _(act):
            act.wait_ge(deg_made, 1)
            nc.scalar.activation(root[:, :], deg[:, :], ACT.Sqrt).then_inc(rooted, 1)

        @block.gpsimd
        def _(pool):
            pool.wait_ge(reduced, 1)
            pool.partition_all_reduce(redg[:, :], red[:, :], P, bass.bass_isa.ReduceOp.max).then_inc(everywhere, 1)

        @block.vector
        def _(dve):
            n = 0

            def then(ins):
                nonlocal n
                n += 1
                ins.then_inc(link, 1)
                dve.wait_ge(link, n)

            dve.memset(ones[:, :], 1.0).then_inc(made, 1)
            then(dve.tensor_tensor(sel[:, 0:E2], ident[0:EW, 0:E2], ident[0:EW, E2:2 * E2], ALU.add))
            then(dve.tensor_tensor(sel[:, 0:E2], sel[:, 0:E2], ident[0:EW, 2 * E2:3 * E2], ALU.add))
            dve.tensor_copy(sel[:, E2:CW7], ident[0:EW, COUNT:COUNT + 1]).then_inc(made, 1)
            dve.wait_ge(mm, 1)
            then(dve.tensor_copy(raw[:, :, :], p_e[:, :, :]))
            dve.wait_ge(diag_in, 16)
            then(dve.tensor_scalar(diag1[:, :], diag[:, :], 1.0, None, ALU.add))
            then(dve.tensor_tensor(deg[:, :], p_d[:, :], diag1[:, :], ALU.add))
            dve.sem_inc(deg_made, 1)
            then(dve.scalar_tensor_tensor(e[:, :, :], raw[:, :, 0:E2], ALPHA, raw[:, :, 0:E2], ALU.mult, ALU.max))
            then(dve.tensor_reduce(red[:, 0:E2], e[:, :, :].rearrange("p t c -> p c t"), AX, ALU.min))
            then(dve.tensor_scalar(red[:, 0:E2], red[:, 0:E2], -1.0, None, ALU.mult))
            dve.tensor_reduce(red[:, E2:CW7], raw[:, :, E2:CW7].rearrange("p t c -> p c t"), AX, ALU.add)\
               .then_inc(reduced, 1)
            dve.wait_ge(rooted, 1)
            then(dve.tensor_scalar(safe[:, :], root[:, :], 1e-30, None, ALU.max))
            then(dve.reciprocal(quot[:, :], safe[:, :]))
            then(dve.tensor_tensor(quot[:, :], quot[:, :], deg[:, :], ALU.mult))
            then(dve.tensor_tensor(safe[:, :], safe[:, :], quot[:, :], ALU.add))
            then(dve.tensor_scalar(safe[:, :], safe[:, :], 0.5, None, ALU.mult))
            then(dve.reciprocal(quot[:, :], safe[:, :]))
            then(dve.tensor_scalar(some[:, :], deg[:, :], 0.0, None, ALU.not_equal))
            then(dve.tensor_tensor(quot[:, :], quot[:, :], some[:, :], ALU.mult))
            then(dve.tensor_scalar(root[:, :], root[:, :], 0.0, None, ALU.mult))
            then(dve.tensor_tensor(dinv[:, :], quot[:, :], root[:, :], ALU.add))
            dve.wait_ge(everywhere, 1)
            then(dve.tensor_tensor(shift[:, 0:HEADS], redg[:, 0:HEADS], redg[:, HEADS:E2], ALU.max))
            then(dve.tensor_scalar(shift[:, 0:HEADS], shift[:, 0:HEADS], FLOOR, None, ALU.add))
            then(dve.tensor_copy(shift[:, HEADS:E2], shift[:, 0:HEADS]))
            dve.tensor_tensor(ecol[:, :].rearrange("p (c t) -> p c t", t=T), e[:, :, :].rearrange("p t c -> p c t"),
                              shift[:, :].unsqueeze(2).broadcast_to([P, E2, T]), ALU.add).then_inc(shifted, 1)
            then(dve.tensor_copy(flag[:, :], redg[:, E2:CW7]))
            dve.wait_ge(turned, 1)
            dve.tensor_copy(erow[:, :, :], p_t[:, :, :]).then_inc(copied, 1)


def attend(nc, keep, d):
    hw, ecol, ident, not_i = (keep[k] for k in ("hw", "ecol", "ident", "not_i"))
    RA, RE, RW = 4, 6, 6
    CREDIT = 16
    HW = CW // 2
    NU = HEADS * T
    ROWS = HEADS * CT
    LAST = CHUNKS
    UNITS = [(j, h) for j in range(T) for h in range(HEADS)]
    DVE_BUSY = [(j, HEADS - 1) for j in (6, 10, 13, 17, 19, 20)]
    DVE_FREE = [(j, HEADS - 1) for j in range(T - 2)]
    AHEAD, ROW_END = 4, 18
    TAIL = {T - 5 + r: r for r in range(AHEAD)}
    BODY = {(r - AHEAD) * ROW_END // (ROWS - 1 - AHEAD): r for r in range(AHEAD, ROWS)}
    BODY0 = {r: r for r in range(ROWS)}
    INV_SEND, MAX_SEND, TAKE_LAG = (0, 1, 2, 3, 4, 5), (10, 11, 12, 19, 20, 21), 3
    with ExitStack() as ctx:
        t = Tools(nc, ctx)
        erow = t.sb("d_erow", [P, HEADS, NP])
        arow = [t.sb(f"d_arow{i}", [P, HALF]) for i in range(2)]
        ones_not_i = t.sb("d_ones_not_i", [P, 2 * CHUNKS - 1, P], BF16)
        mask = t.sb("d_mask", [P, NP], U8)
        L = [t.sb(f"d_l{i}", [P, NP]) for i in range(2)]
        mx = t.sb("d_mx", [P, ROWS])
        scratch = t.sb("d_scratch", [P, 1])
        nm = t.sb("d_nm", [P, ROWS])
        den = t.sb("d_den", [P, ROWS])
        rden = t.sb("d_rden", [P, ROWS])
        nmb = t.sb("d_nmb", [P, 2, HEADS, CW])
        invb = t.sb("d_invb", [P, HEADS, CW])
        at = [t.sb(f"d_at{i}", [P, CW]) for i in range(RA)]
        ex = [t.sb(f"d_ex{i}", [P, CW]) for i in range(RE)]
        W = [t.sb(f"d_w{i}", [P, CW]) for i in range(RW)]
        es = t.sb("d_es", [P, CW])
        es2 = t.sb("d_es2", [P, CW])
        acc = [t.ps(f"d_acc{h}", [P, 2, 512]) for h in range(HEADS)]
        aux = [t.ps(f"d_aux{i}", [P, 512]) for i in range(2)]
        at_in = [t.sem(f"at_in{i}") for i in range(RA)]
        arow_in = [t.sem(f"arow_in{i}") for i in range(2)]
        (erow_in, arow_read, mask_whole, logit_made, nm_made, row_exp, sums_inverted, spread, spread_out) = (
            t.sem(s) for s in ("erow_in", "arow_read", "mask_whole", "logit_made", "nm_made", "row_exp",
                               "sums_inverted", "spread", "spread_out"))
        (diag_zero, table_made, first_seen, arg_made, exp_made, w_dve, w_pool, unit_done, acc_free, es_added,
         es_made, es_saved) = (
            t.sem(s) for s in ("diag_zero", "table_made", "first_seen", "arg_made", "exp_made", "w_dve", "w_pool",
                               "unit_done", "acc_free", "es_added", "es_made", "es_saved"))
        block = ctx.enter_context(nc.Block())

        def is_last(q):
            return isinstance(q, int) and q == LAST

        def tiles(q):
            return RT if is_last(q) else CT

        def width(q):
            return tiles(q) * P

        def on_dve(q):
            return DVE_FREE if isinstance(q, int) and q >= LAST - 1 else DVE_BUSY

        def on_pool(q):
            return [u for u in UNITS if u not in on_dve(q)]

        def made_before(q, on):
            return len(on(0)) * (LAST - 1) + len(on(LAST - 1)) if is_last(q) else len(on(0)) * q

        def wait_weights(eng, q, j, h):
            if j < 0:
                eng.wait_ge(w_pool, made_before(q, on_pool) - (HEADS * (-j) - h) + 1 + CREDIT)
            elif (j, h) in on_dve(q):
                eng.wait_ge(w_dve, made_before(q, on_dve) + on_dve(q).index((j, h)) + 1 + CREDIT)
            else:
                eng.wait_ge(w_pool, made_before(q, on_pool) + on_pool(q).index((j, h)) + 1 + CREDIT)

        def rows_at(q, j):
            rows = []
            body = BODY0 if isinstance(q, int) and q == 0 else BODY
            if j in body and not is_last(q):
                c = q + 1
                if body[j] < HEADS * tiles(c):
                    rows.append((c, body[j]))
            if j in TAIL and not (isinstance(q, int) and q >= LAST - 1):
                rows.append((q + 2, TAIL[j]))
            return rows

        PIECES = [(h, a, CT // 2) for a in range(0, CT, CT // 2) for h in range(HEADS)]
        PIECES_LAST = [(h, 0, RT) for h in range(HEADS)]

        def pieces(q):
            return PIECES_LAST if is_last(q) else PIECES

        def turn(q, i, src):
            n = len(PIECES)
            if src is nm:
                return 2 * n * q + i
            return 2 * n * q + i + len(pieces(q))

        def bank(q, i, src):
            return turn(LAST if is_last(q) else 0, i, src) % 2

        def each_chunk(eng, step):
            step(0)
            with eng.Fori(1, LAST - 1) as q:
                step(q)
            step(LAST - 1)
            step(LAST)

        @block.sync
        def _(sp):
            def row_tile(c, k):
                r0 = (c * CT + k) * P
                if not isinstance(r0, int):
                    r0 = sp.snap(r0)
                for half in range(2):
                    sp.wait_ge(arow_read, 2 * (c * CT + k) + half - 1 + CREDIT)
                    sp.dma_start(arow[half][:, :], d["adj"][bass.ds(r0, P), half * HALF:(half + 1) * HALF])\
                      .then_inc(arow_in[half], 16)

            def save(q):
                col0 = q * CW
                if not isinstance(col0, int):
                    col0 = sp.snap(col0)
                sp.wait_ge(es_made, q + 1)
                sp.dma_start(d["es"][:, bass.ds(col0, width(q))], es[:, 0:width(q)]).then_inc(es_saved, 16)

            def chunk(q):
                w = width(q)
                col0 = q * CW
                if not isinstance(col0, int):
                    col0 = sp.snap(col0)
                for j in range(T):
                    sp.wait_ge(unit_done, NU * q + HEADS * slot_before(j, RA, T) + HEADS + CREDIT)
                    sp.dma_start(at[j % RA][:, 0:w], d["adjT"][j * P:(j + 1) * P, bass.ds(col0, w)])\
                      .then_inc(at_in[j % RA], 16)
                    for c, r in rows_at(q, j):
                        if r % HEADS == 0:
                            row_tile(c, r // HEADS)
                    if j == 6 and not (isinstance(q, int) and q == 0):
                        save(q - 1)

            for k in range(CT):
                row_tile(0, k)
                if k == 0:
                    for h in range(HEADS):
                        sp.dma_start(erow[:, h, :], d["e_rows"][0, h * NP:(h + 1) * NP].partition_broadcast(P))\
                          .then_inc(erow_in, 16)
            each_chunk(sp, chunk)
            save(LAST)
            sp.wait_ge(es_saved, 16 * (LAST + 1))

        @block.gpsimd
        def _(pool):
            pool.sem_inc(w_pool, CREDIT)
            pool.memset(ones_not_i[:, :, :], 1.0).then_inc(table_made, 1)
            pool.wait_ge(table_made, 1)
            pool.tensor_copy(ones_not_i[:, CHUNKS - 1, :], not_i[:, :]).then_inc(table_made, 1)
            pool.wait_ge(table_made, 2)

            def arrived(q, j):
                pool.wait_ge(at_in[j % RA], 16 * (q * loads_per_round(j, RA, T) + loads_before(j, RA) + 1))

            def zero_diagonal(q, j):
                c = slice(j % CT * P, (j % CT + 1) * P)
                a = at[j % RA]
                if isinstance(q, int):
                    if q == j // CT:
                        pool.tensor_tensor(a[:, c], a[:, c], not_i[:, :], ALU.mult).then_inc(diag_zero, 1)
                        return
                elif j // CT < LAST:
                    which = ones_not_i[:, bass.ds(q - j // CT + CHUNKS - 1, 1), :]
                    pool.tensor_tensor(a[:, c], a[:, c], which.rearrange("p a n -> p (a n)"), ALU.mult)\
                        .then_inc(diag_zero, 1)
                    return
                pool.sem_inc(diag_zero, 1)

            def chunk(q):
                w = width(q)
                for j, h in on_pool(q):
                    u = HEADS * j + h
                    ends_step = (j, h + 1) not in on_pool(q)
                    if ends_step and j + 1 < T:
                        arrived(q, j + 1)
                    pool.wait_ge(diag_zero, T * q + j + 1)
                    pool.wait_ge(exp_made, NU * q + u + 1)
                    pool.wait_ge(unit_done, NU * q + u - RW + 1 + CREDIT)
                    pool.tensor_tensor(W[u % RW][:, 0:w], ex[u % RE][:, 0:w], at[j % RA][:, 0:w], ALU.mult)\
                        .then_inc(w_pool, 1)
                    if ends_step and j + 1 < T:
                        zero_diagonal(q, j + 1)
                    elif ends_step and not is_last(q):
                        arrived(q + 1, 0)
                        pool.sem_inc(first_seen, 1)
                        zero_diagonal(q + 1, 0)

            arrived(0, 0)
            zero_diagonal(0, 0)
            each_chunk(pool, chunk)

        @block.scalar
        def _(act):
            act.sem_inc(row_exp, CREDIT)

            def row_unit(c, r):
                k, h = divmod(r, HEADS)
                s = h * CT + k
                act.wait_ge(nm_made, ROWS * c + r + 1)
                nc.scalar.activation(L[r % 2][:, :], L[r % 2][:, :], ACT.Exp, bias=nm[:, s:s + 1],
                                     accum_out=den[:, s:s + 1]).then_inc(row_exp, 1)

            def chunk(q):
                w = width(q)
                for j in range(T):
                    for h in range(HEADS):
                        u = HEADS * j + h
                        act.wait_ge(arg_made, NU * q + u + 1)
                        nc.scalar.activation(ex[u % RE][:, 0:w], ex[u % RE][:, 0:w], ACT.Exp).then_inc(exp_made, 1)
                    for c, r in rows_at(q, j - 1):
                        row_unit(c, r)

            for r in range(ROWS):
                row_unit(0, r)
            each_chunk(act, chunk)

        @block.vector
        def _(dve):
            dve.sem_inc(logit_made, CREDIT)
            dve.sem_inc(arow_read, CREDIT)
            dve.sem_inc(w_dve, CREDIT)
            dve.sem_inc(acc_free, HEADS)

            def mask_tile(c, k):
                n = c * CT + k
                for half in range(2):
                    dve.wait_ge(arow_in[half], 16 * n + 16)
                    dve.tensor_scalar(mask[:, half * HALF:(half + 1) * HALF], arow[half][:, :], 0.0, None, ALU.is_gt)\
                       .then_inc(arow_read, 1)
                dve.wait_ge(arow_read, 2 * n + 2 + CREDIT)
                own = bass.ds(n * P, P)
                dve.tensor_tensor(mask[:, own], mask[:, own], not_i[:, :], ALU.mult).then_inc(mask_whole, 1)
                dve.wait_ge(mask_whole, n + 1)

            def row_unit(c, r):
                u = ROWS * c + r
                k, h = divmod(r, HEADS)
                s = h * CT + k
                if h == 0:
                    mask_tile(c, k)
                dve.wait_ge(row_exp, u - 1 + CREDIT)
                dve.memset(scratch[:, :], 0.0)
                dve.wait_ge(erow_in, 16 * HEADS)
                dve.tensor_tensor_reduce(out=L[r % 2][:, :], in0=mask[:, :], in1=erow[:, h, :], scale=1.0,
                                         scalar=0.0, op0=ALU.mult, op1=ALU.max,
                                         accum_out=mx[:, s:s + 1]).then_inc(logit_made, 1)
                dve.wait_ge(logit_made, u + 1 + CREDIT)
                dve.tensor_scalar(nm[:, s:s + 1], mx[:, s:s + 1], -1.0, None, ALU.mult).then_inc(nm_made, 1)

            def invert(q):
                dve.wait_ge(row_exp, ROWS * q + HEADS * tiles(q) + CREDIT)
                dve.reciprocal(rden[:, :], den[:, :]).then_inc(sums_inverted, 1)
                dve.wait_ge(sums_inverted, 2 * q + 1)
                dve.tensor_scalar(rden[:, :], rden[:, :], 1.0 / HEADS, None, ALU.mult).then_inc(sums_inverted, 1)
                dve.wait_ge(sums_inverted, 2 * q + 2)

            def take(q, i, src):
                h, a, n = pieces(q)[i]
                dve.wait_ge(spread, turn(q, i, src) + 1)
                cols = slice(a * P, (a + n) * P)
                if src is nm:
                    out = nmb[:, bass.ds(q & 1, 1), h, cols].rearrange("p a n -> p (a n)")
                else:
                    out = invb[:, h, cols]
                dve.tensor_copy(out, aux[bank(q, i, src)][:, 0:n * P]).then_inc(spread_out, 1)

            def args(q, j):
                if j == 0:
                    dve.wait_ge(spread_out, turn(q, len(pieces(q)), nm))
                for h in range(HEADS):
                    u = HEADS * j + h
                    wait_weights(dve, q, j - 2, h)
                    dve.tensor_scalar(ex[u % RE][:, 0:width(q)],
                                      nmb[:, bass.ds(q & 1, 1), h, 0:width(q)].rearrange("p a n -> p (a n)"),
                                      ecol[:, h * T + j:h * T + j + 1], 0.0, ALU.add, ALU.min).then_inc(arg_made, 1)

            def finish(q):
                w = width(q)
                wb = min(w, HW)
                if not (isinstance(q, int) and q == 0):
                    dve.wait_ge(es_saved, 16 * q)
                dve.wait_ge(spread_out, turn(q, len(pieces(q)), rden))
                for h in range(HEADS):
                    dve.wait_ge(unit_done, NU * q + NU - HEADS + h + 1 + CREDIT)
                    a = acc[h][:, 0:w // wb, 0:wb]
                    i = invb[:, h, 0:w].rearrange("p (b n) -> p b n", n=wb)
                    o = (es if h == 0 else es2)[:, 0:w].rearrange("p (b n) -> p b n", n=wb)
                    dve.tensor_tensor(o, a, i, ALU.mult).then_inc(acc_free, 1)
                    dve.wait_ge(acc_free, HEADS * q + h + 1 + HEADS)
                    if h:
                        last = dve.tensor_tensor(es[:, 0:w], es[:, 0:w], es2[:, 0:w], ALU.add)
                        last.then_inc(es_added if h < HEADS - 1 else es_made, 1)
                        if h < HEADS - 1:
                            dve.wait_ge(es_added, q + 1)

            def chunk(q):
                w = width(q)
                for j in range(T):
                    if j + 1 < T:
                        args(q, j + 1)
                    elif not is_last(q):
                        args(q + 1, 0)
                    for h in range(HEADS):
                        if (j, h) not in on_dve(q):
                            continue
                        u = HEADS * j + h
                        dve.wait_ge(diag_zero, T * q + j + 1)
                        dve.wait_ge(exp_made, NU * q + u + 1)
                        dve.wait_ge(unit_done, NU * q + u - RW + 1 + CREDIT)
                        dve.tensor_tensor(W[u % RW][:, 0:w], ex[u % RE][:, 0:w], at[j % RA][:, 0:w], ALU.mult)\
                           .then_inc(w_dve, 1)
                    if j == 0 and not (isinstance(q, int) and q == 0):
                        finish(q - 1)
                    for i, step in enumerate(INV_SEND[:len(pieces(q))]):
                        if step + TAKE_LAG == j:
                            take(q, i, rden)
                    if not is_last(q):
                        for i, step in enumerate(MAX_SEND[:len(pieces(q + 1))]):
                            if step + TAKE_LAG == j:
                                take(q + 1, i, nm)
                        if j == ROW_END + 2:
                            invert(q + 1)
                    for c, r in rows_at(q, j):
                        row_unit(c, r)

            for r in range(ROWS):
                row_unit(0, r)
            for i in range(len(PIECES)):
                take(0, i, nm)
            args(0, 0)
            invert(0)
            each_chunk(dve, chunk)
            finish(LAST)

        @block.tensor
        def _(pe):
            pe.sem_inc(unit_done, CREDIT)

            def send(q, i, src):
                h, a, n = pieces(q)[i]
                if src is nm:
                    pe.wait_ge(nm_made, ROWS * q + HEADS * (a + n))
                else:
                    pe.wait_ge(sums_inverted, 2 * q + 2)
                if not (isinstance(q, int) and q == 0 and src is nm and i < 2):
                    pe.wait_ge(spread_out, turn(q, i, src) - 1)
                for k in range(a, a + n):
                    s = h * CT + k
                    m = nc.tensor.matmul(aux[bank(q, i, src)][:, (k - a) * P:(k - a + 1) * P],
                                         src[:, s:s + 1].to_broadcast([P, P]), ident[:, :], start=True, stop=True)
                m.then_inc(spread, 1)

            def chunk(q):
                w = width(q)
                for j in range(T):
                    for h in range(HEADS):
                        if j == 0:
                            pe.wait_ge(acc_free, HEADS * q + h + 1)
                        wait_weights(pe, q, j, h)
                        for b in range(0, w, HW):
                            n = min(HW, w - b)
                            m = nc.tensor.matmul(acc[h][:, b // HW, 0:n], hw[:, j, h * H:(h + 1) * H],
                                                 W[(HEADS * j + h) % RW][:, b:b + n], start=(j == 0), stop=(j == T - 1))
                        m.then_inc(unit_done, 1)
                    for i, step in enumerate(INV_SEND[:len(pieces(q))]):
                        if step == j:
                            send(q, i, rden)
                    if not is_last(q):
                        for i, step in enumerate(MAX_SEND[:len(pieces(q + 1))]):
                            if step == j:
                                send(q + 1, i, nm)

            for i in range(len(PIECES)):
                send(0, i, nm)
            each_chunk(pe, chunk)


def attend_signed(nc, keep, d):
    hw, ident, not_i, flag = (keep[k] for k in ("hw", "ident", "not_i", "flag"))
    GROUPS = [list(range(g, min(g + 4, T))) for g in range(0, T, 4)]
    NG = len(GROUPS)
    with ExitStack() as ctx:
        t = Tools(nc, ctx)
        arow = t.sb("g_arow", [P, NP])
        plus = t.sb("g_plus", [P, NP])
        minus = t.sb("g_minus", [P, NP])
        L = t.sb("g_l", [P, NP])
        W = t.sb("g_w", [P, NP])
        wt = t.sb("g_wt", [P, 512])
        mx, nm, den, rden = (t.sb(f"g_{s}", [P, 1]) for s in ("mx", "nm", "den", "rden"))
        est = t.sb("g_est", [P, P])
        turn = t.ps("g_turn", [P, 512])
        acc = t.ps("g_acc", [P, P])
        (a_in, e_in, diag_zero, logit, prob, weight, turned, copied, multiplied, est_made, est_saved, est_seen, link) = (
            t.sem(s) for s in ("g_a_in", "g_e_in", "g_diag", "g_logit", "g_prob", "g_weight", "g_turned", "g_copied",
                               "g_multiplied", "g_est_made", "g_est_saved", "g_est_seen", "g_link"))
        block = ctx.enter_context(nc.Block())

        def when_signed(eng, program, credits=(), end=lambda: None):
            negative = eng.value_load(flag[0:1, 0:1], min_val=0, max_val=1 << 24)
            with eng.If(negative > 0):
                for counter, n in credits:
                    eng.sem_inc(counter, n)
                with eng.Fori(0, T) as i:
                    program(i)
                end()

        @block.sync
        def _(sp):
            def tile(i):
                at_tile = sp.snap(i * P)
                sp.wait_ge(weight, HEADS * i + 1)
                sp.dma_start(arow[:, :], d["adj"][bass.ds(at_tile, P), :]).then_inc(a_in, 16)
                for h in range(HEADS):
                    sp.wait_ge(weight, HEADS * i + h + 1)
                    sp.dma_start(plus[:, :], d["e_rows"][0, h * NP:(h + 1) * NP].partition_broadcast(P)).then_inc(e_in, 16)
                    sp.dma_start(minus[:, :], d["e_rows"][1, h * NP:(h + 1) * NP].partition_broadcast(P)).then_inc(e_in, 16)
                sp.wait_ge(est_made, i + 2)
                sp.sem_inc(est_seen, 1)
                sp.dma_start(d["es"][:, bass.ds(at_tile, P)], est[:, :]).then_inc(est_saved, 16)
            when_signed(sp, tile, [(est_saved, 16)], lambda: sp.wait_ge(est_saved, 16 * T + 16))

        @block.scalar
        def _(act):
            def tile(i):
                for h in range(HEADS):
                    act.wait_ge(logit, HEADS * i + h + 1)
                    nc.scalar.activation(L[:, :], L[:, :], ACT.Exp, bias=nm[:, :], accum_out=den[:, :]).then_inc(prob, 1)
                    for g, group in enumerate(GROUPS):
                        n = NG * (HEADS * i + h) + g
                        act.wait_ge(turned, n + 1)
                        act.wait_ge(multiplied, n + 1)
                        nc.scalar.activation(wt[:, 0:len(group) * P], turn[:, 0:len(group) * P], ACT.Copy).then_inc(copied, 1)
            when_signed(act, tile, [(copied, 1)])

        @block.vector
        def _(dve):
            def tile(i):
                dve.wait_ge(a_in, 16 * i + 16)
                c = bass.ds(i * P, P)
                dve.tensor_tensor(arow[:, c], arow[:, c], not_i[:, :], ALU.mult).then_inc(diag_zero, 1)
                dve.wait_ge(diag_zero, i + 1)
                for h in range(HEADS):
                    u = HEADS * i + h
                    n = 0

                    def then(ins):
                        nonlocal n
                        n += 1
                        ins.then_inc(link, 1)
                        dve.wait_ge(link, 6 * u + n)

                    dve.wait_ge(e_in, 32 * u + 32)
                    then(dve.scalar_tensor_tensor(plus[:, :], arow[:, :], 0.0, plus[:, :], ALU.is_gt, ALU.mult))
                    then(dve.scalar_tensor_tensor(minus[:, :], arow[:, :], 0.0, minus[:, :], ALU.is_lt, ALU.mult))
                    then(dve.tensor_tensor(L[:, :], plus[:, :], minus[:, :], ALU.add))
                    then(dve.tensor_reduce(mx[:, :], L[:, :], AX, ALU.max))
                    dve.tensor_scalar(nm[:, :], mx[:, :], -1.0, None, ALU.mult).then_inc(logit, 1)
                    dve.wait_ge(prob, u + 1)
                    then(dve.reciprocal(rden[:, :], den[:, :]))
                    then(dve.tensor_scalar(rden[:, :], rden[:, :], 1.0 / HEADS, None, ALU.mult))
                    dve.wait_ge(multiplied, NG * u + 1)
                    dve.scalar_tensor_tensor(W[:, :], L[:, :], rden[:, :], arow[:, :], ALU.mult, ALU.mult)\
                       .then_inc(weight, 1)
                dve.wait_ge(multiplied, NG * HEADS * i + NG * HEADS + 1)
                dve.wait_ge(est_saved, 16 * i + 16)
                dve.tensor_copy(est[:, :], acc[:, :]).then_inc(est_made, 1)
            when_signed(dve, tile, [(weight, 1), (est_made, 1)])

        @block.tensor
        def _(pe):
            def tile(i):
                pe.wait_ge(est_made, i + 1)
                for h in range(HEADS):
                    pe.wait_ge(weight, HEADS * i + h + 2)
                    for g, group in enumerate(GROUPS):
                        n = NG * (HEADS * i + h) + g
                        pe.wait_ge(copied, n + 1)
                        for s, j in enumerate(group):
                            m = nc.tensor.transpose(turn[:, s * P:(s + 1) * P], W[:, j * P:(j + 1) * P], ident[:, :])
                        m.then_inc(turned, 1)
                        pe.wait_ge(copied, n + 2)
                        for s, j in enumerate(group):
                            m = nc.tensor.matmul(acc[:, :], hw[:, j, h * H:(h + 1) * H], wt[:, s * P:(s + 1) * P],
                                                 start=(h == 0 and j == 0), stop=(h == HEADS - 1 and j == T - 1))
                        m.then_inc(multiplied, 1)
            when_signed(pe, tile, [(multiplied, 1)])


def gru(nc, keep, d):
    go = keep["go"]
    CHUNK = BANK
    NC = NP // CHUNK
    with ExitStack() as ctx:
        t = Tools(nc, ctx)
        xT, ns, es = (t.sb(f"e_{s}", [P, NP]) for s in ("xT", "ns", "es"))
        w = t.sb("e_w", [P, 4, 3 * H])
        b = t.sb("e_b", [P, 4, 3])
        brz = t.sb("e_brz", [P, 2, 2])
        r, z, pre, cand, diff = ([t.sb(f"e_{s}{g}", [P, CHUNK]) for g in range(2)] for s in ("r", "z", "pre", "cand", "diff"))
        ps = [[t.ps(f"e_p{g}{i}", [P, 512]) for i in range(4)] for g in range(2)]
        x_in, ns_in, es_in, w_in = (t.sem(s) for s in ("x_in", "ns_in", "es_in", "w_in"))
        gates, sig, pre_made, cand_made, cell_done, link, bias_made = (
            t.sem(s) for s in ("gates", "sig", "pre_made", "cand_made", "cell_done", "link", "bias_made"))
        block = ctx.enter_context(nc.Block())
        R, Z, NI, NH = range(4)

        @block.sync
        def _(sp):
            sp.dma_start(w[:, :, :], d["gru_w"]).then_inc(w_in, 16)
            sp.dma_start(b[:, :, :], d["gru_b"]).then_inc(w_in, 16)
            sp.dma_start(xT[:, :], d["xT"]).then_inc(x_in, 16)
            sp.dma_start(ns[:, :], d["ns"]).then_inc(ns_in, 16)
            sp.dma_start(es[:, :], d["es"]).then_inc(es_in, 16)

        @block.tensor
        def _(pe):
            pe.wait_ge(w_in, 32)
            pe.wait_ge(x_in, 16)
            pe.wait_ge(ns_in, 16)
            pe.wait_ge(es_in, 16)
            with pe.Fori(0, NC) as c:
                cols = bass.ds(c * CHUNK, CHUNK)
                for g, src in enumerate((ns, es)):
                    pe.wait_ge(pre_made, 2 * c + g - 1 + 2)
                    pe.wait_ge(sig, 2 * c + g - 1 + 2)
                    for gate in (R, Z):
                        nc.tensor.matmul(ps[g][gate][:, 0:CHUNK], w[:, 2 * g, gate * H:(gate + 1) * H], src[:, cols], start=True, stop=False)
                        nc.tensor.matmul(ps[g][gate][:, 0:CHUNK], w[:, 2 * g + 1, gate * H:(gate + 1) * H], xT[:, cols], start=False, stop=True)
                    nc.tensor.matmul(ps[g][NI][:, 0:CHUNK], w[:, 2 * g, 2 * H:3 * H], src[:, cols], start=True, stop=True)
                    nc.tensor.matmul(ps[g][NH][:, 0:CHUNK], w[:, 2 * g + 1, 2 * H:3 * H], xT[:, cols], start=True, stop=True).then_inc(gates, 1)

        @block.scalar
        def _(act):
            act.sem_inc(sig, 2)
            act.wait_ge(bias_made, 1)
            with act.Fori(0, NC) as c:
                for g in range(2):
                    u = 2 * c + g
                    act.wait_ge(gates, u + 1)
                    act.wait_ge(cell_done, u - 1 + 2)
                    nc.scalar.activation(r[g][:, :], ps[g][R][:, 0:CHUNK], ACT.Sigmoid, bias=brz[:, g, R:R + 1])
                    nc.scalar.activation(z[g][:, :], ps[g][Z][:, 0:CHUNK], ACT.Sigmoid, bias=brz[:, g, Z:Z + 1]).then_inc(sig, 1)
                    act.wait_ge(pre_made, u + 1 + 2)
                    nc.scalar.activation(cand[g][:, :], pre[g][:, :], ACT.Tanh, bias=b[:, 2 * g, 2:3]).then_inc(cand_made, 1)

        @block.vector
        def _(dve):
            dve.sem_inc(pre_made, 2)
            dve.sem_inc(cell_done, 2)
            dve.wait_ge(w_in, 32)
            for g in range(2):
                m = dve.tensor_tensor(brz[:, g, :], b[:, 2 * g, 0:2], b[:, 2 * g + 1, 0:2], ALU.add)
            m.then_inc(bias_made, 1)
            dve.wait_ge(x_in, 16)
            with dve.Fori(0, NC) as c:
                cols = bass.ds(c * CHUNK, CHUNK)
                for g in range(2):
                    u = 2 * c + g
                    steps = 3 + g
                    base = 7 * c + 3 * g
                    dve.wait_ge(sig, u + 1 + 2)
                    dve.scalar_tensor_tensor(pre[g][:, :], ps[g][NH][:, 0:CHUNK], b[:, 2 * g + 1, 2:3], r[g][:, :], ALU.add, ALU.mult).then_inc(link, 1)
                    dve.wait_ge(link, base + 1)
                    dve.tensor_tensor(pre[g][:, :], ps[g][NI][:, 0:CHUNK], pre[g][:, :], ALU.add).then_inc(pre_made, 1)
                    dve.wait_ge(cand_made, u + 1)
                    dve.tensor_tensor(diff[g][:, :], xT[:, cols], cand[g][:, :], ALU.subtract).then_inc(link, 1)
                    dve.wait_ge(link, base + 2)
                    dve.tensor_tensor(diff[g][:, :], diff[g][:, :], z[g][:, :], ALU.mult).then_inc(link, 1)
                    dve.wait_ge(link, base + 3)
                    if g == 0:
                        dve.tensor_tensor(go[:, cols], diff[g][:, :], cand[g][:, :], ALU.add).then_inc(cell_done, 1)
                    else:
                        dve.tensor_tensor(diff[g][:, :], diff[g][:, :], cand[g][:, :], ALU.add).then_inc(link, 1)
                        dve.wait_ge(link, base + 4)
                        dve.wait_ge(cell_done, u + 2)
                        dve.tensor_tensor(go[:, cols], go[:, cols], diff[g][:, :], ALU.add).then_inc(cell_done, 1)


def wide(col):
    return col.unsqueeze(2).broadcast_to([P, T, H])


class Chain:

    def __init__(self, eng, sem):
        self.eng, self.sem, self.n = eng, sem, 0

    def __call__(self, ins):
        self.n += 1
        ins.then_inc(self.sem, 1)
        self.eng.wait_ge(self.sem, self.n)


def norm_dve(dve, then, t, v, out, sq, stat, var_made, root_made, times):
    mean, var, root, tmp = stat
    then(dve.tensor_reduce(mean[:, :], v[:, :, :], AX, ALU.add))
    then(dve.tensor_scalar(mean[:, :], mean[:, :], 1.0 / H, None, ALU.mult))
    then(dve.tensor_tensor(v[:, :, :], v[:, :, :], wide(mean[:, :]), ALU.subtract))
    then(dve.tensor_tensor(sq[:, :, :], v[:, :, :], v[:, :, :], ALU.mult))
    then(dve.tensor_reduce(var[:, :], sq[:, :, :], AX, ALU.add))
    dve.tensor_scalar(var[:, :], var[:, :], 1.0 / H, EPS, ALU.mult, ALU.add).then_inc(var_made, 1)
    dve.wait_ge(root_made, times)
    then(dve.reciprocal(tmp[:, :], root[:, :]))
    then(dve.tensor_tensor(tmp[:, :], tmp[:, :], var[:, :], ALU.mult))
    then(dve.tensor_tensor(tmp[:, :], tmp[:, :], root[:, :], ALU.add))
    then(dve.tensor_scalar(tmp[:, :], tmp[:, :], 0.5, None, ALU.mult))
    then(dve.reciprocal(root[:, :], tmp[:, :]))
    return dve.tensor_tensor(out[:, :, :], v[:, :, :], wide(root[:, :]), ALU.mult)


def first_norm(nc, keep, d):
    go, ident, diag, diag1, dinv, s_hi, s_lo, q = (
        keep[k] for k in ("go", "ident", "diag", "diag1", "dinv", "s_hi", "s_lo", "q"))
    with ExitStack() as ctx:
        t = Tools(nc, ctx)
        x = t.sb("h_x", [P, T, H])
        v = t.sb("h_v", [P, T, H])
        x1 = t.sb("h_x1", [P, T, H])
        x1T = t.sb("h_x1T", [P, T, P])
        w1 = t.sb("h_w1", [P, H])
        b1 = t.sb("h_b1", [P, H])
        own = t.sb("h_own", [P, T])
        stat = [t.sb(f"h_st{i}", [P, T]) for i in range(4)]
        ps = t.ps("h_ps", [P, T, P])
        x_in, w_in, link, turned, var_made, root_made, x1_made, x1_turned, x1T_made, proj, ps_free = (
            t.sem(s) for s in ("x_in", "w_in", "link", "turned", "var_made", "root_made", "x1_made", "x1_turned",
                               "x1T_made", "proj", "ps_free"))
        block = ctx.enter_context(nc.Block())

        @block.sync
        def _(sp):
            sp.dma_start(x[:, :, :], d["x"]).then_inc(x_in, 16)
            sp.dma_start(w1[:, :], d["w1"]).then_inc(w_in, 16)
            sp.dma_start(b1[:, :], d["b1"].partition_broadcast(P)).then_inc(w_in, 16)

        @block.tensor
        def _(pe):
            for k in range(T):
                m = nc.tensor.transpose(ps[:, k, :], go[:, k * P:(k + 1) * P], ident[:, :])
            m.then_inc(turned, 1)
            pe.wait_ge(x1_made, 1)
            for k in range(T):
                m = nc.tensor.transpose(ps[:, k, :], x1[:, k, :], ident[:, :])
            m.then_inc(x1_turned, 1)
            pe.wait_ge(x1T_made, 1)
            pe.wait_ge(w_in, 32)
            for k in range(T):
                m = nc.tensor.matmul(ps[:, k, :], x1T[:, k, :], w1[:, :], start=True, stop=True)
            m.then_inc(proj, 1)

        @block.scalar
        def _(act):
            act.wait_ge(var_made, 1)
            nc.scalar.activation(stat[2][:, :], stat[1][:, :], ACT.Sqrt).then_inc(root_made, 1)
            act.wait_ge(x1_turned, 1)
            nc.scalar.activation(x1T[:, :, :], ps[:, :, :], ACT.Copy).then_inc(x1T_made, 1)

        @block.vector
        def _(dve):
            then = Chain(dve, link)
            dve.wait_ge(turned, 1)
            then(dve.tensor_tensor(v[:, :, :], ps[:, :, :], wide(diag[:, :]), ALU.mult))
            dve.wait_ge(x_in, 16)
            then(dve.tensor_tensor(v[:, :, :], v[:, :, :], x[:, :, :], ALU.add))
            norm_dve(dve, then, t, v, x1, x, stat, var_made, root_made, 1).then_inc(x1_made, 1)
            then(dve.tensor_tensor(own[:, :], dinv[:, :], diag1[:, :], ALU.mult))
            dve.wait_ge(proj, 1)
            then(dve.tensor_tensor(v[:, :, :], ps[:, :, :], b1[:, :].unsqueeze(1).broadcast_to([P, T, H]), ALU.add))
            then(dve.tensor_tensor(v[:, :, :], v[:, :, :], wide(dinv[:, :]), ALU.mult))
            then(dve.tensor_copy(s_hi[:, :, :], v[:, :, :]))
            dve.tensor_tensor(s_lo[:, :, :], v[:, :, :], s_hi[:, :, :].bitcast(F32), ALU.subtract)
            then(dve.tensor_tensor(x[:, :, :], v[:, :, :], wide(own[:, :]), ALU.mult))
            dve.tensor_tensor(q[:, :, :], x[:, :, :], x1[:, :, :], ALU.add)


def spread_layer(nc, keep, d):
    ident, not_i, dinv, s_hi, s_lo, q = (keep[k] for k in ("ident", "not_i", "dinv", "s_hi", "s_lo", "q"))
    RA, RB = 4, 2
    BANKS = [(b, min(512, NP - b)) for b in range(0, NP, 512)]
    with ExitStack() as ctx:
        t = Tools(nc, ctx)
        at = [t.sb(f"f_at{i}", [P, NP]) for i in range(RA)]
        hi = [t.sb(f"f_hi{i}", [P, NP], F32R) for i in range(RB)]
        lo = [t.sb(f"f_lo{i}", [P, NP], F32R) for i in range(RB)]
        stat = [t.sb(f"f_st{i}", [P, T]) for i in range(4)]
        acc = t.ps("f_acc", [P, T, P])
        sums = acc[:, :, :].rearrange("p t f -> p (t f)")
        at_in = [t.sem(f"at_in{i}") for i in range(RA)]
        diag_zero, hi_done, lo_done, pe_done, sums_out, turned, link, var_made, root_made, y_made, y_saved = (
            t.sem(s) for s in ("diag_zero", "hi_done", "lo_done", "pe_done", "sums_out", "turned", "link",
                               "var_made", "root_made", "y_made", "y_saved"))
        block = ctx.enter_context(nc.Block())
        v = at[0][:, :].rearrange("p (t f) -> p t f", f=H)
        sq = at[1][:, :].rearrange("p (t f) -> p t f", f=H)
        y = at[2][:, :].rearrange("p (t f) -> p t f", f=H)
        accT = at[3]

        @block.sync
        def _(sp):
            for j in range(T):
                if j >= RA:
                    sp.wait_ge(hi_done, j - RA + 1)
                    sp.wait_ge(lo_done, j - RA + 1)
                sp.dma_start(at[j % RA][:, :], d["adjT"][j * P:(j + 1) * P, :]).then_inc(at_in[j % RA], 16)
            sp.wait_ge(y_made, 1)
            sp.dma_start(d["out"], y).then_inc(y_saved, 16)
            sp.wait_ge(y_saved, 16)

        @block.scalar
        def _(act):
            for j in range(T):
                act.wait_ge(diag_zero, j + 1)
                if j >= RB:
                    act.wait_ge(pe_done, j - RB + 1)
                    act.wait_ge(lo_done, j - RB + 1)
                nc.scalar.activation(hi[j % RB][:, :], at[j % RA][:, :], ACT.Copy).then_inc(hi_done, 1)
            act.wait_ge(pe_done, T)
            act.wait_ge(lo_done, T)
            nc.scalar.activation(accT[:, :], sums[:, :], ACT.Copy).then_inc(sums_out, 1)
            act.wait_ge(var_made, 1)
            nc.scalar.activation(stat[2][:, :], stat[1][:, :], ACT.Sqrt).then_inc(root_made, 1)

        @block.vector
        def _(dve):
            for j in range(T):
                dve.wait_ge(at_in[j % RA], 16 * (j // RA + 1))
                c = slice(j * P, (j + 1) * P)
                dve.tensor_tensor(at[j % RA][:, c], at[j % RA][:, c], not_i[:, :], ALU.mult).then_inc(diag_zero, 1)
                dve.wait_ge(hi_done, j + 1)
                if j >= RB:
                    dve.wait_ge(pe_done, j - RB + 1)
                dve.tensor_tensor(lo[j % RB][:, :], at[j % RA][:, :], hi[j % RB][:, :].bitcast(F32), ALU.subtract)\
                   .then_inc(lo_done, 1)
            then = Chain(dve, link)
            dve.wait_ge(turned, 1)
            then(dve.tensor_tensor(v, acc[:, :, :], wide(dinv[:, :]), ALU.mult))
            then(dve.tensor_tensor(v, v, q[:, :, :], ALU.add))
            norm_dve(dve, then, t, v, y, sq, stat, var_made, root_made, 1).then_inc(y_made, 1)

        @block.tensor
        def _(pe):
            for j in range(T):
                for w, m, ready in ((s_hi, hi, hi_done), (s_lo, hi, None), (s_hi, lo, lo_done)):
                    if ready is not None:
                        pe.wait_ge(ready, j + 1)
                    for b, n in BANKS:
                        mm = nc.tensor.matmul(sums[:, b:b + n], w[:, j, :], m[j % RB][:, b:b + n],
                                              start=(j == 0 and w is s_hi and m is hi), stop=(j == T - 1 and m is lo))
                mm.then_inc(pe_done, 1)
            pe.wait_ge(sums_out, 1)
            for k in range(T):
                m = nc.tensor.transpose(acc[:, k, :], accT[:, k * P:(k + 1) * P], ident[:, :])
            m.then_inc(turned, 1)


def build(nc, adj, adjT, x, xT, diag, gat_w, gat_a, gru_w, gru_b, w1, b1, out):
    scratch = {k: nc.dram_tensor(k, s, F32).ap() for k, s in (("e_rows", (2, HEADS * NP)), ("ns_d", (P, NP)), ("es_d", (P, NP)))}
    d = {"adj": adj, "adjT": adjT, "x": x, "xT": xT, "diag": diag, "gat_w": gat_w, "gat_a": gat_a,
         "gru_w": gru_w, "gru_b": gru_b, "w1": w1, "b1": b1,
         "e_rows": scratch["e_rows"], "ns": scratch["ns_d"], "es": scratch["es_d"],
         "out": out.rearrange("(t p) f -> p t f", p=P)}
    with ExitStack() as ctx:
        t = Tools(nc, ctx)
        keep = {"ident": t.sb("ident", [P, P]), "not_i": t.sb("not_i", [P, P]),
                "ecol": t.sb("ecol", [P, E2 * T]), "flag": t.sb("flag", [P, 1], I32),
                "dinv": t.sb("dinv", [P, T]), "diag": t.sb("diag", [P, T]), "diag1": t.sb("diag1", [P, T])}
        with ExitStack() as ctx1:
            t1 = Tools(nc, ctx1)
            keep["hw"] = t1.sb("hw", [P, T, HEADS * H])
            with ExitStack() as ctx2:
                t2 = Tools(nc, ctx2)
                keep |= {"x_hi": t2.sb("x_hi", [P, T, H], F32R), "x_lo": t2.sb("x_lo", [P, T, H], F32R),
                         "up": t2.sb("up", [P, T, EW], BF16), "um": t2.sb("um", [P, T, EW], BF16),
                         "ns": t2.sb("ns", [P, NP]), "csum": t2.sb("csum", [P, NP]), "elog": t2.sb("elog", [EW, NP])}
                project(nc, keep, d)
                aggregate(nc, keep, d)
                logits(nc, keep, d)
            attend(nc, keep, d)
            attend_signed(nc, keep, d)
        keep |= {"go": t.sb("go", [P, NP])}
        gru(nc, keep, d)
        keep |= {"s_hi": t.sb("s_hi", [P, T, H], F32R), "s_lo": t.sb("s_lo", [P, T, H], F32R), "q": t.sb("q", [P, T, H])}
        first_norm(nc, keep, d)
        spread_layer(nc, keep, d)


def kernel(x, adj, L0_gnn_gat_W, L0_gnn_gat_a, L0_gnn_edge_Wih, L0_gnn_edge_Whh, L0_gnn_edge_bih, L0_gnn_edge_bhh,
           L0_gnn_node_Wih, L0_gnn_node_Whh, L0_gnn_node_bih, L0_gnn_node_bhh, L1_gnn_W, L1_gnn_b):
    import numpy as np
    import concourse.bacc as bacc
    from concourse.bass_utils import run_bass_kernel_spmd

    def f(a):
        return np.ascontiguousarray(a)

    adj = np.asarray(adj)
    padded = np.zeros((NP, NP), adj.dtype)
    padded[:N, :N] = adj
    padded_t = np.zeros((NP, NP), adj.dtype)
    padded_t[:N, :N] = adj.T
    diag = np.zeros((NP,), adj.dtype)
    diag[:N] = np.diagonal(adj)
    xp = np.zeros((NP, H), np.asarray(x).dtype)
    xp[:N] = np.asarray(x)
    weights = (L0_gnn_edge_Wih, L0_gnn_edge_Whh, L0_gnn_node_Wih, L0_gnn_node_Whh)
    biases = (L0_gnn_edge_bih, L0_gnn_edge_bhh, L0_gnn_node_bih, L0_gnn_node_bhh)
    arrays = {
        "adj": padded, "adjT": padded_t,
        "x": f(xp.reshape(T, P, H).transpose(1, 0, 2)), "xT": f(xp.T), "diag": f(diag.reshape(T, P).T),
        "gat_w": f(np.asarray(L0_gnn_gat_W).transpose(1, 0, 2).reshape(H, HEADS * H)),
        "gat_a": f(np.asarray(L0_gnn_gat_a).reshape(HEADS * 2 * H)),
        "gru_w": f(np.stack([np.asarray(w).T for w in weights], axis=1)),
        "gru_b": f(np.stack([np.asarray(b).reshape(3, H).T for b in biases], axis=1)),
        "w1": f(np.asarray(L1_gnn_W).T), "b1": f(np.asarray(L1_gnn_b)),
    }
    nc = bacc.Bacc("TRN2", target_bir_lowering=False, num_devices=1)
    args = [nc.dram_tensor(f"in_{k}", a.shape, mybir.dt.from_np(a.dtype), kind="ExternalInput").ap()
            for k, a in arrays.items()]
    out = nc.dram_tensor("y", (NP, H), F32, kind="ExternalOutput").ap()
    build(nc, *args, out)
    r = run_bass_kernel_spmd(nc, [{f"in_{k}": a for k, a in arrays.items()}], core_ids=[0])
    return r.results[0]["y"][:N]
```

```python
import concourse.bass as bass
from concourse import mybir
from concourse.alu_op_type import AluOpType as ALU
from contextlib import ExitStack


N = 3327
P = 128
T = (N + P - 1) // P
NP = T * P
H = 128
HEADS = 3
E2 = 2 * HEADS
EW = 32
COUNT = 3 * E2
ALPHA = 0.2
EPS = 1e-5
FLOOR = 104.0

F32 = mybir.dt.float32
F32R = mybir.dt.float32r
BF16 = mybir.dt.bfloat16
U8 = mybir.dt.uint8
I32 = mybir.dt.int32
ACT = mybir.ActivationFunctionType
AX = mybir.AxisListType.X

HALF = NP // 2
BANK = HALF // 4
CT = 6
CW = CT * P
CHUNKS = T // CT
RT = T - CHUNKS * CT


def slot_before(j, ring, steps):
    if j >= ring:
        return j - ring
    return max(k for k in range(steps) if k % ring == j % ring) - steps


def loads_before(j, ring):
    return j // ring


def loads_per_round(j, ring, steps):
    return len(range(j % ring, steps, ring))


class Tools:

    def __init__(self, nc, ctx):
        self.nc, self.ctx = nc, ctx

    def sb(self, name, shape, dt=F32):
        return self.ctx.enter_context(self.nc.sbuf_tensor(name, shape, dt))

    def ps(self, name, shape, dt=F32):
        return self.ctx.enter_context(self.nc.psum_tensor(name, shape, dt))

    def sem(self, name):
        return self.ctx.enter_context(self.nc.semaphore(name))


def project(nc, keep, d):
    hw, upm, umm, x_hi, x_lo, ident, not_i = (keep[k] for k in ("hw", "up", "um", "x_hi", "x_lo", "ident", "not_i"))
    with ExitStack() as ctx:
        t = Tools(nc, ctx)
        xT = t.sb("a_xT", [P, NP])
        x_sb = t.sb("a_x", [P, T, H])
        wext = t.sb("a_wext", [P, HEADS * H + E2])
        a_row = t.sb("a_arow", [P, E2, H])
        junk = t.sb("a_junk", [P, H])
        u = t.sb("a_u", [P, T, E2])
        part = t.sb("a_part", [P, T, E2], BF16)
        rest = t.sb("a_rest", [P, T, E2])
        pp = [t.ps(f"a_pp{i}", [P, 512]) for i in range(4)]
        x_in, xT_in, w_in, a_in = t.sem("x_in"), t.sem("xT_in"), t.sem("w_in"), t.sem("a_in")
        zeroed, folded, mm, hw_out, u_out, link, made = (
            t.sem(s) for s in ("zeroed", "folded", "mm", "hw_out", "u_out", "link", "made"))
        block = ctx.enter_context(nc.Block())

        @block.sync
        def _(sp):
            sp.dma_start(wext[:, 0:HEADS * H], d["gat_w"]).then_inc(w_in, 16)
            sp.dma_start(xT[:, :], d["xT"]).then_inc(xT_in, 16)
            sp.dma_start(a_row[:, :, :].rearrange("p c f -> p (c f)"), d["gat_a"].partition_broadcast(P)).then_inc(a_in, 16)
            sp.dma_start(x_sb[:, :, :], d["x"]).then_inc(x_in, 16)
            for j, slot in enumerate(keep["at1"]):
                sp.dma_start(slot[:, :], d["adjT"][j * P:(j + 1) * P, 0:HALF]).then_inc(keep["at1_in"][j], 16)

        @block.gpsimd
        def _(pool):
            pool.memset(ident[:, :], 0.0).then_inc(made, 1)
            pool.memset(not_i[:, :], 1.0).then_inc(made, 1)
            pool.wait_ge(made, 2)
            pool.affine_select(out=ident[:, :], in_=ident[:, :], compare_op=ALU.not_equal, fill=1.0,
                               base=0, pattern=[[-1, P]], channel_multiplier=1)
            pool.affine_select(out=not_i[:, :], in_=not_i[:, :], compare_op=ALU.not_equal, fill=0.0,
                               base=0, pattern=[[-1, P]], channel_multiplier=1)

        @block.tensor
        def _(pe):
            pe.wait_ge(w_in, 16)
            pe.wait_ge(folded, E2)
            pe.wait_ge(xT_in, 16)
            for k in range(T):
                if k >= 4:
                    pe.wait_ge(hw_out, k - 3)
                    pe.wait_ge(u_out, k - 3)
                nc.tensor.matmul(pp[k % 4][:, 0:HEADS * H + E2], xT[:, k * P:(k + 1) * P], wext[:, :],
                                 start=True, stop=True).then_inc(mm, 1)

        @block.scalar
        def _(act):
            for k in range(T):
                act.wait_ge(mm, k + 1)
                act.wait_ge(u_out, k + 1)
                nc.scalar.activation(hw[:, k, :], pp[k % 4][:, 0:HEADS * H], ACT.Copy).then_inc(hw_out, 1)

        @block.vector
        def _(dve):
            dve.memset(upm[:, :, :], 0.0).then_inc(zeroed, 1)
            dve.memset(umm[:, :, :], 0.0).then_inc(zeroed, 1)
            dve.wait_ge(w_in, 16)
            dve.wait_ge(a_in, 16)
            for c in range(E2):
                h, side = c % HEADS, c // HEADS
                if c:
                    dve.wait_ge(folded, c)
                dve.tensor_tensor_reduce(out=junk[:, :], in0=wext[:, h * H:(h + 1) * H], in1=a_row[:, 2 * h + side, :],
                                         scale=1.0, scalar=0.0, op0=ALU.mult, op1=ALU.add,
                                         accum_out=wext[:, HEADS * H + c:HEADS * H + c + 1]).then_inc(folded, 1)
            dve.wait_ge(x_in, 16)
            dve.tensor_copy(x_hi[:, :, :], x_sb[:, :, :]).then_inc(link, 1)
            dve.wait_ge(link, 1)
            dve.tensor_tensor(x_lo[:, :, :], x_sb[:, :, :], x_hi[:, :, :].bitcast(F32), ALU.subtract)
            for k in range(T):
                dve.wait_ge(mm, k + 1)
                dve.tensor_copy(u[:, k, :], pp[k % 4][:, HEADS * H:HEADS * H + E2]).then_inc(u_out, 1)
            dve.wait_ge(u_out, T)
            dve.wait_ge(zeroed, 2)
            n = 1

            def then(ins):
                nonlocal n
                n += 1
                ins.then_inc(link, 1)
                dve.wait_ge(link, n)

            def split(dst):
                then(dve.tensor_copy(part[:, :, :], u[:, :, :]))
                then(dve.tensor_copy(dst[:, :, 0:E2], part[:, :, :]))
                then(dve.tensor_tensor(rest[:, :, :], u[:, :, :], part[:, :, :], ALU.subtract))
                then(dve.tensor_copy(part[:, :, :], rest[:, :, :]))
                then(dve.tensor_copy(dst[:, :, E2:2 * E2], part[:, :, :]))
                then(dve.tensor_tensor(rest[:, :, :], rest[:, :, :], part[:, :, :], ALU.subtract))
                then(dve.tensor_copy(dst[:, :, 2 * E2:3 * E2], rest[:, :, :]))

            split(upm)
            then(dve.tensor_tensor(u[:, :, 0:HEADS], u[:, :, 0:HEADS], u[:, :, HEADS:E2], ALU.add))
            then(dve.tensor_copy(u[:, :, HEADS:E2], u[:, :, 0:HEADS]))
            split(umm)
            then(dve.memset(umm[:, :, COUNT:COUNT + 1], 1.0))


def aggregate(nc, keep, d):
    upm, umm, x_hi, x_lo, not_i, csum, ns, elog = (
        keep[k] for k in ("up", "um", "x_hi", "x_lo", "not_i", "csum", "ns", "elog"))
    POOL_COLS = HALF - 224
    at, at_in = keep["at1"], keep["at1_in"]
    RA, RB = len(at), 2
    with ExitStack() as ctx:
        t = Tools(nc, ctx)
        hi = [t.sb(f"b_hi{i}", [P, HALF], F32R) for i in range(RB)]
        lo = [t.sb(f"b_lo{i}", [P, HALF], F32R) for i in range(RB)]
        sg = [t.sb(f"b_sg{i}", [P, HALF], BF16) for i in range(RB)]
        mi = [t.sb(f"b_mi{i}", [P, HALF], BF16) for i in range(RB)]
        acc_ns = [t.ps(f"b_ns{i}", [P, 512]) for i in range(4)]
        acc_e = [t.ps(f"b_e{i}", [P, 512]) for i in range(4)]
        diag_zero, act_done, lo_done, mask_done, sum_done, pe_done, acc_ready, ns_out, e_out = (
            t.sem(s) for s in ("diag_zero", "act_done", "lo_done", "mask_done", "sum_done", "pe_done",
                               "acc_ready", "ns_out", "e_out"))
        hi_done, tail_sum = t.sem("hi_done"), t.sem("tail_sum")
        block = ctx.enter_context(nc.Block())

        @block.sync
        def _(sp):
            for half in range(2):
                for j in range(0 if half else RA, T):
                    before = T * half + slot_before(j, RA, T) + 1 + RA
                    sp.wait_ge(act_done, before)
                    sp.wait_ge(lo_done, before)
                    sp.wait_ge(sum_done, before)
                    sp.dma_start(at[j % RA][:, :], d["adjT"][j * P:(j + 1) * P, half * HALF:(half + 1) * HALF])\
                      .then_inc(at_in[j % RA], 16)

        @block.gpsimd
        def _(pool):
            pool.sem_inc(sum_done, RA)
            for half in range(2):
                for j in range(T):
                    pool.wait_ge(diag_zero, T * half + j + 1)
                    cs = csum[:, half * HALF:half * HALF + POOL_COLS]
                    if j == 0:
                        pool.tensor_copy(cs, at[0][:, 0:POOL_COLS]).then_inc(sum_done, 1)
                    else:
                        pool.wait_ge(sum_done, T * half + j + RA)
                        pool.tensor_tensor(cs, cs, at[j % RA][:, 0:POOL_COLS], ALU.add).then_inc(sum_done, 1)

        @block.scalar
        def _(act):
            act.sem_inc(act_done, RA)
            act.sem_inc(ns_out, 4)

            def prepare(k):
                j = k % T
                act.wait_ge(diag_zero, k + 1)
                act.wait_ge(pe_done, k + 1)
                act.wait_ge(lo_done, k + 1 - RB + RA)
                nc.scalar.activation(hi[k % RB][:, :], at[j % RA][:, :], ACT.Copy).then_inc(hi_done, 1)
                nc.scalar.activation(sg[k % RB][:, :], at[j % RA][:, :], ACT.Sign).then_inc(act_done, 1)

            for half in range(2):
                for k in range(T * half + (half > 0), T * half + T + (half == 0)):
                    prepare(k)
                act.wait_ge(acc_ready, half + 1)
                for q in range(4):
                    at0 = half * HALF + q * BANK
                    nc.scalar.activation(ns[:, at0:at0 + BANK], acc_ns[q][:, 0:BANK], ACT.Copy).then_inc(ns_out, 1)

        @block.vector
        def _(dve):
            dve.sem_inc(lo_done, RA)
            dve.sem_inc(e_out, 4)

            def prepare(k):
                half, j = divmod(k, T)
                dve.wait_ge(at_in[j % RA], 16 * (half * loads_per_round(j, RA, T) + loads_before(j, RA) + 1))
                c = j * P - half * HALF
                if 0 <= c < HALF:
                    dve.tensor_tensor(at[j % RA][:, c:c + P], at[j % RA][:, c:c + P], not_i[:, :], ALU.mult)\
                       .then_inc(diag_zero, 1)
                    dve.wait_ge(diag_zero, k + 1)
                else:
                    dve.sem_inc(diag_zero, 1)
                cs = csum[:, half * HALF + POOL_COLS:(half + 1) * HALF]
                if j == 0:
                    dve.tensor_copy(cs, at[0][:, POOL_COLS:HALF]).then_inc(tail_sum, 1)
                else:
                    dve.wait_ge(tail_sum, k)
                    dve.tensor_tensor(cs, cs, at[j % RA][:, POOL_COLS:HALF], ALU.add).then_inc(tail_sum, 1)
                dve.wait_ge(pe_done, k + 1)
                dve.tensor_scalar(mi[k % RB][:, :], at[j % RA][:, :], 0.0, None, ALU.is_lt).then_inc(mask_done, 1)
                dve.wait_ge(hi_done, k + 1)
                dve.tensor_tensor(lo[k % RB][:, :], at[j % RA][:, :], hi[k % RB][:, :].bitcast(F32), ALU.subtract)\
                   .then_inc(lo_done, 1)

            for half in range(2):
                for k in range(T * half + (half > 0), T * half + T + (half == 0)):
                    prepare(k)
                dve.wait_ge(acc_ready, half + 1)
                for q in range(4):
                    at0 = half * HALF + q * BANK
                    dve.tensor_copy(elog[:, at0:at0 + BANK], acc_e[q][0:EW, 0:BANK]).then_inc(e_out, 1)

        @block.tensor
        def _(pe):
            pe.sem_inc(pe_done, RB)
            with pe.Fori(0, 2) as half:
                for j in range(T):
                    k = T * half + j
                    first, last = j == 0, j == T - 1
                    pe.wait_ge(act_done, k + 1 + RA)
                    for w, m in ((x_hi, hi), (x_lo, hi)):
                        for q in range(4):
                            if first and w is x_hi:
                                pe.wait_ge(ns_out, 4 * half + q + 1)
                            nc.tensor.matmul(acc_ns[q][:, 0:BANK], w[:, j, :], m[j % RB][:, q * BANK:(q + 1) * BANK],
                                             start=first and w is x_hi, stop=False)
                    for q in range(4):
                        if first:
                            pe.wait_ge(e_out, 4 * half + q + 1)
                        nc.tensor.matmul(acc_e[q][0:EW, 0:BANK], upm[:, j, :], sg[j % RB][:, q * BANK:(q + 1) * BANK],
                                         start=first, stop=False)
                    pe.wait_ge(lo_done, k + 1 + RA)
                    pe.wait_ge(mask_done, k + 1)
                    for q in range(4):
                        nc.tensor.matmul(acc_ns[q][:, 0:BANK], x_hi[:, j, :], lo[j % RB][:, q * BANK:(q + 1) * BANK],
                                         start=False, stop=last)
                    for q in range(4):
                        mm = nc.tensor.matmul(acc_e[q][0:EW, 0:BANK], umm[:, j, :], mi[j % RB][:, q * BANK:(q + 1) * BANK],
                                              start=False, stop=last)
                    mm.then_inc(pe_done, 1)
                pe.wait_ge(pe_done, T * half + T + RB)
                pe.sem_inc(acc_ready, 1)


def logits(nc, keep, d):
    csum, elog, ecol, flag, dinv, diag, diag1, ident = (
        keep[k] for k in ("csum", "elog", "ecol", "flag", "dinv", "diag", "diag1", "ident"))
    CW7 = E2 + 1
    SUMS = [range(0, 20), range(20, T)]
    with ExitStack() as ctx:
        t = Tools(nc, ctx)
        part = t.sb("c_part", [P, T, EW])
        raw = t.sb("c_raw", [P, T, E2])
        e = t.sb("c_e", [P, T, E2])
        red = t.sb("c_red", [P, CW7])
        redg = t.sb("c_redg", [P, CW7])
        shift = t.sb("c_shift", [P, E2])
        erow = t.sb("c_erow", [HEADS * T, 2, P])
        deg = t.sb("c_deg", [P, T])
        root = t.sb("c_root", [P, T])
        safe = t.sb("c_safe", [P, T])
        quot = t.sb("c_quot", [P, T])
        some = t.sb("c_some", [P, T])
        p_e = t.ps("c_pe", [P, 2, 16, EW])
        p_d = t.ps("c_pd", [P, 20, P])
        p_t = t.ps("c_pt", [HEADS * T, 2, P])
        (e_turned, sums_turned, sums_read, link, reduced, everywhere, shifted, turned, copied, saved, deg_made,
         rooted, diag_in) = (
            t.sem(s) for s in ("e_turned", "sums_turned", "sums_read", "link", "reduced", "everywhere", "shifted",
                               "turned", "copied", "e_saved", "deg_made", "rooted", "diag_in"))
        block = ctx.enter_context(nc.Block())

        @block.sync
        def _(sp):
            sp.dma_start(diag[:, :], d["diag"]).then_inc(diag_in, 16)
            sp.dma_start(d["ns"], keep["ns"][:, :]).then_inc(saved, 16)
            sp.wait_ge(copied, 1)
            sp.dma_start(d["e_rows"].rearrange("s (c p) -> c s p", p=P), erow[:, :, :]).then_inc(saved, 16)
            sp.wait_ge(saved, 32)

        @block.tensor
        def _(pe):
            for k in range(T):
                m = nc.tensor.transpose(p_e[:, k // 16, k % 16, :], elog[0:EW, k * P:(k + 1) * P], ident[0:EW, 0:EW])
            m.then_inc(e_turned, 1)
            for k in SUMS[0]:
                m = nc.tensor.transpose(p_d[:, k, :], csum[:, k * P:(k + 1) * P], ident[:, :])
            m.then_inc(sums_turned, 1)
            pe.wait_ge(shifted, 1)
            for s in range(2):
                m = nc.tensor.transpose(p_t[:, s, :], ecol[:, s * HEADS * T:(s + 1) * HEADS * T], ident[:, :])
            m.then_inc(turned, 1)
            pe.wait_ge(sums_read, 1)
            for k in SUMS[1]:
                m = nc.tensor.transpose(p_d[:, k - SUMS[1][0], :], csum[:, k * P:(k + 1) * P], ident[:, :])
            m.then_inc(sums_turned, 1)

        @block.scalar
        def _(act):
            act.wait_ge(deg_made, 1)
            nc.scalar.activation(root[:, :], deg[:, :], ACT.Sqrt).then_inc(rooted, 1)

        @block.gpsimd
        def _(pool):
            pool.wait_ge(reduced, 1)
            pool.partition_all_reduce(redg[:, :], red[:, :], P, bass.bass_isa.ReduceOp.max).then_inc(everywhere, 1)

        @block.vector
        def _(dve):
            n = 0

            def then(ins):
                nonlocal n
                n += 1
                ins.then_inc(link, 1)
                dve.wait_ge(link, n)

            dve.wait_ge(e_turned, 1)
            dve.tensor_copy(part[:, 0:16, :], p_e[:, 0, :, :])
            then(dve.tensor_copy(part[:, 16:T, :], p_e[:, 1, 0:T - 16, :]))
            then(dve.tensor_tensor(raw[:, :, :], part[:, :, 0:E2], part[:, :, E2:2 * E2], ALU.add))
            then(dve.tensor_tensor(raw[:, :, :], raw[:, :, :], part[:, :, 2 * E2:3 * E2], ALU.add))
            then(dve.scalar_tensor_tensor(e[:, :, :], raw[:, :, :], ALPHA, raw[:, :, :], ALU.mult, ALU.max))
            then(dve.tensor_reduce(red[:, 0:E2], e[:, :, :].rearrange("p t c -> p c t"), AX, ALU.min))
            then(dve.tensor_scalar(red[:, 0:E2], red[:, 0:E2], -1.0, None, ALU.mult))
            dve.tensor_reduce(red[:, E2:CW7], part[:, :, COUNT:COUNT + 1].rearrange("p t c -> p c t"), AX, ALU.add)\
               .then_inc(reduced, 1)
            dve.wait_ge(everywhere, 1)
            then(dve.tensor_tensor(shift[:, 0:HEADS], redg[:, 0:HEADS], redg[:, HEADS:E2], ALU.max))
            then(dve.tensor_scalar(shift[:, 0:HEADS], shift[:, 0:HEADS], FLOOR, None, ALU.add))
            then(dve.tensor_copy(shift[:, HEADS:E2], shift[:, 0:HEADS]))
            dve.tensor_tensor(ecol[:, :].rearrange("p (c t) -> p c t", t=T), e[:, :, :].rearrange("p t c -> p c t"),
                              shift[:, :].unsqueeze(2).broadcast_to([P, E2, T]), ALU.add).then_inc(shifted, 1)
            dve.tensor_copy(flag[:, :], redg[:, E2:CW7])
            dve.wait_ge(turned, 1)
            dve.tensor_copy(erow[:, :, :], p_t[:, :, :]).then_inc(copied, 1)
            for g, ks in enumerate(SUMS):
                dve.wait_ge(sums_turned, g + 1)
                dve.tensor_reduce(deg[:, ks[0]:ks[-1] + 1], p_d[:, 0:len(ks), :], AX, ALU.add).then_inc(sums_read, 1)
            dve.wait_ge(sums_read, 2)
            dve.wait_ge(diag_in, 16)
            then(dve.tensor_scalar(diag1[:, :], diag[:, :], 1.0, None, ALU.add))
            dve.tensor_tensor(deg[:, :], deg[:, :], diag1[:, :], ALU.add).then_inc(deg_made, 1)
            dve.wait_ge(deg_made, 1)
            dve.wait_ge(rooted, 1)
            then(dve.tensor_scalar(safe[:, :], root[:, :], 1e-30, None, ALU.max))
            then(dve.reciprocal(quot[:, :], safe[:, :]))
            then(dve.tensor_tensor(quot[:, :], quot[:, :], deg[:, :], ALU.mult))
            then(dve.tensor_tensor(safe[:, :], safe[:, :], quot[:, :], ALU.add))
            then(dve.tensor_scalar(safe[:, :], safe[:, :], 0.5, None, ALU.mult))
            then(dve.reciprocal(quot[:, :], safe[:, :]))
            then(dve.tensor_scalar(some[:, :], deg[:, :], 0.0, None, ALU.not_equal))
            then(dve.tensor_tensor(quot[:, :], quot[:, :], some[:, :], ALU.mult))
            then(dve.tensor_scalar(root[:, :], root[:, :], 0.0, None, ALU.mult))
            dve.tensor_tensor(dinv[:, :], quot[:, :], root[:, :], ALU.add)


def attend(nc, keep, d):
    hw, ecol, ident, not_i = (keep[k] for k in ("hw", "ecol", "ident", "not_i"))
    RA, RE, RW = 4, 6, 6
    CREDIT = 16
    HW = CW // 2
    NU = HEADS * T
    ROWS = HEADS * CT
    LAST = CHUNKS
    UNITS = [(j, h) for j in range(T) for h in range(HEADS)]
    DVE_FIRST = [(j, HEADS - 1) for j in (19, 20)]
    DVE_BUSY = [(j, HEADS - 1) for j in (6, 10, 13, 17, 19, 20)]
    DVE_FREE = [(j, HEADS - 1) for j in range(T - 2)]
    ROW_END = 18
    OWN_MASKS = 2
    TAIL = {20: 0, 21: 1, 22: 2, 24: 3}
    BODY = {0: 4, 1: 5, 3: 6, 4: 7, 5: 8, 7: 9, 8: 10, 9: 11, 11: 12, 12: 13, 13: 14, 15: 15, 16: 16, 17: 17}
    BODY0 = {r + r // 6 - 1: r for r in range(ROWS)}
    INV_SEND, MAX_SEND, TAKE_LAG = (0, 1, 2, 3, 4, 5), (10, 11, 12, 19, 20, 21), 3
    with ExitStack() as ctx:
        t = Tools(nc, ctx)
        erow = t.sb("d_erow", [P, HEADS, NP])
        arow = [t.sb(f"d_arow{i}", [P, HALF]) for i in range(2)]
        ones_not_i = t.sb("d_ones_not_i", [P, 2 * CHUNKS - 1, P], BF16)
        mask = t.sb("d_mask", [P, NP], U8)
        L = [t.sb(f"d_l{i}", [P, NP]) for i in range(2)]
        mx = t.sb("d_mx", [P, ROWS])
        scratch = t.sb("d_scratch", [P, 1])
        nm = t.sb("d_nm", [P, ROWS])
        den = t.sb("d_den", [P, ROWS])
        rden = t.sb("d_rden", [P, ROWS])
        nmb = t.sb("d_nmb", [P, 2, HEADS, CW])
        invb = t.sb("d_invb", [P, HEADS, CW])
        at = [t.sb(f"d_at{i}", [P, CW]) for i in range(RA)]
        ex = [t.sb(f"d_ex{i}", [P, CW]) for i in range(RE)]
        W = [t.sb(f"d_w{i}", [P, CW]) for i in range(RW)]
        es = t.sb("d_es", [P, CW])
        es2 = t.sb("d_es2", [P, CW])
        acc = [t.ps(f"d_acc{h}", [P, 2, 512]) for h in range(HEADS)]
        aux = [t.ps(f"d_aux{i}", [P, 512]) for i in range(2)]
        at_in = [t.sem(f"at_in{i}") for i in range(RA)]
        mask2 = nmb[:, 1, :, :].rearrange("p h n -> p (h n)")[:, 0:NP // 4].bitcast(U8)
        erow_in = [t.sem(f"erow_in{h}") for h in range(HEADS)]
        arow_read = [t.sem(f"arow_read{i}") for i in range(2)]
        arow_in = [t.sem(f"arow_in{i}") for i in range(2)]
        (mask_whole, logit_made, nm_made, row_exp, sums_inverted, spread, spread_out) = (
            t.sem(s) for s in ("mask_whole", "logit_made", "nm_made", "row_exp",
                               "sums_inverted", "spread", "spread_out"))
        (diag_zero, table_made, first_seen, spread_seen, arg_made, exp_made, w_dve, w_pool, unit_done, acc_free, es_added,
         es_made, es_saved) = (
            t.sem(s) for s in ("diag_zero", "table_made", "first_seen", "spread_seen", "arg_made", "exp_made", "w_dve", "w_pool",
                               "unit_done", "acc_free", "es_added", "es_made", "es_saved"))
        block = ctx.enter_context(nc.Block())

        def is_last(q):
            return isinstance(q, int) and q == LAST

        def tiles(q):
            return RT if is_last(q) else CT

        def width(q):
            return tiles(q) * P

        def on_dve(q):
            if isinstance(q, int) and q == 0:
                return DVE_FIRST
            return DVE_FREE if isinstance(q, int) and q >= LAST - 1 else DVE_BUSY

        def on_pool(q):
            return [u for u in UNITS if u not in on_dve(q)]

        def made_before(q, on):
            if isinstance(q, int) and q == 0:
                return 0
            if is_last(q):
                return made_before(LAST - 1, on) + len(on(LAST - 1))
            return len(on(1)) * q + len(on(0)) - len(on(1))

        def wait_weights(eng, q, j, h):
            if j < 0:
                eng.wait_ge(w_pool, made_before(q, on_pool) - (HEADS * (-j) - h) + 1 + CREDIT)
            elif (j, h) in on_dve(q):
                eng.wait_ge(w_dve, made_before(q, on_dve) + on_dve(q).index((j, h)) + 1 + CREDIT)
            else:
                eng.wait_ge(w_pool, made_before(q, on_pool) + on_pool(q).index((j, h)) + 1 + CREDIT)

        def rows_at(q, j):
            rows = []
            body = BODY0 if isinstance(q, int) and q == 0 else BODY
            if j in body and not is_last(q):
                c = q + 1
                if body[j] < HEADS * tiles(c):
                    rows.append((c, body[j]))
            if j in TAIL and not (isinstance(q, int) and q >= LAST - 1):
                rows.append((q + 2, TAIL[j]))
            return rows

        def masks_at(q, j):
            return [(c, r // HEADS) for c, r in rows_at(q, j + 1) if r % HEADS == 0]

        PIECES = [(h, a, CT // 2) for a in range(0, CT, CT // 2) for h in range(HEADS)]
        PIECES_LAST = [(h, 0, RT) for h in range(HEADS)]

        def pieces(q):
            return PIECES_LAST if is_last(q) else PIECES

        def turn(q, i, src):
            n = len(PIECES)
            if src is nm:
                return 2 * n * q + i
            return 2 * n * q + i + len(pieces(q))

        def bank(q, i, src):
            return turn(LAST if is_last(q) else 0, i, src) % 2

        def make_mask(eng, mask, c, k):
            n = c * CT + k
            for half in range(2):
                eng.wait_ge(arow_in[half], 16 * n + 16)
                eng.tensor_scalar(mask[:, half * HALF:(half + 1) * HALF], arow[half][:, :], 0.0, None, ALU.is_gt)\
                   .then_inc(arow_read[half], 1)

        def each_chunk(eng, step):
            step(0)
            with eng.Fori(1, LAST - 1) as q:
                step(q)
            step(LAST - 1)
            step(LAST)

        @block.sync
        def _(sp):
            def row_tile(c, k):
                r0 = (c * CT + k) * P
                if not isinstance(r0, int):
                    r0 = sp.snap(r0)
                for half in range(2):
                    sp.wait_ge(arow_read[half], c * CT + k + CREDIT)
                    sp.dma_start(arow[half][:, :], d["adj"][bass.ds(r0, P), half * HALF:(half + 1) * HALF])\
                      .then_inc(arow_in[half], 16)

            def save(q):
                col0 = q * CW
                if not isinstance(col0, int):
                    col0 = sp.snap(col0)
                sp.wait_ge(es_made, q + 1)
                sp.dma_start(d["es"][:, bass.ds(col0, width(q))], es[:, 0:width(q)]).then_inc(es_saved, 16)

            def chunk(q):
                w = width(q)
                col0 = q * CW
                if not isinstance(col0, int):
                    col0 = sp.snap(col0)
                for j in range(T):
                    sp.wait_ge(unit_done, NU * q + HEADS * slot_before(j, RA, T) + HEADS + CREDIT)
                    sp.dma_start(at[j % RA][:, 0:w], d["adjT"][j * P:(j + 1) * P, bass.ds(col0, w)])\
                      .then_inc(at_in[j % RA], 16)
                    for c, k in masks_at(q, j):
                        row_tile(c, k)
                    if j == 6 and not (isinstance(q, int) and q == 0):
                        save(q - 1)

            for k in range(CT):
                row_tile(0, k)
                if k == 0:
                    for h in range(HEADS):
                        sp.dma_start(erow[:, h, :], d["e_rows"][0, h * NP:(h + 1) * NP].partition_broadcast(P))\
                          .then_inc(erow_in[h], 16)
            row_tile(1, 0)
            each_chunk(sp, chunk)
            save(LAST)
            sp.wait_ge(es_saved, 16 * (LAST + 1))

        @block.gpsimd
        def _(pool):
            pool.sem_inc(w_pool, CREDIT)
            pool.memset(ones_not_i[:, :, :], 1.0).then_inc(table_made, 1)
            pool.wait_ge(table_made, 1)
            pool.tensor_copy(ones_not_i[:, CHUNKS - 1, :], not_i[:, :]).then_inc(table_made, 1)
            pool.wait_ge(table_made, 2)

            def arrived(q, j):
                pool.wait_ge(at_in[j % RA], 16 * (q * loads_per_round(j, RA, T) + loads_before(j, RA) + 1))

            def zero_diagonal(q, j):
                c = slice(j % CT * P, (j % CT + 1) * P)
                a = at[j % RA]
                if isinstance(q, int):
                    if q == j // CT:
                        pool.tensor_tensor(a[:, c], a[:, c], not_i[:, :], ALU.mult).then_inc(diag_zero, 1)
                        return
                elif j // CT < LAST:
                    which = ones_not_i[:, bass.ds(q - j // CT + CHUNKS - 1, 1), :]
                    pool.tensor_tensor(a[:, c], a[:, c], which.rearrange("p a n -> p (a n)"), ALU.mult)\
                        .then_inc(diag_zero, 1)
                    return
                pool.sem_inc(diag_zero, 1)

            def chunk(q):
                w = width(q)
                for j, h in on_pool(q):
                    u = HEADS * j + h
                    ends_step = (j, h + 1) not in on_pool(q)
                    if ends_step and j + 1 < T:
                        arrived(q, j + 1)
                    pool.wait_ge(diag_zero, T * q + j + 1)
                    pool.wait_ge(exp_made, NU * q + u + 1)
                    pool.wait_ge(unit_done, NU * q + u - RW + 1 + CREDIT)
                    pool.tensor_tensor(W[u % RW][:, 0:w], ex[u % RE][:, 0:w], at[j % RA][:, 0:w], ALU.mult)\
                        .then_inc(w_pool, 1)
                    if ends_step and j + 1 < T:
                        zero_diagonal(q, j + 1)
                    elif ends_step and not is_last(q):
                        arrived(q + 1, 0)
                        pool.sem_inc(first_seen, 1)
                        zero_diagonal(q + 1, 0)

            for k in range(OWN_MASKS, CT):
                if k >= 2:
                    pool.wait_ge(logit_made, HEADS * (k - 1) + CREDIT)
                make_mask(pool, mask if k % 2 == 0 else mask2, 0, k)
            arrived(0, 0)
            zero_diagonal(0, 0)
            each_chunk(pool, chunk)

        @block.scalar
        def _(act):
            act.sem_inc(row_exp, CREDIT)

            def row_unit(c, r):
                k, h = divmod(r, HEADS)
                s = h * CT + k
                act.wait_ge(nm_made, ROWS * c + r + 1)
                nc.scalar.activation(L[r % 2][:, :], L[r % 2][:, :], ACT.Exp, bias=nm[:, s:s + 1],
                                     accum_out=den[:, s:s + 1]).then_inc(row_exp, 1)

            def take(q, i, src):
                h, a, n = pieces(q)[i]
                act.wait_ge(spread, turn(q, i, src) + 1)
                cols = slice(a * P, (a + n) * P)
                if src is nm:
                    act.sem_inc(spread_seen, 1)
                    out = nmb[:, bass.ds(q & 1, 1), h, cols].rearrange("p a n -> p (a n)")
                else:
                    if i == 0 and not (isinstance(q, int) and q == 0):
                        act.wait_ge(es_made, q)
                    out = invb[:, h, cols]
                nc.scalar.activation(out, aux[bank(q, i, src)][:, 0:n * P], ACT.Copy).then_inc(spread_out, 1)

            def chunk(q):
                w = width(q)
                for j in range(T):
                    for h in range(HEADS):
                        u = HEADS * j + h
                        act.wait_ge(arg_made, NU * q + u + 1)
                        nc.scalar.activation(ex[u % RE][:, 0:w], ex[u % RE][:, 0:w], ACT.Exp).then_inc(exp_made, 1)
                    for i, step in enumerate(INV_SEND[:len(pieces(q))]):
                        if step + TAKE_LAG == j:
                            take(q, i, rden)
                    if not is_last(q):
                        for i, step in enumerate(MAX_SEND[:len(pieces(q + 1))]):
                            if step + TAKE_LAG == j:
                                take(q + 1, i, nm)
                    for c, r in rows_at(q, j - 1):
                        row_unit(c, r)

            for r in range(ROWS):
                row_unit(0, r)
                if r == HEADS * CT // 2 + HEADS:
                    for i in range(HEADS):
                        take(0, i, nm)
            for i in range(HEADS, len(PIECES)):
                take(0, i, nm)
            each_chunk(act, chunk)

        @block.vector
        def _(dve):
            dve.sem_inc(logit_made, CREDIT)
            for half in range(2):
                dve.sem_inc(arow_read[half], CREDIT)
            dve.sem_inc(w_dve, CREDIT)
            dve.sem_inc(acc_free, HEADS)

            def mask_tile(c, k, mask=mask):
                n = c * CT + k
                if not (isinstance(c, int) and c == 0 and k >= OWN_MASKS):
                    make_mask(dve, mask, c, k)
                for half in range(2):
                    dve.wait_ge(arow_read[half], n + 1 + CREDIT)
                own = bass.ds(n * P, P)
                dve.tensor_tensor(mask[:, own], mask[:, own], not_i[:, :], ALU.mult).then_inc(mask_whole, 1)

            def row_unit(c, r, mask=mask):
                u = ROWS * c + r
                k, h = divmod(r, HEADS)
                s = h * CT + k
                if h == 0:
                    dve.wait_ge(mask_whole, c * CT + k + 1)
                dve.wait_ge(row_exp, u - 1 + CREDIT)
                dve.memset(scratch[:, :], 0.0)
                dve.wait_ge(erow_in[h], 16)
                dve.tensor_tensor_reduce(out=L[r % 2][:, :], in0=mask[:, :], in1=erow[:, h, :], scale=1.0,
                                         scalar=0.0, op0=ALU.mult, op1=ALU.max,
                                         accum_out=mx[:, s:s + 1]).then_inc(logit_made, 1)
                dve.wait_ge(logit_made, u + 1 + CREDIT)
                dve.tensor_scalar(nm[:, s:s + 1], mx[:, s:s + 1], -1.0, None, ALU.mult).then_inc(nm_made, 1)

            def invert(q):
                dve.wait_ge(row_exp, ROWS * q + HEADS * tiles(q) + CREDIT)
                dve.reciprocal(rden[:, :], den[:, :]).then_inc(sums_inverted, 1)
                dve.wait_ge(sums_inverted, 2 * q + 1)
                dve.tensor_scalar(rden[:, :], rden[:, :], 1.0 / HEADS, None, ALU.mult).then_inc(sums_inverted, 1)
                dve.wait_ge(sums_inverted, 2 * q + 2)

            def args(q, j):
                if j == 0:
                    dve.wait_ge(spread_out, turn(q, len(pieces(q)), nm))
                for h in range(HEADS):
                    u = HEADS * j + h
                    wait_weights(dve, q, j - 2, h)
                    dve.tensor_scalar(ex[u % RE][:, 0:width(q)],
                                      nmb[:, bass.ds(q & 1, 1), h, 0:width(q)].rearrange("p a n -> p (a n)"),
                                      ecol[:, h * T + j:h * T + j + 1], 0.0, ALU.add, ALU.min).then_inc(arg_made, 1)

            def finish(q):
                w = width(q)
                wb = min(w, HW)
                if not (isinstance(q, int) and q == 0):
                    dve.wait_ge(es_saved, 16 * q)
                dve.wait_ge(spread_out, turn(q, len(pieces(q)), rden))
                for h in range(HEADS):
                    dve.wait_ge(unit_done, NU * q + NU - HEADS + h + 1 + CREDIT)
                    a = acc[h][:, 0:w // wb, 0:wb]
                    i = invb[:, h, 0:w].rearrange("p (b n) -> p b n", n=wb)
                    o = (es if h == 0 else es2)[:, 0:w].rearrange("p (b n) -> p b n", n=wb)
                    dve.tensor_tensor(o, a, i, ALU.mult).then_inc(acc_free, 1)
                    dve.wait_ge(acc_free, HEADS * q + h + 1 + HEADS)
                    if h:
                        last = dve.tensor_tensor(es[:, 0:w], es[:, 0:w], es2[:, 0:w], ALU.add)
                        last.then_inc(es_added if h < HEADS - 1 else es_made, 1)
                        if h < HEADS - 1:
                            dve.wait_ge(es_added, q + 1)

            def chunk(q):
                w = width(q)
                for j in range(T):
                    if j + 1 < T:
                        args(q, j + 1)
                    elif not is_last(q):
                        args(q + 1, 0)
                    for h in range(HEADS):
                        if (j, h) not in on_dve(q):
                            continue
                        u = HEADS * j + h
                        dve.wait_ge(diag_zero, T * q + j + 1)
                        dve.wait_ge(exp_made, NU * q + u + 1)
                        dve.wait_ge(unit_done, NU * q + u - RW + 1 + CREDIT)
                        dve.tensor_tensor(W[u % RW][:, 0:w], ex[u % RE][:, 0:w], at[j % RA][:, 0:w], ALU.mult)\
                           .then_inc(w_dve, 1)
                    if j == 0 and not (isinstance(q, int) and q == 0):
                        finish(q - 1)
                    if not is_last(q) and j == ROW_END + 2:
                        invert(q + 1)
                    for c, r in rows_at(q, j):
                        row_unit(c, r)
                    for c, k in masks_at(q, j):
                        mask_tile(c, k)

            for r in range(ROWS):
                slot = mask if r // HEADS % 2 == 0 else mask2
                if r % HEADS == 0:
                    mask_tile(0, r // HEADS, slot)
                row_unit(0, r, slot)
            mask_tile(1, 0)
            invert(0)
            dve.wait_ge(spread_out, HEADS)
            args(0, 0)
            row_unit(1, 0)
            each_chunk(dve, chunk)
            finish(LAST)

        @block.tensor
        def _(pe):
            pe.sem_inc(unit_done, CREDIT)

            def send(q, i, src):
                h, a, n = pieces(q)[i]
                if src is nm:
                    pe.wait_ge(nm_made, ROWS * q + HEADS * (a + n))
                else:
                    pe.wait_ge(sums_inverted, 2 * q + 2)
                if not (isinstance(q, int) and q == 0 and src is nm and i < 2):
                    pe.wait_ge(spread_out, turn(q, i, src) - 1)
                for k in range(a, a + n):
                    s = h * CT + k
                    m = nc.tensor.matmul(aux[bank(q, i, src)][:, (k - a) * P:(k - a + 1) * P],
                                         src[:, s:s + 1].to_broadcast([P, P]), ident[:, :], start=True, stop=True)
                m.then_inc(spread, 1)

            def chunk(q):
                w = width(q)
                for j in range(T):
                    for h in range(HEADS):
                        if j == 0:
                            pe.wait_ge(acc_free, HEADS * q + h + 1)
                        wait_weights(pe, q, j, h)
                        for b in range(0, w, HW):
                            n = min(HW, w - b)
                            m = nc.tensor.matmul(acc[h][:, b // HW, 0:n], hw[:, j, h * H:(h + 1) * H],
                                                 W[(HEADS * j + h) % RW][:, b:b + n], start=(j == 0), stop=(j == T - 1))
                        m.then_inc(unit_done, 1)
                    for i, step in enumerate(INV_SEND[:len(pieces(q))]):
                        if step == j:
                            send(q, i, rden)
                    if not is_last(q):
                        for i, step in enumerate(MAX_SEND[:len(pieces(q + 1))]):
                            if step == j:
                                send(q + 1, i, nm)

            for i in range(len(PIECES)):
                send(0, i, nm)
            each_chunk(pe, chunk)


def attend_signed(nc, keep, d):
    hw, ident, not_i, flag = (keep[k] for k in ("hw", "ident", "not_i", "flag"))
    GROUPS = [list(range(g, min(g + 4, T))) for g in range(0, T, 4)]
    NG = len(GROUPS)
    with ExitStack() as ctx:
        t = Tools(nc, ctx)
        arow = t.sb("g_arow", [P, NP])
        plus = t.sb("g_plus", [P, NP])
        minus = t.sb("g_minus", [P, NP])
        L = t.sb("g_l", [P, NP])
        W = t.sb("g_w", [P, NP])
        wt = t.sb("g_wt", [P, 512])
        mx, nm, den, rden = (t.sb(f"g_{s}", [P, 1]) for s in ("mx", "nm", "den", "rden"))
        est = t.sb("g_est", [P, P])
        turn = t.ps("g_turn", [P, 512])
        acc = t.ps("g_acc", [P, P])
        (a_in, e_in, diag_zero, logit, prob, weight, turned, copied, multiplied, est_made, est_saved, est_seen, link) = (
            t.sem(s) for s in ("g_a_in", "g_e_in", "g_diag", "g_logit", "g_prob", "g_weight", "g_turned", "g_copied",
                               "g_multiplied", "g_est_made", "g_est_saved", "g_est_seen", "g_link"))
        block = ctx.enter_context(nc.Block())

        def when_signed(eng, program, credits=(), end=lambda: None):
            negative = eng.value_load(flag[0:1, 0:1], min_val=0, max_val=1 << 24)
            with eng.If(negative > 0):
                for counter, n in credits:
                    eng.sem_inc(counter, n)
                with eng.Fori(0, T) as i:
                    program(i)
                end()

        @block.sync
        def _(sp):
            def tile(i):
                at_tile = sp.snap(i * P)
                sp.wait_ge(weight, HEADS * i + 1)
                sp.dma_start(arow[:, :], d["adj"][bass.ds(at_tile, P), :]).then_inc(a_in, 16)
                for h in range(HEADS):
                    sp.wait_ge(weight, HEADS * i + h + 1)
                    sp.dma_start(plus[:, :], d["e_rows"][0, h * NP:(h + 1) * NP].partition_broadcast(P)).then_inc(e_in, 16)
                    sp.dma_start(minus[:, :], d["e_rows"][1, h * NP:(h + 1) * NP].partition_broadcast(P)).then_inc(e_in, 16)
                sp.wait_ge(est_made, i + 2)
                sp.sem_inc(est_seen, 1)
                sp.dma_start(d["es"][:, bass.ds(at_tile, P)], est[:, :]).then_inc(est_saved, 16)
            when_signed(sp, tile, [(est_saved, 16)], lambda: sp.wait_ge(est_saved, 16 * T + 16))

        @block.scalar
        def _(act):
            def tile(i):
                for h in range(HEADS):
                    act.wait_ge(logit, HEADS * i + h + 1)
                    nc.scalar.activation(L[:, :], L[:, :], ACT.Exp, bias=nm[:, :], accum_out=den[:, :]).then_inc(prob, 1)
                    for g, group in enumerate(GROUPS):
                        n = NG * (HEADS * i + h) + g
                        act.wait_ge(turned, n + 1)
                        act.wait_ge(multiplied, n + 1)
                        nc.scalar.activation(wt[:, 0:len(group) * P], turn[:, 0:len(group) * P], ACT.Copy).then_inc(copied, 1)
            when_signed(act, tile, [(copied, 1)])

        @block.vector
        def _(dve):
            def tile(i):
                dve.wait_ge(a_in, 16 * i + 16)
                c = bass.ds(i * P, P)
                dve.tensor_tensor(arow[:, c], arow[:, c], not_i[:, :], ALU.mult).then_inc(diag_zero, 1)
                dve.wait_ge(diag_zero, i + 1)
                for h in range(HEADS):
                    u = HEADS * i + h
                    n = 0

                    def then(ins):
                        nonlocal n
                        n += 1
                        ins.then_inc(link, 1)
                        dve.wait_ge(link, 6 * u + n)

                    dve.wait_ge(e_in, 32 * u + 32)
                    then(dve.scalar_tensor_tensor(plus[:, :], arow[:, :], 0.0, plus[:, :], ALU.is_gt, ALU.mult))
                    then(dve.scalar_tensor_tensor(minus[:, :], arow[:, :], 0.0, minus[:, :], ALU.is_lt, ALU.mult))
                    then(dve.tensor_tensor(L[:, :], plus[:, :], minus[:, :], ALU.add))
                    then(dve.tensor_reduce(mx[:, :], L[:, :], AX, ALU.max))
                    dve.tensor_scalar(nm[:, :], mx[:, :], -1.0, None, ALU.mult).then_inc(logit, 1)
                    dve.wait_ge(prob, u + 1)
                    then(dve.reciprocal(rden[:, :], den[:, :]))
                    then(dve.tensor_scalar(rden[:, :], rden[:, :], 1.0 / HEADS, None, ALU.mult))
                    dve.wait_ge(multiplied, NG * u + 1)
                    dve.scalar_tensor_tensor(W[:, :], L[:, :], rden[:, :], arow[:, :], ALU.mult, ALU.mult)\
                       .then_inc(weight, 1)
                dve.wait_ge(multiplied, NG * HEADS * i + NG * HEADS + 1)
                dve.wait_ge(est_saved, 16 * i + 16)
                dve.tensor_copy(est[:, :], acc[:, :]).then_inc(est_made, 1)
            when_signed(dve, tile, [(weight, 1), (est_made, 1)])

        @block.tensor
        def _(pe):
            def tile(i):
                pe.wait_ge(est_made, i + 1)
                for h in range(HEADS):
                    pe.wait_ge(weight, HEADS * i + h + 2)
                    for g, group in enumerate(GROUPS):
                        n = NG * (HEADS * i + h) + g
                        pe.wait_ge(copied, n + 1)
                        for s, j in enumerate(group):
                            m = nc.tensor.transpose(turn[:, s * P:(s + 1) * P], W[:, j * P:(j + 1) * P], ident[:, :])
                        m.then_inc(turned, 1)
                        pe.wait_ge(copied, n + 2)
                        for s, j in enumerate(group):
                            m = nc.tensor.matmul(acc[:, :], hw[:, j, h * H:(h + 1) * H], wt[:, s * P:(s + 1) * P],
                                                 start=(h == 0 and j == 0), stop=(h == HEADS - 1 and j == T - 1))
                        m.then_inc(multiplied, 1)
            when_signed(pe, tile, [(multiplied, 1)])


def gru(nc, keep, d):
    go = keep["go"]
    CHUNK = BANK
    NC = NP // CHUNK
    PARTS = [(0, 2), (2, NC)]
    with ExitStack() as ctx:
        t = Tools(nc, ctx)
        xT = keep["at"][4][:, :]
        ns, es = (keep[k][:, :, :].rearrange("p t f -> p (t f)") for k in ("v", "x1"))
        X, NS, ES = range(3)
        w = t.sb("e_w", [P, 4, 3 * H])
        w_hi = t.sb("e_whi", [P, 4, 3 * H], F32R)
        w_lo = t.sb("e_wlo", [P, 4, 3 * H], F32R)
        in_hi = t.sb("e_ihi", [P, 2, 3, CHUNK], F32R)
        in_lo = t.sb("e_ilo", [P, 2, 3, CHUNK], F32R)
        bias = t.sb("e_b", [P, 4, 3])
        brz = t.sb("e_brz", [P, 2, 2])
        r, z, pre, cand = ([keep["at"][5][:, (2 * i + g) * CHUNK:(2 * i + g + 1) * CHUNK] for g in range(2)]
                           for i in range(4))
        diff = [t.sb(f"e_diff{g}", [P, CHUNK]) for g in range(2)]
        ps = [[t.ps(f"e_p{g}{i}", [P, 512]) for i in range(4)] for g in range(2)]
        w_in = t.sem("w_in")
        rows_in = [t.sem(f"rows_in{part}") for part in range(len(PARTS))]
        w_split, slot_seen, hi_made, hi_seen, lo_made = (
            t.sem(s) for s in ("w_split", "slot_seen", "hi_made", "hi_seen", "lo_made"))
        gates, sig, pre_made, cand_made, cell_done, link, bias_made = (
            t.sem(s) for s in ("gates", "sig", "pre_made", "cand_made", "cell_done", "link", "bias_made"))
        block = ctx.enter_context(nc.Block())
        R, Z, NI, NH = range(4)

        @block.sync
        def _(sp):
            sp.dma_start(bias[:, :, :], d["gru_b"]).then_inc(w_in, 16)
            sp.dma_start(w[:, :, :], d["gru_w"]).then_inc(w_in, 16)
            for part, (a, b) in enumerate(PARTS):
                cols = slice(a * CHUNK, b * CHUNK)
                for dst, src in ((xT, "xT"), (ns, "ns"), (es, "es")):
                    sp.dma_start(dst[:, cols], d[src][:, cols]).then_inc(rows_in[part], 16)
            sp.dma_start(keep["x"][:, :, :], d["x"]).then_inc(keep["x_in"], 16)
            sp.dma_start(keep["w1"][:, :], d["w1"]).then_inc(keep["w1_in"], 16)
            sp.dma_start(keep["b1"][:, :], d["b1"].partition_broadcast(P)).then_inc(keep["b1_in"], 16)
            for j, slot in enumerate(keep["at"][:EARLY]):
                sp.dma_start(slot[:, :], d["adjT"][j * P:(j + 1) * P, :]).then_inc(keep["at_in"][j], 16)

        @block.tensor
        def _(pe):
            pe.sem_inc(gates, 4)
            pe.wait_ge(w_split, 2)
            with pe.Fori(0, NC) as c:
                def chunk_of(halves, k):
                    return halves[:, bass.ds(c & 1, 1), k, :].rearrange("p a n -> p (a n)")

                def product(out, cell, gate, k, start, stop):
                    cols = slice(gate * H, (gate + 1) * H)
                    for i, (w_half, in_half) in enumerate(((w_hi, in_hi), (w_lo, in_hi), (w_hi, in_lo))):
                        m = nc.tensor.matmul(out[:, 0:CHUNK], w_half[:, cell, cols], chunk_of(in_half, k),
                                             start=start and i == 0, stop=stop and i == 2)
                    return m

                for g, k in enumerate((NS, ES)):
                    pe.wait_ge(lo_made, 3 * c + k + 1)
                    pe.wait_ge(pre_made, 2 * c + g - 1 + 2)
                    pe.wait_ge(sig, 2 * c + g - 1 + 2)
                    for gate in (R, Z):
                        product(ps[g][gate], 2 * g, gate, k, True, False)
                        product(ps[g][gate], 2 * g + 1, gate, X, False, True)
                    product(ps[g][NI], 2 * g, 2, k, True, True)
                    product(ps[g][NH], 2 * g + 1, 2, X, True, True).then_inc(gates, 1)

        @block.gpsimd
        def _(pool):
            for part, (first, end) in enumerate(PARTS):
                pool.wait_ge(rows_in[part], 48)
                with pool.Fori(first, end) as c:
                    cols = bass.ds(c * CHUNK, CHUNK)
                    for k, src in enumerate((xT, ns, es)):
                        hi, lo = (x[:, bass.ds(c & 1, 1), k, :].rearrange("p a n -> p (a n)") for x in (in_hi, in_lo))
                        pool.wait_ge(hi_made, 3 * c + k + 1)
                        pool.sem_inc(hi_seen, 1)
                        pool.tensor_tensor(lo, src[:, cols], hi.bitcast(F32), ALU.subtract).then_inc(lo_made, 1)

        @block.scalar
        def _(act):
            act.sem_inc(sig, 2)

            def split(c):
                cols = bass.ds(c * CHUNK, CHUNK)
                act.wait_ge(gates, 2 * c + 2)
                act.sem_inc(slot_seen, 1)
                for k, src in enumerate((xT, ns, es)):
                    hi = in_hi[:, bass.ds(c & 1, 1), k, :].rearrange("p a n -> p (a n)")
                    nc.scalar.activation(hi, src[:, cols], ACT.Copy).then_inc(hi_made, 1)

            def cells(c):
                for g in range(2):
                    u = 2 * c + g
                    act.wait_ge(gates, u + 1 + 4)
                    act.wait_ge(cell_done, u - 1 + 2)
                    nc.scalar.activation(r[g][:, :], ps[g][R][:, 0:CHUNK], ACT.Sigmoid, bias=brz[:, g, R:R + 1])
                    nc.scalar.activation(z[g][:, :], ps[g][Z][:, 0:CHUNK], ACT.Sigmoid, bias=brz[:, g, Z:Z + 1]).then_inc(sig, 1)
                for g in range(2):
                    act.wait_ge(pre_made, 2 * c + g + 1 + 2)
                    nc.scalar.activation(cand[g][:, :], pre[g][:, :], ACT.Tanh, bias=bias[:, 2 * g, 2:3]).then_inc(cand_made, 1)

            act.wait_ge(rows_in[0], 48)
            split(0)
            split(1)
            act.wait_ge(bias_made, 1)
            cells(0)
            act.wait_ge(rows_in[1], 48)
            with act.Fori(1, NC - 1) as c:
                split(c + 1)
                cells(c)
            cells(NC - 1)

        @block.vector
        def _(dve):
            dve.sem_inc(pre_made, 2)
            dve.sem_inc(cell_done, 2)
            dve.wait_ge(w_in, 32)
            for g in range(2):
                m = dve.tensor_tensor(brz[:, g, :], bias[:, 2 * g, 0:2], bias[:, 2 * g + 1, 0:2], ALU.add)
            m.then_inc(bias_made, 1)
            dve.tensor_copy(w_hi[:, :, :], w[:, :, :]).then_inc(w_split, 1)
            dve.wait_ge(w_split, 1)
            dve.tensor_tensor(w_lo[:, :, :], w[:, :, :], w_hi[:, :, :].bitcast(F32), ALU.subtract).then_inc(w_split, 1)
            for part, (first, end) in enumerate(PARTS):
                dve.wait_ge(rows_in[part], 48)
                with dve.Fori(first, end) as c:
                    cols = bass.ds(c * CHUNK, CHUNK)
                    for g in range(2):
                        dve.wait_ge(sig, 2 * c + g + 1 + 2)
                        dve.scalar_tensor_tensor(pre[g][:, :], ps[g][NH][:, 0:CHUNK], bias[:, 2 * g + 1, 2:3], r[g][:, :], ALU.add, ALU.mult).then_inc(link, 1)
                        dve.wait_ge(link, 7 * c + g + 1)
                        dve.tensor_tensor(pre[g][:, :], ps[g][NI][:, 0:CHUNK], pre[g][:, :], ALU.add).then_inc(pre_made, 1)
                    for g in range(2):
                        u = 2 * c + g
                        base = 7 * c + 2 + 2 * g
                        dve.wait_ge(cand_made, u + 1)
                        dve.tensor_tensor(diff[g][:, :], xT[:, cols], cand[g][:, :], ALU.subtract).then_inc(link, 1)
                        dve.wait_ge(link, base + 1)
                        dve.tensor_tensor(diff[g][:, :], diff[g][:, :], z[g][:, :], ALU.mult).then_inc(link, 1)
                        dve.wait_ge(link, base + 2)
                        if g == 0:
                            dve.tensor_tensor(go[:, cols], diff[g][:, :], cand[g][:, :], ALU.add).then_inc(cell_done, 1)
                        else:
                            dve.tensor_tensor(diff[g][:, :], diff[g][:, :], cand[g][:, :], ALU.add).then_inc(link, 1)
                            dve.wait_ge(link, base + 3)
                            dve.wait_ge(cell_done, u + 2)
                            dve.tensor_tensor(go[:, cols], go[:, cols], diff[g][:, :], ALU.add).then_inc(cell_done, 1)


class Chain:

    def __init__(self, eng, sem):
        self.eng, self.sem, self.n = eng, sem, 0

    def __call__(self, ins):
        self.n += 1
        ins.then_inc(self.sem, 1)
        self.eng.wait_ge(self.sem, self.n)


EARLY = 4


NORM_GROUPS = [range(0, 8), range(8, 20), range(20, T)]


def norm_stats(dve, then, ks, v, stats, mean_var, var, var_made):
    a, b = ks[0], ks[-1] + 1
    for k in ks:
        m = dve.bn_stats(stats[:, k, :], v[:, k, :])
    then(m)
    for k in ks:
        m = dve.bn_aggr(mean_var[:, k, :], stats[:, k, :])
    then(m)
    dve.tensor_scalar(var[:, a:b], mean_var[:, a:b, 1], EPS, None, ALU.add).then_inc(var_made, 1)


def norm_apply(dve, then, ks, v, out, mean_var, var, root, tmp, root_made, group):
    a, b = ks[0], ks[-1] + 1
    dve.wait_ge(root_made, group + 1)
    then(dve.reciprocal(tmp[:, a:b], root[:, a:b]))
    then(dve.tensor_tensor(tmp[:, a:b], tmp[:, a:b], var[:, a:b], ALU.mult))
    then(dve.tensor_tensor(tmp[:, a:b], tmp[:, a:b], root[:, a:b], ALU.add))
    then(dve.tensor_scalar(tmp[:, a:b], tmp[:, a:b], 0.5, None, ALU.mult))
    then(dve.reciprocal(root[:, a:b], tmp[:, a:b]))
    for k in ks:
        m = dve.tensor_scalar(out[:, k, :], v[:, k, :], mean_var[:, k, 0:1], root[:, k:k + 1], ALU.subtract, ALU.mult)
    return m


def wide(col):
    return col.unsqueeze(2).broadcast_to([P, T, H])


def first_norm(nc, keep, d):
    go, ident, diag, dinv, s_hi, s_lo, v, x1, x, w1, b1 = (
        keep[k] for k in ("go", "ident", "diag", "dinv", "s_hi", "s_lo", "v", "x1", "x", "w1", "b1"))
    with ExitStack() as ctx:
        t = Tools(nc, ctx)
        bias = t.sb("h_bias", [P, T, H])
        x1T = t.sb("h_x1T", [P, T, P])
        stats = t.sb("h_stats", [P, T, 6])
        mean_var = t.sb("h_mv", [P, T, 2])
        var, root, tmp = (t.sb(f"h_{s}", [P, T]) for s in ("var", "root", "tmp"))
        ps = t.ps("h_ps", [P, T, P])
        link, turned, var_made, root_made, x1_made, x1_turned, x1T_made, proj, bias_made, s_made, hi_made = (
            t.sem(s) for s in ("link", "turned", "var_made", "root_made", "x1_made", "x1_turned", "x1T_made", "proj",
                               "bias_made", "s_made", "hi_made"))
        block = ctx.enter_context(nc.Block())

        @block.sync
        def _(sp):
            for j, slot in list(enumerate(keep["at"]))[EARLY:]:
                sp.dma_start(slot[:, :], d["adjT"][j * P:(j + 1) * P, :]).then_inc(keep["at_in"][j], 16)

        @block.tensor
        def _(pe):
            for ks in NORM_GROUPS:
                for k in ks:
                    m = nc.tensor.transpose(ps[:, k, :], go[:, k * P:(k + 1) * P], ident[:, :])
                m.then_inc(turned, 1)
            for g, ks in enumerate(NORM_GROUPS):
                pe.wait_ge(x1_made, g + 1)
                for k in ks:
                    m = nc.tensor.transpose(ps[:, k, :], x1[:, k, :], ident[:, :])
                m.then_inc(x1_turned, 1)
            pe.wait_ge(keep["w1_in"], 16)
            for g, ks in enumerate(NORM_GROUPS):
                pe.wait_ge(x1T_made, g + 1)
                for k in ks:
                    m = nc.tensor.matmul(ps[:, k, :], x1T[:, k, :], w1[:, :], start=True, stop=True)
                m.then_inc(proj, 1)

        @block.scalar
        def _(act):
            for g, ks in enumerate(NORM_GROUPS):
                a, b = ks[0], ks[-1] + 1
                act.wait_ge(var_made, g + 1)
                nc.scalar.activation(root[:, a:b], var[:, a:b], ACT.Sqrt).then_inc(root_made, 1)
            for g, ks in enumerate(NORM_GROUPS):
                a, b = ks[0], ks[-1] + 1
                act.wait_ge(x1_turned, g + 1)
                nc.scalar.activation(x1T[:, a:b, :], ps[:, a:b, :], ACT.Copy).then_inc(x1T_made, 1)
            for g, ks in enumerate(NORM_GROUPS):
                a, b = ks[0], ks[-1] + 1
                act.wait_ge(s_made, g + 1)
                nc.scalar.activation(s_hi[:, a:b, :], v[:, a:b, :], ACT.Copy).then_inc(hi_made, 1)

        @block.gpsimd
        def _(pool):
            pool.wait_ge(keep["b1_in"], 16)
            pool.tensor_tensor(bias[:, :, :], b1[:, :].unsqueeze(1).broadcast_to([P, T, H]), wide(dinv[:, :]), ALU.mult)\
                .then_inc(bias_made, 1)

        @block.vector
        def _(dve):
            then = Chain(dve, link)
            dve.wait_ge(keep["x_in"], 16)
            for g, ks in enumerate(NORM_GROUPS):
                dve.wait_ge(turned, g + 1)
                for k in ks:
                    m = dve.scalar_tensor_tensor(v[:, k, :], ps[:, k, :], diag[:, k:k + 1], x[:, k, :], ALU.mult, ALU.add)
                then(m)
                norm_stats(dve, then, ks, v, stats, mean_var, var, var_made)
            for g, ks in enumerate(NORM_GROUPS):
                norm_apply(dve, then, ks, v, x1, mean_var, var, root, tmp, root_made, g).then_inc(x1_made, 1)
            dve.wait_ge(bias_made, 1)
            for g, ks in enumerate(NORM_GROUPS):
                dve.wait_ge(proj, g + 1)
                for k in ks:
                    m = dve.scalar_tensor_tensor(v[:, k, :], ps[:, k, :], dinv[:, k:k + 1], bias[:, k, :], ALU.mult, ALU.add)
                m.then_inc(s_made, 1)
            for g, ks in enumerate(NORM_GROUPS):
                a, b = ks[0], ks[-1] + 1
                dve.wait_ge(hi_made, g + 1)
                dve.tensor_tensor(s_lo[:, a:b, :], v[:, a:b, :], s_hi[:, a:b, :].bitcast(F32), ALU.subtract)


def spread_layer(nc, keep, d):
    ident, not_i, dinv, diag1, s_hi, s_lo, s, x1, at, at_in = (
        keep[k] for k in ("ident", "not_i", "dinv", "diag1", "s_hi", "s_lo", "v", "x1", "at", "at_in"))
    RA, RB = len(at), 2
    BANKS = [(b, min(512, NP - b)) for b in range(0, NP, 512)]
    with ExitStack() as ctx:
        t = Tools(nc, ctx)
        own = t.sb("f_own", [P, T])
        q = t.sb("f_q", [P, T, H])
        hi = [t.sb(f"f_hi{i}", [P, NP], F32R) for i in range(RB)]
        lo = [t.sb(f"f_lo{i}", [P, NP], F32R) for i in range(RB)]
        stats = t.sb("f_stats", [P, T, 6])
        mean_var = t.sb("f_mv", [P, T, 2])
        var, root, tmp = (t.sb(f"f_{s}", [P, T]) for s in ("var", "root", "tmp"))
        acc = t.ps("f_acc", [P, T, P])
        sums = acc[:, :, :].rearrange("p t f -> p (t f)")
        own_made, own_s, q_made = t.sem("own_made"), t.sem("own_s"), t.sem("q_made")
        diag_zero, hi_done, lo_done, pe_done, sums_out, turned, link, var_made, root_made, y_made, y_saved = (
            t.sem(s) for s in ("diag_zero", "hi_done", "lo_done", "pe_done", "sums_out", "turned", "link",
                               "var_made", "root_made", "y_made", "y_saved"))
        block = ctx.enter_context(nc.Block())
        v = at[0][:, :].rearrange("p (t f) -> p t f", f=H)
        y = at[2][:, :].rearrange("p (t f) -> p t f", f=H)
        accT = at[3]

        @block.sync
        def _(sp):
            for j in range(RA, T):
                sp.wait_ge(hi_done, j - RA + 1)
                sp.wait_ge(lo_done, j - RA + 1)
                sp.dma_start(at[j % RA][:, :], d["adjT"][j * P:(j + 1) * P, :]).then_inc(at_in[j % RA], 16)
            for g, ks in enumerate(NORM_GROUPS):
                a, b = ks[0], ks[-1] + 1
                sp.wait_ge(y_made, g + 1)
                sp.dma_start(d["out"][:, a:b, :], y[:, a:b, :]).then_inc(y_saved, 16)
            sp.wait_ge(y_saved, 16 * len(NORM_GROUPS))

        @block.gpsimd
        def _(pool):
            pool.tensor_tensor(own[:, :], dinv[:, :], diag1[:, :], ALU.mult).then_inc(own_made, 1)
            pool.wait_ge(own_made, 1)
            pool.tensor_tensor(q[:, :, :], s[:, :, :], wide(own[:, :]), ALU.mult).then_inc(own_s, 1)
            pool.wait_ge(own_s, 1)
            pool.tensor_tensor(q[:, :, :], q[:, :, :], x1[:, :, :], ALU.add).then_inc(q_made, 1)

        @block.scalar
        def _(act):
            for j in range(T):
                act.wait_ge(diag_zero, j + 1)
                if j >= RB:
                    act.wait_ge(pe_done, j - RB + 1)
                    act.wait_ge(lo_done, j - RB + 1)
                nc.scalar.activation(hi[j % RB][:, :], at[j % RA][:, :], ACT.Copy).then_inc(hi_done, 1)
            act.wait_ge(lo_done, T)
            act.wait_ge(pe_done, T)
            for ks in NORM_GROUPS:
                cols = slice(ks[0] * P, (ks[-1] + 1) * P)
                nc.scalar.activation(accT[:, cols], sums[:, cols], ACT.Copy).then_inc(sums_out, 1)
            for g, ks in enumerate(NORM_GROUPS):
                a, b = ks[0], ks[-1] + 1
                act.wait_ge(var_made, g + 1)
                nc.scalar.activation(root[:, a:b], var[:, a:b], ACT.Sqrt).then_inc(root_made, 1)

        @block.vector
        def _(dve):
            def zero_diagonal(j):
                dve.wait_ge(at_in[j % RA], 16 * (j // RA + 1))
                c = slice(j * P, (j + 1) * P)
                dve.tensor_tensor(at[j % RA][:, c], at[j % RA][:, c], not_i[:, :], ALU.mult).then_inc(diag_zero, 1)

            zero_diagonal(0)
            for j in range(T):
                if j + 1 < T:
                    zero_diagonal(j + 1)
                dve.wait_ge(hi_done, j + 1)
                if j >= RB:
                    dve.wait_ge(pe_done, j - RB + 1)
                dve.tensor_tensor(lo[j % RB][:, :], at[j % RA][:, :], hi[j % RB][:, :].bitcast(F32), ALU.subtract)\
                   .then_inc(lo_done, 1)
            then = Chain(dve, link)
            dve.wait_ge(q_made, 1)
            for g, ks in enumerate(NORM_GROUPS):
                dve.wait_ge(turned, g + 1)
                for k in ks:
                    m = dve.scalar_tensor_tensor(v[:, k, :], acc[:, k, :], dinv[:, k:k + 1], q[:, k, :], ALU.mult, ALU.add)
                then(m)
                norm_stats(dve, then, ks, v, stats, mean_var, var, var_made)
            for g, ks in enumerate(NORM_GROUPS):
                norm_apply(dve, then, ks, v, y, mean_var, var, root, tmp, root_made, g).then_inc(y_made, 1)

        @block.tensor
        def _(pe):
            for j in range(T):
                for w, m, ready in ((s_hi, hi, hi_done), (s_lo, hi, None), (s_hi, lo, lo_done)):
                    if ready is not None:
                        pe.wait_ge(ready, j + 1)
                    for b, n in BANKS:
                        mm = nc.tensor.matmul(sums[:, b:b + n], w[:, j, :], m[j % RB][:, b:b + n],
                                              start=(j == 0 and w is s_hi and m is hi), stop=(j == T - 1 and m is lo))
                mm.then_inc(pe_done, 1)
            for g, ks in enumerate(NORM_GROUPS):
                pe.wait_ge(sums_out, g + 1)
                for k in ks:
                    m = nc.tensor.transpose(acc[:, k, :], accT[:, k * P:(k + 1) * P], ident[:, :])
                m.then_inc(turned, 1)


def build(nc, adj, adjT, x, xT, diag, gat_w, gat_a, gru_w, gru_b, w1, b1, out):
    scratch = {k: nc.dram_tensor(k, s, F32).ap() for k, s in (("e_rows", (2, HEADS * NP)), ("ns_d", (P, NP)), ("es_d", (P, NP)))}
    d = {"adj": adj, "adjT": adjT, "x": x, "xT": xT, "diag": diag, "gat_w": gat_w, "gat_a": gat_a,
         "gru_w": gru_w, "gru_b": gru_b, "w1": w1, "b1": b1,
         "e_rows": scratch["e_rows"], "ns": scratch["ns_d"], "es": scratch["es_d"],
         "out": out.rearrange("(t p) f -> p t f", p=P)}
    with ExitStack() as ctx:
        t = Tools(nc, ctx)
        keep = {"ident": t.sb("ident", [P, P]), "not_i": t.sb("not_i", [P, P]),
                "ecol": t.sb("ecol", [P, E2 * T]), "flag": t.sb("flag", [P, 1], I32),
                "dinv": t.sb("dinv", [P, T]), "diag": t.sb("diag", [P, T]), "diag1": t.sb("diag1", [P, T])}
        with ExitStack() as ctx1:
            t1 = Tools(nc, ctx1)
            keep["hw"] = t1.sb("hw", [P, T, HEADS * H])
            with ExitStack() as ctx2:
                t2 = Tools(nc, ctx2)
                keep |= {"x_hi": t2.sb("x_hi", [P, T, H], F32R), "x_lo": t2.sb("x_lo", [P, T, H], F32R),
                         "up": t2.sb("up", [P, T, EW], BF16), "um": t2.sb("um", [P, T, EW], BF16),
                         "ns": t2.sb("ns", [P, NP]), "csum": t2.sb("csum", [P, NP]), "elog": t2.sb("elog", [EW, NP])}
                keep |= {"at1": [t2.sb(f"b_at{i}", [P, HALF]) for i in range(4)],
                         "at1_in": [t2.sem(f"b_at_in{i}") for i in range(4)]}
                project(nc, keep, d)
                aggregate(nc, keep, d)
                logits(nc, keep, d)
            attend(nc, keep, d)
            attend_signed(nc, keep, d)
        keep |= {"s_hi": t.sb("s_hi", [P, T, H], F32R), "s_lo": t.sb("s_lo", [P, T, H], F32R), "v": t.sb("v", [P, T, H]),
                 "x1": t.sb("x1", [P, T, H])}
        keep |= {"at": [t.sb(f"f_at{i}", [P, NP]) for i in range(6)], "at_in": [t.sem(f"f_at_in{i}") for i in range(6)]}
        with ExitStack() as ctx3:
            t3 = Tools(nc, ctx3)
            keep |= {"go": t3.sb("go", [P, NP]), "x": t3.sb("x", [P, T, H]), "w1": t3.sb("w1", [P, H]),
                     "b1": t3.sb("b1", [P, H])}
            keep |= {k: t.sem(k) for k in ("x_in", "w1_in", "b1_in")}
            gru(nc, keep, d)
            first_norm(nc, keep, d)
        spread_layer(nc, keep, d)


def kernel(x, adj, L0_gnn_gat_W, L0_gnn_gat_a, L0_gnn_edge_Wih, L0_gnn_edge_Whh, L0_gnn_edge_bih, L0_gnn_edge_bhh,
           L0_gnn_node_Wih, L0_gnn_node_Whh, L0_gnn_node_bih, L0_gnn_node_bhh, L1_gnn_W, L1_gnn_b):
    import numpy as np
    import concourse.bacc as bacc
    from concourse.bass_utils import run_bass_kernel_spmd

    def f(a):
        return np.ascontiguousarray(a)

    adj = np.asarray(adj)
    padded = np.zeros((NP, NP), adj.dtype)
    padded[:N, :N] = adj
    padded_t = np.zeros((NP, NP), adj.dtype)
    padded_t[:N, :N] = adj.T
    diag = np.zeros((NP,), adj.dtype)
    diag[:N] = np.diagonal(adj)
    xp = np.zeros((NP, H), np.asarray(x).dtype)
    xp[:N] = np.asarray(x)
    weights = (L0_gnn_edge_Wih, L0_gnn_edge_Whh, L0_gnn_node_Wih, L0_gnn_node_Whh)
    biases = (L0_gnn_edge_bih, L0_gnn_edge_bhh, L0_gnn_node_bih, L0_gnn_node_bhh)
    arrays = {
        "adj": padded, "adjT": padded_t,
        "x": f(xp.reshape(T, P, H).transpose(1, 0, 2)), "xT": f(xp.T), "diag": f(diag.reshape(T, P).T),
        "gat_w": f(np.asarray(L0_gnn_gat_W).transpose(1, 0, 2).reshape(H, HEADS * H)),
        "gat_a": f(np.asarray(L0_gnn_gat_a).reshape(HEADS * 2 * H)),
        "gru_w": f(np.stack([np.asarray(w).T for w in weights], axis=1)),
        "gru_b": f(np.stack([np.asarray(b).reshape(3, H).T for b in biases], axis=1)),
        "w1": f(np.asarray(L1_gnn_W).T), "b1": f(np.asarray(L1_gnn_b)),
    }
    nc = bacc.Bacc("TRN2", target_bir_lowering=False, num_devices=1)
    args = [nc.dram_tensor(f"in_{k}", a.shape, mybir.dt.from_np(a.dtype), kind="ExternalInput").ap()
            for k, a in arrays.items()]
    out = nc.dram_tensor("y", (NP, H), F32, kind="ExternalOutput").ap()
    build(nc, *args, out)
    r = run_bass_kernel_spmd(nc, [{f"in_{k}": a for k, a in arrays.items()}], core_ids=[0])
    return r.results[0]["y"][:N]
```
